# Optimizing a Trainium2 kernel written in Bass

```python
import numpy as np
import jax
import jax.numpy as jnp

def _softmax(x, axis=-1):
    return jax.nn.softmax(x, axis=axis)

def _gelu(x):
    return jax.nn.gelu(x, approximate=True)

def _silu(x):
    return jax.nn.silu(x)

def _sigmoid(x):
    return jax.nn.sigmoid(x)

def _layernorm(x, axis=-1, eps=1e-05):
    m = jnp.mean(x, axis=axis, keepdims=True)
    v = jnp.var(x, axis=axis, keepdims=True)
    return (x - m) / jnp.sqrt(v + eps)

def _scatter_add(tgt, idx, src, axis=0):
    return tgt.at[idx].add(src)

def _segment_sum(src, seg, n):
    return jax.ops.segment_sum(src, seg, n)
kernel_name = 'mk_seq_preln_d2_jaxref_r8_1499e8'

def setup_inputs(seed: int=0):
    np.random.seed(seed)
    _w = jnp.asarray

    def _L0_attn_setup():
        import jax, jax.numpy as jnp
        import numpy as np
        B, S, DM, H = (4, 128, 128, 16)
        D = DM // H

        def _split_heads(x):
            return x.reshape(x.shape[0], x.shape[1], H, D).transpose(0, 2, 1, 3)
        key = jax.random.key(seed)
        ks = jax.random.split(key, 16)
        sc = 0.02
        return {'hidden_states': jax.random.normal(ks[0], (B, S, DM), jnp.float32), 'wq': jax.random.normal(ks[1], (DM, DM), jnp.float32) * sc, 'bq': jax.random.normal(ks[2], (DM,), jnp.float32) * sc, 'wk': jax.random.normal(ks[3], (DM, DM), jnp.float32) * sc, 'bk': jax.random.normal(ks[4], (DM,), jnp.float32) * sc, 'wv': jax.random.normal(ks[5], (DM, DM), jnp.float32) * sc, 'bv': jax.random.normal(ks[6], (DM,), jnp.float32) * sc, 'wo': jax.random.normal(ks[7], (DM, DM), jnp.float32) * sc, 'bo': jax.random.normal(ks[8], (DM,), jnp.float32) * sc, 'wfq': jax.random.normal(ks[9], (DM, DM), jnp.float32) * sc, 'bfq': jax.random.normal(ks[10], (DM,), jnp.float32) * sc, 'wfg': jax.random.normal(ks[11], (DM, DM), jnp.float32) * sc, 'bfg': jax.random.normal(ks[12], (DM,), jnp.float32) * sc, 'up': jax.random.normal(ks[13], (H, 1, D), jnp.float32) * sc, 'uz': jax.random.normal(ks[14], (H, 1, D), jnp.float32) * sc}
    _L0_attn_in = _L0_attn_setup()

    def _L0_ffn_setup():
        import jax, jax.numpy as jnp
        import numpy as np
        E = 64
        K = 6
        CAP = 64
        ROUTE_SCALE = 1.0
        key = jax.random.key(seed)
        ks = jax.random.split(key, 9)
        B, S, D, I = (2, 128, 128, 88)
        SI = 2 * I
        s = 0.02
        return {'x': jax.random.normal(ks[0], (B, S, D), jnp.float32), 'gate_w': jax.random.normal(ks[1], (E, D), jnp.float32) * s, 'gate_b': jnp.zeros((E,), jnp.float32), 'w1': jax.random.normal(ks[2], (E, I, D), jnp.float32) * s, 'w2': jax.random.normal(ks[3], (E, D, I), jnp.float32) * s, 'w3': jax.random.normal(ks[4], (E, I, D), jnp.float32) * s, 'ws1': jax.random.normal(ks[5], (SI, D), jnp.float32) * s, 'ws2': jax.random.normal(ks[6], (D, SI), jnp.float32) * s, 'ws3': jax.random.normal(ks[7], (SI, D), jnp.float32) * s}
    _L0_ffn_in = _L0_ffn_setup()

    def _L1_attn_setup():
        import jax, jax.numpy as jnp
        import numpy as np
        B, N, D = (4, 512, 128)
        HEADS = 4
        DH = D // HEADS
        FF = 4 * D
        EPS = 1e-05

        def layer_norm(x, g, b):
            mu = jnp.mean(x, axis=-1, keepdims=True)
            var = jnp.mean(jnp.square(x - mu), axis=-1, keepdims=True)
            return (x - mu) * jax.lax.rsqrt(var + EPS) * g + b

        def linear_attn(q, k, v):
            scale = DH ** (-0.25)
            q = jax.nn.softmax(q * scale, axis=-1)
            k = jax.nn.softmax(k * scale, axis=-2)
            context = jnp.einsum('bhnd,bhne->bhde', k, v)
            return jnp.einsum('bhnd,bhde->bhne', q, context)
        key = jax.random.key(seed)
        ks = jax.random.split(key, 16)
        s = lambda fan_in: 1.0 / np.sqrt(fan_in)
        inp = {'x': jax.random.normal(ks[0], (B, N, D), jnp.float32), 'ln1_g': jnp.ones((D,), jnp.float32), 'ln1_b': jnp.zeros((D,), jnp.float32), 'wq': jax.random.normal(ks[1], (D, D), jnp.float32) * s(D), 'wk': jax.random.normal(ks[2], (D, D), jnp.float32) * s(D), 'wv': jax.random.normal(ks[3], (D, D), jnp.float32) * s(D), 'wo': jax.random.normal(ks[4], (D, D), jnp.float32) * s(D), 'bo': jnp.zeros((D,), jnp.float32), 'ln2_g': jnp.ones((D,), jnp.float32), 'ln2_b': jnp.zeros((D,), jnp.float32), 'w_ff1': jax.random.normal(ks[5], (D, FF), jnp.float32) * s(D), 'b_ff1': jnp.zeros((FF,), jnp.float32), 'w_ff2': jax.random.normal(ks[6], (FF, D), jnp.float32) * s(FF), 'b_ff2': jnp.zeros((D,), jnp.float32), 'w_d': jax.random.normal(ks[7], (D, D), jnp.float32) * s(D), 'b_d': jnp.zeros((D,), jnp.float32)}
        return inp
    _L1_attn_in = _L1_attn_setup()

    def _L1_ffn_setup():
        import jax, jax.numpy as jnp
        import numpy as np
        D_MODEL, D_FF, N_EXPERTS, TOP_K = (128, 256, 8, 2)
        B, S = (2, 256)
        key = jax.random.key(seed)
        ks = jax.random.split(key, 6)
        sd = 1.0 / np.sqrt(D_MODEL)
        sf = 1.0 / np.sqrt(D_FF)
        return {'x': jax.random.normal(ks[0], (B, S, D_MODEL), jnp.float32), 'router_w': jax.random.normal(ks[1], (N_EXPERTS, D_MODEL), jnp.float32) * sd, 'gate_w': jax.random.normal(ks[2], (N_EXPERTS, D_MODEL, D_FF), jnp.float32) * sd, 'gate_b': jnp.zeros((N_EXPERTS, D_FF), jnp.float32), 'up_w': jax.random.normal(ks[3], (N_EXPERTS, D_MODEL, D_FF), jnp.float32) * sd, 'up_b': jnp.zeros((N_EXPERTS, D_FF), jnp.float32), 'down_w': jax.random.normal(ks[4], (N_EXPERTS, D_FF, D_MODEL), jnp.float32) * sf, 'down_b': jnp.zeros((N_EXPERTS, D_MODEL), jnp.float32)}
    _L1_ffn_in = _L1_ffn_setup()
    _d = {'L0_attn_hidden_states': _L0_attn_in['hidden_states'], 'L0_attn_wq': _L0_attn_in['wq'], 'L0_attn_bq': _L0_attn_in['bq'], 'L0_attn_wk': _L0_attn_in['wk'], 'L0_attn_bk': _L0_attn_in['bk'], 'L0_attn_wv': _L0_attn_in['wv'], 'L0_attn_bv': _L0_attn_in['bv'], 'L0_attn_wo': _L0_attn_in['wo'], 'L0_attn_bo': _L0_attn_in['bo'], 'L0_attn_wfq': _L0_attn_in['wfq'], 'L0_attn_bfq': _L0_attn_in['bfq'], 'L0_attn_wfg': _L0_attn_in['wfg'], 'L0_attn_bfg': _L0_attn_in['bfg'], 'L0_attn_up': _L0_attn_in['up'], 'L0_attn_uz': _L0_attn_in['uz'], 'L0_ffn_gate_w': _L0_ffn_in['gate_w'], 'L0_ffn_gate_b': _L0_ffn_in['gate_b'], 'L0_ffn_w1': _L0_ffn_in['w1'], 'L0_ffn_w2': _L0_ffn_in['w2'], 'L0_ffn_w3': _L0_ffn_in['w3'], 'L0_ffn_ws1': _L0_ffn_in['ws1'], 'L0_ffn_ws2': _L0_ffn_in['ws2'], 'L0_ffn_ws3': _L0_ffn_in['ws3'], 'L1_attn_ln1_g': _L1_attn_in['ln1_g'], 'L1_attn_ln1_b': _L1_attn_in['ln1_b'], 'L1_attn_wq': _L1_attn_in['wq'], 'L1_attn_wk': _L1_attn_in['wk'], 'L1_attn_wv': _L1_attn_in['wv'], 'L1_attn_wo': _L1_attn_in['wo'], 'L1_attn_bo': _L1_attn_in['bo'], 'L1_attn_ln2_g': _L1_attn_in['ln2_g'], 'L1_attn_ln2_b': _L1_attn_in['ln2_b'], 'L1_attn_w_ff1': _L1_attn_in['w_ff1'], 'L1_attn_b_ff1': _L1_attn_in['b_ff1'], 'L1_attn_w_ff2': _L1_attn_in['w_ff2'], 'L1_attn_b_ff2': _L1_attn_in['b_ff2'], 'L1_attn_w_d': _L1_attn_in['w_d'], 'L1_attn_b_d': _L1_attn_in['b_d'], 'L1_ffn_router_w': _L1_ffn_in['router_w'], 'L1_ffn_gate_w': _L1_ffn_in['gate_w'], 'L1_ffn_gate_b': _L1_ffn_in['gate_b'], 'L1_ffn_up_w': _L1_ffn_in['up_w'], 'L1_ffn_up_b': _L1_ffn_in['up_b'], 'L1_ffn_down_w': _L1_ffn_in['down_w'], 'L1_ffn_down_b': _L1_ffn_in['down_b']}
    _x0 = _d['L0_attn_hidden_states']
    _d['L0_attn_hidden_states'] = jax.random.normal(jax.random.fold_in(jax.random.key(seed), 1), (4, 1024, 128), dtype=_x0.dtype)
    del _x0
    return _d

def reference(L0_attn_hidden_states, L0_attn_wq, L0_attn_bq, L0_attn_wk, L0_attn_bk, L0_attn_wv, L0_attn_bv, L0_attn_wo, L0_attn_bo, L0_attn_wfq, L0_attn_bfq, L0_attn_wfg, L0_attn_bfg, L0_attn_up, L0_attn_uz, L0_ffn_gate_w, L0_ffn_gate_b, L0_ffn_w1, L0_ffn_w2, L0_ffn_w3, L0_ffn_ws1, L0_ffn_ws2, L0_ffn_ws3, L1_attn_ln1_g, L1_attn_ln1_b, L1_attn_wq, L1_attn_wk, L1_attn_wv, L1_attn_wo, L1_attn_bo, L1_attn_ln2_g, L1_attn_ln2_b, L1_attn_w_ff1, L1_attn_b_ff1, L1_attn_w_ff2, L1_attn_b_ff2, L1_attn_w_d, L1_attn_b_d, L1_ffn_router_w, L1_ffn_gate_w, L1_ffn_gate_b, L1_ffn_up_w, L1_ffn_up_b, L1_ffn_down_w, L1_ffn_down_b):

    def _L0_attn_ref(hidden_states, wq, bq, wk, bk, wv, bv, wo, bo, wfq, bfq, wfg, bfg, up, uz):
        import jax, jax.numpy as jnp
        import numpy as np
        B, S, DM, H = (4, 128, 128, 16)
        D = DM // H

        def _split_heads(x):
            return x.reshape(x.shape[0], x.shape[1], H, D).transpose(0, 2, 1, 3)
        key_len = hidden_states.shape[1]
        mixed_q = hidden_states @ wq + bq
        mixed_k = hidden_states @ wk + bk
        mixed_v = hidden_states @ wv + bv
        glo = jnp.mean(mixed_q, axis=1, keepdims=True)
        c = jnp.tanh(mixed_q @ wfq + bfq + (glo @ wfg + bfg))
        c = _split_heads(c)
        p = jnp.sum(c * up[None], axis=-1)
        z = jnp.sum(c * uz[None], axis=-1)
        P = jax.nn.sigmoid(p) * key_len
        Z = jax.nn.sigmoid(z) * key_len
        j = jnp.arange(key_len, dtype=P.dtype)
        G = -(j[None, None, None, :] - P[..., None]) ** 2 * 2.0 / Z[..., None] ** 2
        q = _split_heads(mixed_q)
        k = _split_heads(mixed_k)
        v = _split_heads(mixed_v)
        scores = jnp.einsum('bhqd,bhkd->bhqk', q, k) / jnp.sqrt(jnp.float32(D))
        scores = scores + G
        probs = jax.nn.softmax(scores, axis=-1)
        ctx = jnp.einsum('bhqk,bhkd->bhqd', probs, v)
        ctx = ctx.transpose(0, 2, 1, 3).reshape(ctx.shape[0], key_len, H * D)
        return ctx @ wo + bo

    def _L0_ffn_ref(x, gate_w, gate_b, w1, w2, w3, ws1, ws2, ws3):
        import jax, jax.numpy as jnp
        import numpy as np
        E = 64
        K = 6
        CAP = 64
        ROUTE_SCALE = 1.0
        shape = x.shape
        D = shape[-1]
        xf = x.reshape(-1, D)
        T = xf.shape[0]
        scores = jax.nn.softmax(xf @ gate_w.T, axis=-1)
        _, idx = jax.lax.top_k(scores + gate_b, K)
        weights = jnp.take_along_axis(scores, idx, axis=1) * ROUTE_SCALE
        flat_e = idx.reshape(-1)
        order = jnp.argsort(flat_e)
        se = flat_e[order]
        counts = jnp.bincount(flat_e, length=E)
        starts = jnp.cumsum(counts) - counts
        pos = jnp.arange(T * K) - starts[se]
        tok = order // K
        xb = jnp.zeros((E, CAP, D), xf.dtype).at[se, pos].set(xf[tok], mode='drop')
        h = jax.nn.silu(jnp.einsum('ecd,eid->eci', xb, w1)) * jnp.einsum('ecd,eid->eci', xb, w3)
        yb = jnp.einsum('eci,edi->ecd', h, w2)
        valid = (pos < CAP).astype(xf.dtype)
        contrib = yb[se, jnp.minimum(pos, CAP - 1)]
        wf = weights.reshape(-1)[order] * valid
        y = jnp.zeros_like(xf).at[tok].add(contrib * wf[:, None])
        z = jax.nn.silu(xf @ ws1.T) * (xf @ ws3.T) @ ws2.T
        return (y + z).reshape(shape)

    def _L1_attn_ref(x, ln1_g, ln1_b, wq, wk, wv, wo, bo, ln2_g, ln2_b, w_ff1, b_ff1, w_ff2, b_ff2, w_d, b_d):
        import jax, jax.numpy as jnp
        import numpy as np
        B, N, D = (4, 512, 128)
        HEADS = 4
        DH = D // HEADS
        FF = 4 * D
        EPS = 1e-05

        def layer_norm(x, g, b):
            mu = jnp.mean(x, axis=-1, keepdims=True)
            var = jnp.mean(jnp.square(x - mu), axis=-1, keepdims=True)
            return (x - mu) * jax.lax.rsqrt(var + EPS) * g + b

        def linear_attn(q, k, v):
            scale = DH ** (-0.25)
            q = jax.nn.softmax(q * scale, axis=-1)
            k = jax.nn.softmax(k * scale, axis=-2)
            context = jnp.einsum('bhnd,bhne->bhde', k, v)
            return jnp.einsum('bhnd,bhde->bhne', q, context)
        b, n, d = x.shape
        h = layer_norm(x, ln1_g, ln1_b)
        q = (h @ wq).reshape(b, n, HEADS, DH).transpose(0, 2, 1, 3)
        k = (h @ wk).reshape(b, n, HEADS, DH).transpose(0, 2, 1, 3)
        v = (h @ wv).reshape(b, n, HEADS, DH).transpose(0, 2, 1, 3)
        attn = linear_attn(q, k, v)
        attn = attn.transpose(0, 2, 1, 3).reshape(b, n, d)
        x = x + attn @ wo + bo
        h = layer_norm(x, ln2_g, ln2_b)
        x = x + jax.nn.gelu(h @ w_ff1 + b_ff1) @ w_ff2 + b_ff2
        return x @ w_d + b_d

    def _L1_ffn_ref(x, router_w, gate_w, gate_b, up_w, up_b, down_w, down_b):
        import jax, jax.numpy as jnp
        import numpy as np
        D_MODEL, D_FF, N_EXPERTS, TOP_K = (128, 256, 8, 2)
        B, S = (2, 256)
        b, s, d = x.shape
        xf = x.reshape(b * s, d)
        n = xf.shape[0]
        router_logits = xf @ router_w.T
        probs = jax.nn.softmax(router_logits, axis=-1)
        topv, topi = jax.lax.top_k(probs, TOP_K)
        mask = jnp.zeros_like(probs).at[jnp.arange(n)[:, None], topi].set(1.0)
        probs = probs * mask
        probs = probs / (probs.sum(axis=-1, keepdims=True) + 1e-09)
        g = jnp.einsum('nd,edf->nef', xf, gate_w) + gate_b
        u = jnp.einsum('nd,edf->nef', xf, up_w) + up_b
        h = jax.nn.silu(g) * u
        expert_out = jnp.einsum('nef,efd->ned', h, down_w) + down_b
        y = jnp.einsum('ne,ned->nd', probs, expert_out)
        return y.reshape(b, s, d)
    x = L0_attn_hidden_states
    x = x + _L0_attn_ref(_layernorm(x, axis=-1), L0_attn_wq, L0_attn_bq, L0_attn_wk, L0_attn_bk, L0_attn_wv, L0_attn_bv, L0_attn_wo, L0_attn_bo, L0_attn_wfq, L0_attn_bfq, L0_attn_wfg, L0_attn_bfg, L0_attn_up, L0_attn_uz)
    x = x + _L0_ffn_ref(_layernorm(x, axis=-1), L0_ffn_gate_w, L0_ffn_gate_b, L0_ffn_w1, L0_ffn_w2, L0_ffn_w3, L0_ffn_ws1, L0_ffn_ws2, L0_ffn_ws3)
    x = x + _L1_attn_ref(_layernorm(x, axis=-1), L1_attn_ln1_g, L1_attn_ln1_b, L1_attn_wq, L1_attn_wk, L1_attn_wv, L1_attn_wo, L1_attn_bo, L1_attn_ln2_g, L1_attn_ln2_b, L1_attn_w_ff1, L1_attn_b_ff1, L1_attn_w_ff2, L1_attn_b_ff2, L1_attn_w_d, L1_attn_b_d)
    x = x + _L1_ffn_ref(_layernorm(x, axis=-1), L1_ffn_router_w, L1_ffn_gate_w, L1_ffn_gate_b, L1_ffn_up_w, L1_ffn_up_b, L1_ffn_down_w, L1_ffn_down_b)
    return x

_drawn_inputs = setup_inputs


def setup_inputs(seed=0):
    import zlib

    import numpy as np

    out = dict(_drawn_inputs(seed))
    spreads = {'L0_ffn_gate_b': (0.0, 0.8),
     'L1_attn_ln1_g': (1.0, 0.6),
     'L1_attn_ln1_b': (0.0, 0.1),
     'L1_attn_bo': (0.0, 0.1),
     'L1_attn_ln2_g': (1.0, 0.2),
     'L1_attn_ln2_b': (0.0, 0.1),
     'L1_attn_b_ff1': (0.0, 0.1),
     'L1_attn_b_ff2': (0.0, 0.1),
     'L1_attn_b_d': (0.0, 0.1),
     'L1_ffn_gate_b': (0.0, 0.285),
     'L1_ffn_up_b': (0.0, 0.283),
     'L1_ffn_down_b': (0.0, 0.1)}
    factors = {'L0_attn_wq': 8.0,
     'L0_attn_bq': 8.0,
     'L0_attn_wk': 8.0,
     'L0_attn_bk': 8.0,
     'L0_attn_wv': 6.64,
     'L0_attn_bv': 3.398,
     'L0_attn_wo': 3.434,
     'L0_attn_wfq': 8.0,
     'L0_attn_bfq': 8.0,
     'L0_attn_wfg': 8.0,
     'L0_attn_bfg': 8.0,
     'L0_attn_up': 8.0,
     'L0_attn_uz': 8.0,
     'L0_ffn_gate_w': 8.0,
     'L0_ffn_w1': 8.0,
     'L0_ffn_w2': 8.0,
     'L0_ffn_w3': 8.0,
     'L0_ffn_ws1': 3.606,
     'L0_ffn_ws2': 3.474,
     'L0_ffn_ws3': 3.406,
     'L1_attn_wq': 6.336,
     'L1_attn_wk': 3.608}
    for name, (base, spread) in spreads.items():
        noise = np.random.default_rng([zlib.crc32(name.encode()), seed]).standard_normal(out[name].shape)
        drawn = base * np.exp(spread * noise) if base else spread * noise
        out[name] = jnp.asarray(drawn.astype(out[name].dtype))
    for name, factor in factors.items():
        out[name] = (out[name] * factor).astype(out[name].dtype)
    return out
```

```python
from contextlib import ExitStack

import concourse.bass as bass
from concourse import mybir

F32 = mybir.dt.float32
F32R = mybir.dt.float32r
BF16 = mybir.dt.bfloat16
I32 = mybir.dt.int32
U32 = mybir.dt.uint32
ALU = mybir.AluOpType
ACT = mybir.ActivationFunctionType
X_AXIS = mybir.AxisListType.X

P = 128
D = 128
B, S = 4, 1024
NT = B * S // P
TB = S // P
H0, DH0 = 16, 8
GH = 4
NG = H0 // GH
R = 32
EPS = 1e-5
START = 1


def stand_alone(eng):
    eng.nop(nofuse=True)


class Steps:

    def __init__(self, eng, sem, base=0, alone=False):
        self.eng, self.sem, self.base, self.alone, self.n = eng, sem, base, alone, 0

    def done(self, ins):
        ins.then_inc(self.sem, 1)
        self.n += 1

    def settle(self):
        self.eng.wait_ge(self.sem, self.base + self.n)
        if self.alone:
            stand_alone(self.eng)

    def do(self, ins):
        self.done(ins)
        self.settle()
def project_batches(nc, t, sem, ps):
    ctx = ExitStack()
    with ctx:
        def sb(name, shape, dt=F32):
            return ctx.enter_context(nc.sbuf_tensor(name, shape, dt))

        wqkv = sb("wqkv", [P, 3 * D])
        wfq, wfg = sb("wfq", [P, D]), sb("wfg", [P, D])
        cols = sb("cols", [P, 5])
        biases = sb("biases", [P, 3 * D])
        hmask = sb("hmask", [P, H0])
        upz = sb("upz", [P, 2, H0])
        stats = sb("stats", [P, TB, 6])
        mv = sb("mv", [P, TB, 2])
        rstd = sb("rstd", [P, TB])
        half = sb("half", [P, TB])
        xn = sb("xn", [P, TB, D])
        xT = sb("xT", [P, S])
        qT = sb("qT", [P, S])
        cT = sb("cT", [P, S])
        glo = sb("glo", [P, 2])
        cbias = sb("cbias", [P, 3])
        ez = sb("ez", [P, TB, 2, H0])
        g1 = sb("g1", [P, TB, 2, H0])
        g2 = sb("g2", [P, TB, H0])
        g3 = sb("g3", [P, TB, H0])
        X, qkv, gco = t["X"], t["qkv"], t["gco"]

        loaded, own, rst, trd, act, pe = (sem(n) for n in (
            "p1_loaded", "p1_dve_steps", "p1_rstd_ready", "p1_xn_ready", "p1_act_steps", "p1_pe_steps"))
        tok, evac = sem("p1_qkv_ready"), sem("p1_qkv_taken")
        halfs = sem("p1_half_ready")
        block = ctx.enter_context(nc.Block())

        @block.sync
        def _(sp):
            for b in range(B):
                sp.dma_start(X[:, b * TB:(b + 1) * TB, :],
                             t["x"][b].rearrange("(t p) d -> p t d", p=P)).then_inc(loaded, 16)
            for i, n in enumerate(("wq", "wk", "wv")):
                sp.dma_start(wqkv[:, i * D:(i + 1) * D], t[n]).then_inc(loaded, 16)
            sp.dma_start(wfq[:], t["wfq"]).then_inc(loaded, 16)
            sp.dma_start(wfg[:], t["wfg"]).then_inc(loaded, 16)
            sp.dma_start(hmask[:], t["hmask"]).then_inc(loaded, 16)
            for i, n in enumerate(("bq", "bk", "bv")):
                sp.dma_start(biases[:, i * D:(i + 1) * D],
                             t[n].partition_broadcast(P)).then_inc(loaded, 16)
            for i, n in enumerate(("bq", "bfq", "bfg", "up", "uz")):
                v = t[n] if n[0] == "b" else t[n].rearrange("h a d -> (h a d)")
                sp.dma_start(cols[:, i:i + 1], v.rearrange("(p a) -> p a", a=1)).then_inc(loaded, 16)
        N_LOADED = 16 * (B + 3 + 3 + 3 + 5)

        DVE_STEPS = TB + 11
        ACT_STEPS = 2 + 1 + 2 + 1
        PE_STEPS = 5

        @block.gpsimd
        def _(pool):
            pool.memset(half[:], -0.5).then_inc(halfs, 1)
            pool.wait_ge(halfs, 1)
            with pool.Fori(0, B) as b:
                pool.wait_ge(own, 3 + b * DVE_STEPS + TB + 2)
                pool.tensor_tensor(rstd[:], rstd[:], half[:], ALU.pow).then_inc(rst, 1)

        @block.vector
        def _(dve):
            dve.wait_ge(loaded, N_LOADED)
            s0 = Steps(dve, own)
            for i in range(2):
                s0.done(dve.tensor_scalar(upz[:, i, :], hmask[:], cols[:, 3 + i:4 + i], None, ALU.mult))
            s0.do(dve.tensor_tensor(cbias[:, 0:1], cols[:, 1:2], cols[:, 2:3], ALU.add))
            with dve.Fori(0, B) as b:
                s = Steps(dve, own, 3 + b * DVE_STEPS, alone=True)
                for i in range(TB):
                    s.done(dve.bn_stats(stats[:, i, :], X[:, b * TB + i, :]))
                s.settle()
                for i in range(TB):
                    last = dve.bn_aggr(mv[:, i, :], stats[:, i, :])
                s.do(last)
                s.do(dve.tensor_scalar(rstd[:], mv[:, :, 1], EPS, None, ALU.add))
                dve.wait_ge(rst, b + 1)
                for i in range(TB):
                    last = dve.tensor_scalar(xn[:, i, :], X[:, b * TB + i, :], mv[:, i, 0:1],
                                             rstd[:, i:i + 1], ALU.subtract, ALU.mult)
                last.then_inc(trd, 1)
                dve.wait_ge(act, b * ACT_STEPS + 3)
                s.do(dve.reduce_sum(glo[:, 0:1], qT[:], X_AXIS))
                s.do(dve.tensor_scalar(glo[:, 1:2], glo[:, 0:1], 1.0 / S, None, ALU.mult))
                for i in range(TB):
                    dve.wait_ge(tok, b * TB + i + 1)
                    dve.tensor_tensor(qkv[:, b * TB + i, :], ps[4 + i % 2][:, 0:3 * D], biases[:],
                                      ALU.add).then_inc(evac, 1)
                dve.wait_ge(pe, b * PE_STEPS + 3)
                s.do(dve.tensor_tensor(cbias[:, 1:2], ps[6][:, 0:1], cbias[:, 0:1], ALU.add))
                dve.wait_ge(act, b * ACT_STEPS + 6)
                s.do(dve.tensor_scalar(g1[:], ez[:], 1.0, None, ALU.add))
                s.do(dve.reciprocal(g2[:], g1[:, :, 0, :]))
                s.do(dve.tensor_scalar(g2[:], g2[:], float(S), -float(S // 2), ALU.mult, ALU.add))
                s.do(dve.tensor_tensor(g3[:], g1[:, :, 1, :], g1[:, :, 1, :], ALU.mult))
                s.done(dve.tensor_scalar(gco[:, bass.ds(b * TB, TB), 0, :], g3[:], -2.0 / S ** 2, None,
                                         ALU.mult))
                s.do(dve.scalar_tensor_tensor(out=gco[:, bass.ds(b * TB, TB), 1, :], in0=g3[:],
                                              scalar=4.0 / S ** 2, in1=g2[:], op0=ALU.mult, op1=ALU.mult))
                assert s.n == DVE_STEPS, s.n

        @block.scalar
        def _(a):
            a.wait_ge(loaded, N_LOADED)
            with a.Fori(0, B) as b:
                s = Steps(a, act, b * ACT_STEPS)
                a.wait_ge(pe, b * PE_STEPS + 1)
                s.do(a.activation(xT[:], t["tp"][:], ACT.Copy))
                for c in range(2):
                    a.wait_ge(pe, b * PE_STEPS + 2)
                    s.done(a.activation(qT[:, c * 512:(c + 1) * 512], ps[2 + c][:], ACT.Identity,
                                        bias=cols[:, 0:1]))
                a.wait_ge(pe, b * PE_STEPS + 4)
                a.wait_ge(own, 3 + b * DVE_STEPS + TB + 5)
                for c in range(2):
                    s.done(a.activation(cT[:, c * 512:(c + 1) * 512], ps[2 + c][:], ACT.Tanh,
                                        bias=cbias[:, 1:2]))
                a.wait_ge(pe, b * PE_STEPS + 5)
                s.done(a.activation(ez[:].rearrange("p t a h -> p (t a h)"), ps[7][:, 0:2 * H0 * TB],
                                    ACT.Exp, scale=-1.0))
                assert s.n == ACT_STEPS

        @block.tensor
        def _(e):
            e.wait_ge(loaded, N_LOADED)
            with e.Fori(0, B) as b:
                e.wait_ge(trd, b + 1)
                for i in range(TB):
                    last = e.transpose(t["tp"][:, i * P:(i + 1) * P], xn[:, i, :], t["ident"][:])
                last.then_inc(pe, 1)
                e.wait_ge(act, b * ACT_STEPS + 1)
                for c in range(2):
                    last = e.matmul(ps[2 + c][:], wqkv[:, 0:D], xT[:, c * 512:(c + 1) * 512],
                                    start=True, stop=True)
                last.then_inc(pe, 1)
                for i in range(TB):
                    if i >= 2:
                        e.wait_ge(evac, b * TB + i - 1)
                    e.matmul(ps[4 + i % 2][:, 0:3 * D], xT[:, i * P:(i + 1) * P], wqkv[:],
                             start=True, stop=True).then_inc(tok, 1)
                e.wait_ge(own, 3 + b * DVE_STEPS + TB + 4)
                e.matmul(ps[6][:, 0:1], wfg[:], glo[:, 1:2], start=True, stop=True).then_inc(pe, 1)
                for c in range(2):
                    last = e.matmul(ps[2 + c][:], wfq[:], qT[:, c * 512:(c + 1) * 512],
                                    start=True, stop=True)
                last.then_inc(pe, 1)
                e.wait_ge(act, b * ACT_STEPS + 5)
                for i in range(TB):
                    last = e.matmul(ps[7][:, i * 2 * H0:(i + 1) * 2 * H0], cT[:, i * P:(i + 1) * P],
                                    upz[:].rearrange("p a h -> p (a h)"), start=True, stop=True)
                last.then_inc(pe, 1)
                e.wait_ge(act, b * ACT_STEPS + 6)
                e.wait_ge(evac, b * TB + TB)


def attend(nc, t, sem, ps):
    ctx = ExitStack()
    with ctx:
        def sb(name, shape, dt=F32):
            return ctx.enter_context(nc.sbuf_tensor(name, shape, dt))

        STEPS = 16
        BS = NG * STEPS
        QH = S // 2
        SCALE = DH0 ** -0.5
        INIT = 4 + NG
        qrow = [sb(f"qrow{i}", [P, TB, GH, R], F32R) for i in range(2)]
        krow = [sb(f"krow{i}", [P, TB, GH, R], F32R) for i in range(2)]
        vaug = [sb(f"vaug{i}", [P, TB, GH, R]) for i in range(NG)]
        qT = [sb(f"aqT{i}", [P, S], F32R) for i in range(NG)]
        kT = [sb(f"akT{i}", [P, S], F32R) for i in range(NG)]
        probs = sb("probs", [P, 4, 2, QH])
        mx = sb("mx", [P, TB, GH])
        mrow = sb("mrow", [P, TB, GH, R], F32R)
        scaled = sb("scaled", [P, TB, R])
        kconst = sb("kconst", [P, TB, 8])
        ctxT = [sb(f"ctxT{i}", [P, QH]) for i in range(2)]
        zeros = sb("zeros", [P, 1536])
        qscale = sb("qscale", [P, TB])
        rden = sb("rden", [P, 4, GH])
        qkv, gco, att = t["qkv"], t["gco"], t["att"]
        scores, ctxp, tp = t["scores"], [ps[4], ps[5]], t["tp2"]
        f32 = lambda ap: ap.bitcast(F32)

        (ld, pool_own, s_ready, p_ready, pv_done, half_copied,
         tp_full, tp_free, dve_own, dve_c, init, zeroed) = (sem("p2_" + n) for n in (
             "loaded", "pool_steps", "scores_ready", "probs_ready", "pv_done", "half_copied",
             "tp_full", "tp_free", "dve_steps", "den_ready", "init_done", "rows_zeroed"))
        block = ctx.enter_context(nc.Block())

        def turn(at, u):
            return [(at, "Q", u, None), (at + 2.5, "K", u, None)]

        def maxima(at, u):
            return [(at + j * 0.4375, "X", u, (j // TB, j % TB)) for j in range(GH * TB)]\
                + [(at + 14.2, "M", u, None)]

        FIRST = [(0, "Q", 0, None), (0, "K", 0, None), *maxima(0, 0), (0, "Q", 1, None), (0, "K", 1, None)]

        def batch_events(last):
            out = []
            for g in range(NG):
                k = g * STEPS
                if not (last and g + 1 == NG):
                    out += maxima(k, g + 1)
                if not (last and g + 2 >= NG):
                    out += turn(k + 5.1, g + 2)
                if g:
                    out.append((k + 3.3, "C", 2 * g - 1, None))
                out.append((k + 11.3, "C", 2 * g, None))
            return sorted(out, key=lambda x: x[0]) + [(BS + 1, "C", 2 * NG - 1, None)]

        NF, NE = len(FIRST), len(batch_events(False))
        bodies = lambda last: (batch_events(last), lambda b: NF + b * NE)

        @block.sync
        def _(sp):
            for counter in (tp_full, pv_done, tp_free, p_ready, half_copied):
                sp.sem_inc(counter, START)
            sp.dma_start(kconst[:], t["kconst"]).then_inc(ld, 16)
            sp.wait_ge(init, INIT)
            rows = t["ybuf"].rearrange("(p n) d -> p (n d)", p=P)
            n = rows.shape[1] // zeros.shape[1]
            for i in range(n):
                sp.dma_start(rows[:, bass.ts(i, zeros.shape[1])], zeros[:]).then_inc(zeroed, 16)
            sp.wait_ge(zeroed, 16 * n)

        POOL_STEPS = 14
        POOL_FIRST = 2 * GH + NG

        @block.gpsimd
        def _(pool):
            for v in vaug:
                pool.memset(v[:], 0.0).then_inc(init, 1)
            for q in qrow:
                pool.memset(f32(q[:]), 0.0)
            pool.memset(f32(mrow[:]), 0.0).then_inc(init, 1)
            pool.memset(zeros[:], 0.0).then_inc(init, 1)
            pool.memset(qscale[:], SCALE).then_inc(init, 1)
            pool.memset(mx[:], 0.0).then_inc(init, 1)
            pool.wait_ge(ld, 16)
            pool.wait_ge(init, INIT)
            s = Steps(pool, pool_own)
            for i in range(2):
                for h in range(GH):
                    s.done(pool.tensor_copy(krow[i][:, :, h, 24:32], kconst[:]))
            for v in vaug:
                s.done(pool.memset(v[:, :, :, DH0:DH0 + 1], 1.0))
            s.settle()
            assert s.n == POOL_FIRST

            def build(b, u):
                g, i = u % NG, u % 2
                unit = b * NG + u
                s = Steps(pool, pool_own, POOL_FIRST + unit * POOL_STEPS, alone=True)
                tiles = bass.ds((b + u // NG) * TB, TB)
                part = lambda w: qkv[:, tiles, w * D + g * R:w * D + (g + 1) * R]\
                    .rearrange("p t (h d) -> p t h d", h=GH)
                co = lambda w: gco[:, tiles, w, g * GH:(g + 1) * GH]
                tmp = scaled[:].rearrange("p t (h d) -> p t h d", h=GH)
                s.settle()
                if u >= 2:
                    pool.wait_ge(dve_own, 2 * (unit - 1))
                    pool.wait_ge(pv_done, START + (b * NG + max(u - NG + 1, 0)) * STEPS)
                    stand_alone(pool)
                q, k, v = qrow[i], krow[i], vaug[g]
                s.done(pool.tensor_tensor(scaled[:], qkv[:, tiles, g * R:(g + 1) * R],
                                          qscale[:].unsqueeze(2).broadcast_to([P, TB, R]), ALU.mult))
                s.done(pool.tensor_copy(k[:, :, :, 0:8], part(1)))
                s.done(pool.tensor_copy(q[:, :, :, 24], co(0)))
                s.done(pool.tensor_copy(q[:, :, :, 28], co(1)))
                s.done(pool.tensor_copy(v[:, :, :, 0:DH0], part(2)))
                s.settle()
                s.done(pool.tensor_copy(q[:, :, :, 0:8], tmp))
                s.done(pool.tensor_copy(k[:, :, :, 16:24], f32(k[:, :, :, 0:8])))
                s.done(pool.tensor_tensor(k[:, :, :, 8:16], part(1), f32(k[:, :, :, 0:8]), ALU.subtract))
                s.done(pool.tensor_copy(q[:, :, :, 25], f32(q[:, :, :, 24])))
                s.done(pool.tensor_tensor(q[:, :, :, 26], co(0), f32(q[:, :, :, 24]), ALU.subtract))
                s.settle()
                s.done(pool.tensor_copy(q[:, :, :, 27], f32(q[:, :, :, 26])))
                s.done(pool.tensor_tensor(q[:, :, :, 29], co(1), f32(q[:, :, :, 28]), ALU.subtract))
                s.done(pool.tensor_copy(q[:, :, :, 8:16], f32(q[:, :, :, 0:8])))
                s.done(pool.tensor_tensor(q[:, :, :, 16:24], tmp, f32(q[:, :, :, 0:8]), ALU.subtract))
                assert s.n == POOL_STEPS, s.n

            for u in range(2):
                build(0, u)
            with pool.Fori(0, B - 1) as b:
                for u in range(2, NG + 2):
                    build(b, u)
            for u in range(2, NG):
                build(B - 1, u)

        @block.tensor
        def _(e):
            def event(b, seen, ev):
                _, kind, u, at = ev
                e.wait_ge(tp_free, START + seen)
                if kind == "C":
                    e.wait_ge(half_copied, START + b * 2 * NG + u + 1)
                    for i in range(4):
                        last = e.transpose(tp[:, i * P:(i + 1) * P], ctxT[u % 2][:, i * P:(i + 1) * P],
                                           t["ident"][:])
                elif kind == "X":
                    h, i = at
                    for c in range(2):
                        last = e.matmul(tp[:, c * 512:(c + 1) * 512],
                                        qT[u % NG][h * R:(h + 1) * R, i * P:(i + 1) * P],
                                        kT[u % NG][h * R:(h + 1) * R, c * 512:(c + 1) * 512],
                                        start=True, stop=True)
                else:
                    if kind == "M":
                        e.wait_ge(dve_own, (b * NG + u + 1) * 2)
                    else:
                        e.wait_ge(pool_own, POOL_FIRST + (b * NG + u + 1) * POOL_STEPS)
                    src = {"Q": qrow[u % 2], "K": krow[u % 2], "M": mrow}[kind]
                    for i in range(TB):
                        last = e.transpose(tp[:, i * P:(i + 1) * P],
                                           f32(src[:, i, :, :]).rearrange("p h r -> p (h r)"), t["ident"][:])
                last.then_inc(tp_full, 1)

            def score_step(b, n):
                g, hf, kt, pair = n // 32, n // 16 % 2, n // 2 % 8, n % 2
                if n:
                    e.wait_ge(p_ready, START + b * 2 * BS + max(n - 1, 0))
                for j in range(2):
                    h = 2 * pair + j
                    last = e.matmul(scores[:, n % 2, j, :],
                                    kT[g][h * R:(h + 1) * R, kt * P:(kt + 1) * P],
                                    qT[g][h * R:(h + 1) * R, hf * QH:(hf + 1) * QH],
                                    start=True, stop=True)
                last.then_inc(s_ready, 1)

            def values_step(b, k):
                g, hf, kt = k // STEPS, k // 8 % 2, k % 8
                e.wait_ge(p_ready, START + b * 2 * BS + 2 * k + 2)
                if kt == 0:
                    e.wait_ge(half_copied, START + b * 2 * NG + max(2 * g + hf - 1, 0))
                for h in range(GH):
                    last = e.matmul(ctxp[hf][h * R:(h + 1) * R, :], vaug[g][:, kt, h, :],
                                    probs[:, (2 * k + h // 2) % 4, h % 2, :],
                                    start=(kt == 0), stop=(kt == 7))
                last.then_inc(pv_done, 1)

            def batch(b, last):
                events, base = bodies(last)
                seen = [0]

                def events_to(place):
                    while seen[0] < len(events) and events[seen[0]][0] < place:
                        event(b, base(b) + seen[0], events[seen[0]])
                        seen[0] += 1

                e.wait_ge(tp_free, START + base(b))
                for k in range(BS + 1):
                    if k % STEPS == 0 and 0 < k < BS:
                        n = [x[1:3] for x in events].index(("M", k // STEPS))
                        e.wait_ge(tp_free, START + base(b) + n + 1)
                    if k < BS:
                        score_step(b, 2 * k)
                        events_to(k + 0.3)
                        score_step(b, 2 * k + 1)
                        events_to(k + 0.7)
                    if k:
                        values_step(b, k - 1)
                    events_to(k + 1)
                events_to(BS + 2)
                e.wait_ge(tp_free, START + base(b) + len(events))

            for n, ev in enumerate(FIRST):
                event(0, n, ev)
            with e.Fori(0, B - 1) as b:
                batch(b, False)
            batch(B - 1, True)

        @block.scalar
        def _(a):
            with a.Fori(0, B) as b:
                for n in range(2 * BS):
                    a.wait_ge(s_ready, b * 2 * BS + n + 1)
                    if n % 2 == 0:
                        a.wait_ge(pv_done, START + b * BS + max(n // 2 - 1, 0))
                    a.activation(probs[:, n % 4, :, :], scores[:, n % 2, :, :], ACT.Exp)\
                        .then_inc(p_ready, 1)

        @block.vector
        def _(dve):
            dve.wait_ge(init, INIT)

            def event(b, seen, ev):
                _, kind, u, at = ev
                if kind == "C":
                    dve.wait_ge(pv_done, START + b * BS + 8 * (u + 1))
                    dve.tensor_copy(ctxT[u % 2][:], ctxp[u % 2][:]).then_inc(half_copied, 1)
                    dve.wait_ge(tp_full, START + seen + 1)
                    v = tp[:, 0:512].rearrange("p (i h r) -> p i h r", i=4, h=GH)
                    dve.reciprocal(rden[:], v[:, :, :, DH0]).then_inc(dve_c, 1)
                    dve.wait_ge(dve_c, b * 2 * NG + u + 1)
                    g, hf = u // 2, u % 2
                    o = att[:, bass.ds(b * TB + 4 * hf, 4), g * R:(g + 1) * R]\
                        .rearrange("p i (h d) -> p i h d", h=GH)
                    dve.tensor_tensor(o, v[:, :, :, 0:DH0],
                                      rden[:].unsqueeze(3).broadcast_to([P, 4, GH, DH0]),
                                      ALU.mult).then_inc(tp_free, 1)
                elif kind == "X":
                    h, i = at
                    dve.wait_ge(tp_full, START + seen + 1)
                    dve.reduce_max(mx[:, i, h:h + 1], tp[:], X_AXIS).then_inc(tp_free, 1)
                elif kind == "M":
                    dve.wait_ge(tp_free, START + seen)
                    s = Steps(dve, dve_own, (b * NG + u) * 2)
                    s.do(dve.tensor_copy(mrow[:, :, :, 30], mx[:]))
                    s.do(dve.tensor_tensor(mrow[:, :, :, 31], mx[:], f32(mrow[:, :, :, 30]), ALU.subtract))
                    dve.wait_ge(tp_full, START + seen + 1)
                    q = qT[u % NG][:]
                    dve.tensor_tensor(q, f32(q), tp[:], ALU.add).then_inc(tp_free, 1)
                else:
                    dve.wait_ge(tp_full, START + seen + 1)
                    dve.tensor_copy({"Q": qT, "K": kT}[kind][u % NG][:], tp[:]).then_inc(tp_free, 1)

            def batch(b, last):
                events, base = bodies(last)
                for n, ev in enumerate(events):
                    event(b, base(b) + n, ev)

            for n, ev in enumerate(FIRST):
                event(0, n, ev)
            with dve.Fori(0, B - 1) as b:
                batch(b, False)
            batch(B - 1, True)
CH = 4
NC = NT // CH
E0, K0, CAP, I0 = 64, 6, 64, 88
SI = 2 * I0
ROW = 2 * D
N_TOK = B * S


def finish_stats(dve, s, stats, mv, tmp, n):
    s.done(dve.tensor_tensor(mv[:, 0, :], stats[:, :, 1], stats[:, :, 4], ALU.add))
    s.done(dve.tensor_tensor(tmp[:, 0, :], stats[:, :, 1], stats[:, :, 4], ALU.subtract))
    s.do(dve.tensor_tensor(tmp[:, 1, :], stats[:, :, 2], stats[:, :, 5], ALU.add))
    s.done(dve.tensor_scalar(mv[:, 0, :], mv[:, 0, :], 0.5, None, ALU.mult))
    s.done(dve.tensor_scalar(tmp[:, 1, :], tmp[:, 1, :], 1.0 / D, EPS, ALU.mult, ALU.add))
    s.do(dve.scalar_tensor_tensor(out=tmp[:, 0, :], in0=tmp[:, 0, :], scalar=0.25, in1=tmp[:, 0, :],
                                  op0=ALU.mult, op1=ALU.mult))
    s.do(dve.tensor_tensor(mv[:, 1, :], tmp[:, 0, :], tmp[:, 1, :], ALU.add))


STATS_STEPS = 7


def output_projection(nc, t, sem, ps):
    ctx = ExitStack()
    with ctx:
        def sb(name, shape, dt=F32):
            return ctx.enter_context(nc.sbuf_tensor(name, shape, dt))

        wo, bo = sb("wo0", [P, D]), sb("bo0", [P, D])
        ctile = sb("ctile", [P, 2, CH, D])
        cT = sb("ctxTt", [P, 2, CH * P])
        stats, tmp = sb("stats3", [P, NT, 6]), sb("tmp3", [P, 2, NT])
        X, att, mv = t["X"], t["att"], t["mv"]
        loaded, biased, taken, turned, turned_sb, proj, added, own, varr = (sem("p3_" + n) for n in (
            "loaded", "x_biased", "ctx_taken", "turned", "turned_copied", "projected", "added",
            "dve_steps", "var_ready"))
        block = ctx.enter_context(nc.Block())

        @block.sync
        def _(sp):
            for counter in (turned, added):
                sp.sem_inc(counter, START)
            sp.dma_start(wo[:], t["wo"]).then_inc(loaded, 16)
            sp.dma_start(bo[:], t["bo"].partition_broadcast(P)).then_inc(loaded, 16)

        @block.gpsimd
        def _(pool):
            pool.wait_ge(loaded, 32)
            with pool.Fori(0, NC) as c:
                pool.tensor_tensor(X[:, bass.ds(c * CH, CH), :], X[:, bass.ds(c * CH, CH), :],
                                   bo[:].unsqueeze(1).broadcast_to([P, CH, D]), ALU.add).then_inc(biased, 1)
            pool.wait_ge(own, STATS_STEPS)
            pool.tensor_tensor(mv[:, 1, :], mv[:, 1, :], t["neg_half"][:, 0:NT], ALU.pow).then_inc(varr, 1)
            pool.wait_ge(varr, 1)

        @block.scalar
        def _(a):
            with a.Fori(0, NC // 2) as c2:
                for i in range(2):
                    c = 2 * c2 + i
                    a.wait_ge(turned, START + c)
                    a.activation(ctile[:, i, :, :], att[:, bass.ds(c * CH, CH), :], ACT.Copy).then_inc(taken, 1)
                    a.wait_ge(turned, START + c + 1)
                    a.activation(cT[:, i, :], ps[i][:], ACT.Copy).then_inc(turned_sb, 1)

        @block.tensor
        def _(e):
            e.wait_ge(loaded, 32)
            with e.Fori(0, NC // 2) as c2:
                for i in range(2):
                    c = 2 * c2 + i
                    e.wait_ge(taken, c + 1)
                    for k in range(CH):
                        last = e.transpose(ps[i][:, k * P:(k + 1) * P], ctile[:, i, k, :], t["ident"][:])
                    last.then_inc(turned, 1)
                    e.wait_ge(turned_sb, c + 1)
                    e.wait_ge(added, START + c)
                    for k in range(CH):
                        last = e.matmul(ps[2 + i][:, k * D:(k + 1) * D], cT[:, i, k * P:(k + 1) * P], wo[:],
                                        start=True, stop=True)
                    last.then_inc(proj, 1)

        @block.vector
        def _(dve):
            with dve.Fori(0, NC // 2) as c2:
                for i in range(2):
                    c = 2 * c2 + i
                    dve.wait_ge(proj, c + 1)
                    dve.wait_ge(biased, c + 1)
                    xc = X[:, bass.ds(c * CH, CH), :]
                    dve.tensor_tensor(xc, xc, ps[2 + i][:].rearrange("p (k d) -> p k d", k=CH),
                                      ALU.add).then_inc(added, 1)
                    dve.wait_ge(added, START + c + 1)
                    for k in range(CH):
                        dve.bn_stats(stats[:, c * CH + k, :], X[:, c * CH + k, :]).then_inc(t["stat_sem"], 1)
            dve.wait_ge(t["stat_sem"], NT)
            finish_stats(dve, Steps(dve, own), stats, mv, tmp, NT)


def gate_and_shared(nc, t, sem, ps):
    ctx = ExitStack()
    with ctx:
        def sb(name, shape, dt=F32):
            return ctx.enter_context(nc.sbuf_tensor(name, shape, dt))

        gw, gb = sb("gw", [P, E0]), sb("gb", [P, E0])
        ws1, ws3 = sb("ws1", [P, SI]), sb("ws3", [P, SI])
        ws2 = sb("ws2", [I0, 2, D])
        tokv = sb("tokv", [P, NT])
        xrow = sb("xrow", [P, 2, CH, ROW])
        xnT = sb("xnT", [P, 2, CH * P])
        mx, den = sb("gmx", [P, 2, CH]), sb("gden", [P, 2, CH])
        sc = sb("gsc", [P, CH, E0])
        sel, rep, mask = sb("sel", [P, CH, E0]), sb("rep", [P, CH, E0]), sb("mask", [P, CH, E0])
        top = sb("top", [P, CH, 8])
        keyrow = sb("keyrow", [P, CH, E0])
        zero = sb("gzero", [P, E0])
        silu = sb("silu", [I0, 2 * CH * P])
        hid = sb("hid", [I0, 2, 2 * CH * P])
        X, mv, keys = t["X"], t["mv"], t["keys"]
        (loaded, norm, turned, turned_sb, up, sil, hrd, down, gat, ex, own, kt, stored, ysum) = (
            sem("p4_" + n) for n in ("loaded", "x_normed", "turned", "turned_copied", "up_done", "silu_done",
                                     "hidden_ready", "down_done", "gate_done", "exp_done", "dve_steps",
                                     "keys_turned", "rows_stored", "z_added"))
        block = ctx.enter_context(nc.Block())
        rows = t["rows"].rearrange("(c k p) r -> c p k r", k=CH, p=P)
        DVE_STEPS = 9 + 3 * CH
        FIRST = 2

        @block.sync
        def _(sp):
            for counter in (stored, hrd, ysum, kt):
                sp.sem_inc(counter, START)
            for dst, src in ((gw[:], "gate_wT"), (ws1[:], "ws1T"), (ws3[:], "ws3T"), (ws2[:], "ws2T"),
                             (tokv[:], "tokv")):
                sp.dma_start(dst, t[src]).then_inc(loaded, 16)
            sp.dma_start(gb[:], t["gate_b0"].partition_broadcast(P)).then_inc(loaded, 16)
            with sp.Fori(0, NC // 2) as c2:
                for i in range(2):
                    c = 2 * c2 + i
                    sp.wait_ge(own, FIRST + (c + 1) * DVE_STEPS)
                    sp.dma_start(rows[c], xrow[:, i, :, :]).then_inc(stored, 16)
            sp.wait_ge(stored, START + 16 * NC)

        @block.scalar
        def _(a):
            with a.Fori(0, NC // 2) as c2:
                for i in range(2):
                    c = 2 * c2 + i
                    a.wait_ge(turned, c + 1)
                    a.activation(xnT[:, i, :], ps[0][:], ACT.Copy).then_inc(turned_sb, 1)
                    a.wait_ge(own, FIRST + c * DVE_STEPS + 2)
                    a.activation(xrow[:, i, :, D:D + E0], sc[:], ACT.Exp).then_inc(ex, 1)
                    a.wait_ge(up, c + 1)
                    a.wait_ge(hrd, START + c)
                    a.activation(silu[:], t["bank23"][0:I0, :], ACT.Silu).then_inc(sil, 1)

        @block.tensor
        def _(e):
            e.wait_ge(loaded, 16 * 6)
            with e.Fori(0, NC // 2) as c2:
                for i in range(2):
                    c = 2 * c2 + i
                    e.wait_ge(norm, c + 1)
                    for k in range(CH):
                        last = e.transpose(ps[0][:, k * P:(k + 1) * P], xrow[:, i, k, 0:D], t["ident"][:])
                    last.then_inc(turned, 1)
                    e.wait_ge(turned_sb, c + 1)
                    for k in range(CH):
                        last = e.matmul(ps[1][:, k * E0:(k + 1) * E0], xnT[:, i, k * P:(k + 1) * P], gw[:],
                                        start=True, stop=True)
                    last.then_inc(gat, 1)
                    e.wait_ge(hrd, START + c)
                    for w, bank in ((ws1, 2), (ws3, 4)):
                        for f in range(2):
                            last = e.matmul(ps[bank + f][0:I0, :], w[:, f * I0:(f + 1) * I0], xnT[:, i, :],
                                            start=True, stop=True)
                    last.then_inc(up, 1)
                    e.wait_ge(hrd, START + c + 1)
                    e.wait_ge(ysum, START + c)
                    for k in range(CH):
                        for f in range(2):
                            last = e.matmul(ps[6][:, k * D:(k + 1) * D],
                                            hid[:, i, f * CH * P + k * P:f * CH * P + (k + 1) * P],
                                            ws2[:, f, :], start=(f == 0), stop=(f == 1))
                    last.then_inc(down, 1)
                    e.wait_ge(own, FIRST + (c + 1) * DVE_STEPS)
                    stand_alone(e)
                    for k in range(CH):
                        last = e.transpose(ps[7][0:E0, k * P:(k + 1) * P], keyrow[:, k, :], t["ident"][:])
                    last.then_inc(kt, 1)

        @block.vector
        def _(dve):
            dve.wait_ge(loaded, 16 * 6)
            s = Steps(dve, own)
            s.done(dve.memset(zero[:], 0.0))
            s.do(dve.memset(xrow[:], 0.0))

            def normalise(c, i):
                for k in range(CH):
                    tile = c * CH + k
                    last = dve.tensor_scalar(xrow[:, i, k, 0:D], X[:, tile, :], mv[:, 0, bass.ds(tile, 1)],
                                             mv[:, 1, bass.ds(tile, 1)], ALU.subtract, ALU.mult)
                last.then_inc(norm, 1)

            with dve.Fori(0, NC // 2) as c2:
                for i in range(2):
                    c = 2 * c2 + i
                    s = Steps(dve, own, FIRST + c * DVE_STEPS, alone=True)
                    dve.wait_ge(stored, START + 16 * c)
                    normalise(c, i)
                    dve.wait_ge(gat, c + 1)
                    g = ps[1][:, 0:CH * E0].rearrange("p (k e) -> p k e", k=CH)
                    bc = lambda ap: ap.unsqueeze(2).broadcast_to([P, CH, E0])
                    score, rank = xrow[:, i, :, D:D + E0], xrow[:, i, :, D + E0:ROW]
                    s.do(dve.reduce_max(mx[:, i, :], g, X_AXIS))
                    s.do(dve.tensor_tensor(sc[:], g, bc(mx[:, i, :]), ALU.subtract))
                    dve.wait_ge(sil, c + 1)
                    dve.tensor_tensor(hid[:, i, :], silu[:], t["bank45"][0:I0, :], ALU.mult).then_inc(hrd, 1)
                    dve.wait_ge(ex, c + 1)
                    s.do(dve.reduce_sum(den[:, i, :], score, X_AXIS))
                    s.do(dve.reciprocal(den[:, i, :], den[:, i, :]))
                    s.do(dve.tensor_tensor(score, score, bc(den[:, i, :]), ALU.mult))
                    s.do(dve.tensor_tensor(sel[:], score, gb[:].unsqueeze(1).broadcast_to([P, CH, E0]),
                                           ALU.add))
                    for k in range(CH):
                        s.done(dve.max(top[:, k, :], sel[:, k, :]))
                    s.settle()
                    s.do(dve.memset(top[:, :, K0:8], 3.0e38))
                    for k in range(CH):
                        s.done(dve.match_replace(rep[:, k, :], top[:, k, :], sel[:, k, :], -3.0e38))
                    s.settle()
                    s.do(dve.tensor_tensor(mask[:], rep[:], sel[:], ALU.not_equal))
                    for k in range(CH):
                        s.done(dve.tensor_tensor_scan(xrow[:, i, k, D + E0:ROW], mask[:, k, :], zero[:],
                                                      0.0, ALU.add, ALU.add))
                    dve.wait_ge(kt, START + c)
                    s.do(dve.tensor_tensor(keyrow[:], mask[:], bc(tokv[:, bass.ds(c * CH, CH)]), ALU.mult))
                    assert s.n == DVE_STEPS
                    dve.wait_ge(down, c + 1)
                    xc = X[:, bass.ds(c * CH, CH), :]
                    dve.tensor_tensor(xc, xc, ps[6][:].rearrange("p (k d) -> p k d", k=CH),
                                      ALU.add).then_inc(ysum, 1)
                    dve.wait_ge(kt, START + c + 1)
                    dve.tensor_copy(keys[:, bass.ds(c * CH * P, CH * P)], ps[7][0:E0, :]).then_inc(t["keys_in"], 1)
            dve.wait_ge(t["keys_in"], NC)


def pick_slots(nc, t, sem, ps):
    ctx = ExitStack()
    with ctx:
        def sb(name, shape, dt=F32):
            return ctx.enter_context(nc.sbuf_tensor(name, shape, dt))

        half = N_TOK // 2
        fold = sb("fold", [P, half])
        work = sb("work", [P, half])
        first = sb("firstk", [P, CAP])
        both = sb("bothk", [E0, 2 * CAP])
        both2 = sb("bothk2", [E0, 2 * CAP])
        found = sb("found", [E0, CAP])
        keys, slotv = t["keys"], t["slotv"]
        own, turned = sem("p5_dve_steps"), sem("p5_turned")
        block = ctx.enter_context(nc.Block())

        @block.vector
        def _(dve):
            s = Steps(dve, own)
            s.done(dve.tensor_copy(fold[0:E0, :], keys[:, 0:half]))
            s.do(dve.tensor_copy(fold[E0:P, :], keys[:, half:N_TOK]))

            def largest(out, a, b):
                for r in range(CAP // 8):
                    s.do(dve.max(out[:, r * 8:(r + 1) * 8], a[:]))
                    s.do(dve.match_replace(b[:], out[:, r * 8:(r + 1) * 8], a[:], 0.0))
                    a, b = b, a
            largest(first, fold, work)
            s.done(dve.tensor_copy(both[:, 0:CAP], first[0:E0, :]))
            s.do(dve.tensor_copy(both[:, CAP:2 * CAP], first[E0:P, :]))
            largest(found, both, both2)
            dve.wait_ge(turned, 1)
            v = ps[0][0:CAP, 0:E0].rearrange("p (j o) -> p j o", o=2)
            s.done(dve.tensor_copy(slotv[0:CAP, :], v[:, :, 0]))
            s.do(dve.tensor_copy(slotv[CAP:P, :], v[:, :, 1]))
            s.do(dve.tensor_scalar(t["tok"][:], slotv[:], -1.0, float(N_TOK), ALU.mult, ALU.add))
            s.do(dve.tensor_scalar(t["gidx"][:], t["tok"][:], float(N_TOK - 1), None, ALU.min))
            s.do(dve.tensor_scalar(t["full"][:], slotv[:], 0.0, None, ALU.is_gt))
            t["pick_steps"] = s.n

        @block.tensor
        def _(e):
            e.wait_ge(own, t["pick_steps"] - 5)
            e.transpose(ps[0][0:CAP, 0:E0], found[:], t["ident"][0:E0, 0:E0]).then_inc(turned, 1)


def routed_experts(nc, t, sem, ps):
    ctx = ExitStack()
    with ctx:
        def sb(name, shape, dt=F32):
            return ctx.enter_context(nc.sbuf_tensor(name, shape, dt))

        GT = 4
        NGR = E0 // 2 // GT
        EG = 2 * GT
        w1 = sb("w1b", [P, 2, EG * I0])
        w3 = sb("w3b", [P, 2, EG * I0])
        w2 = sb("w2b", [I0, 2, EG * D])
        xg = [sb(f"xg{i}", [P, GT, ROW]) for i in range(2)]
        sidx = [sb(f"sidx{i}", [P, GT], I32) for i in range(2)]
        didx = [sb(f"didx{i}", [P, GT], I32) for i in range(2)]
        yo = [sb(f"yo{i}", [P, GT, D]) for i in range(2)]
        xT = sb("xgT", [P, GT * P])
        silu = sb("silu5", [I0, GT * P])
        hid = sb("hid5", [I0, GT * P])
        sr = sb("scorerank", [P, GT, 2])
        dst = sb("dstf", [P, GT])
        wl, ixr, gth, turned, turned_sb, up, sil, hrd, down, own, sct, yrd = (sem("p6_" + n) for n in (
            "weights", "index_ready", "gathered", "turned", "turned_copied", "up_done", "silu_done",
            "hidden_ready", "down_done", "dve_steps", "scattered", "y_ready"))
        block = ctx.enter_context(nc.Block())
        DVE_STEPS = EG + 4
        tok, full, gidx = t["tok"], t["full"], t["gidx"]

        @block.sync
        def _(sp):
            for counter in (down, yrd, hrd):
                sp.sem_inc(counter, START)
            with sp.Fori(0, NGR // 2) as g2:
                for i in range(2):
                    g = 2 * g2 + i
                    sp.wait_ge(down, START + g)
                    sp.dma_start(w1[:, i, :], t["w1T"][:, bass.ds(g * EG * I0, EG * I0)]).then_inc(wl, 16)
                    sp.dma_start(w3[:, i, :], t["w3T"][:, bass.ds(g * EG * I0, EG * I0)]).then_inc(wl, 16)
                    sp.dma_start(w2[:, i, :], t["w2T"][:, bass.ds(g * EG * D, EG * D)]).then_inc(wl, 16)

        @block.gpsimd
        def _(pool):
            def scatter(g, i):
                pool.wait_ge(yrd, START + g + 1)
                stand_alone(pool)
                for k in range(GT):
                    pool.indirect_dma_start(
                        out=t["ybuf"], out_offset=bass.IndirectOffsetOnAxis(ap=didx[i][:, k:k + 1], axis=0),
                        in_=yo[i][:, k, :], in_offset=None, bounds_check=N_TOK * K0 - 1,
                        oob_is_err=False).then_inc(sct, 16)

            with pool.Fori(0, NGR // 2) as g2:
                for i in range(2):
                    g = 2 * g2 + i
                    pool.wait_ge(yrd, START + g)
                    stand_alone(pool)
                    pool.tensor_copy(sidx[i][:], gidx[:, bass.ds(g * GT, GT)]).then_inc(ixr, 1)
                    pool.wait_ge(ixr, g + 1)
                    stand_alone(pool)
                    for k in range(GT):
                        pool.indirect_dma_start(
                            out=xg[i][:, k, :], out_offset=None, in_=t["rows"],
                            in_offset=bass.IndirectOffsetOnAxis(ap=sidx[i][:, k:k + 1], axis=0)
                        ).then_inc(gth, 16)
                    scatter(g, i)
                pool.wait_ge(sct, 16 * GT * 2 * (g2 + 1))
                stand_alone(pool)
            pool.wait_ge(sct, 16 * GT * NGR)

        @block.scalar
        def _(a):
            with a.Fori(0, NGR // 2) as g2:
                for i in range(2):
                    g = 2 * g2 + i
                    a.wait_ge(turned, g + 1)
                    a.activation(xT[:], ps[0][:], ACT.Copy).then_inc(turned_sb, 1)
                    a.wait_ge(up, g + 1)
                    a.activation(silu[:], ps[1][0:I0, :], ACT.Silu).then_inc(sil, 1)

        @block.tensor
        def _(e):
            with e.Fori(0, NGR // 2) as g2:
                for i in range(2):
                    g = 2 * g2 + i
                    e.wait_ge(gth, (g + 1) * 16 * GT)
                    for k in range(GT):
                        last = e.transpose(ps[0][:, k * P:(k + 1) * P], xg[i][:, k, 0:D], t["ident"][:])
                    last.then_inc(turned, 1)
                    e.wait_ge(turned_sb, g + 1)
                    e.wait_ge(wl, (g + 1) * 48)
                    e.wait_ge(hrd, START + g)
                    for w, bank in ((w1, 1), (w3, 2)):
                        for x in range(EG):
                            last = e.matmul(ps[bank][0:I0, x * CAP:(x + 1) * CAP],
                                            w[:, i, x * I0:(x + 1) * I0], xT[:, x * CAP:(x + 1) * CAP],
                                            start=True, stop=True)
                    last.then_inc(up, 1)
                    e.wait_ge(hrd, START + g + 1)
                    e.wait_ge(yrd, START + g)
                    for x in range(EG):
                        last = e.matmul(ps[3][(x % 2) * CAP:(x % 2 + 1) * CAP, (x // 2) * D:(x // 2 + 1) * D],
                                        hid[:, x * CAP:(x + 1) * CAP], w2[:, i, x * D:(x + 1) * D],
                                        start=True, stop=True)
                    last.then_inc(down, 1)

        @block.vector
        def _(dve):
            with dve.Fori(0, NGR // 2) as g2:
                for i in range(2):
                    g = 2 * g2 + i
                    s = Steps(dve, own, g * DVE_STEPS)
                    dve.wait_ge(gth, (g + 1) * 16 * GT)
                    dve.wait_ge(yrd, START + g)
                    for k in range(GT):
                        v = xg[i][:, k, D:ROW].rearrange("p (a e) -> p a e", a=2)
                        for o in range(2):
                            h = slice(o * CAP, (o + 1) * CAP)
                            s.done(dve.tensor_copy(sr[h, k, :], v[h, :, bass.ds(g * EG + 2 * k + o, 1)]
                                                   .squeeze(2)))
                    s.settle()
                    s.do(dve.tensor_tensor(sr[:, :, 0], sr[:, :, 0], full[:, bass.ds(g * GT, GT)], ALU.mult))
                    s.do(dve.scalar_tensor_tensor(out=dst[:], in0=tok[:, bass.ds(g * GT, GT)],
                                                  scalar=float(K0), in1=sr[:, :, 1], op0=ALU.mult,
                                                  op1=ALU.add))
                    s.do(dve.scalar_tensor_tensor(out=dst[:], in0=full[:, bass.ds(g * GT, GT)],
                                                  scalar=-8.0, in1=dst[:], op0=ALU.mult, op1=ALU.add))
                    s.do(dve.tensor_scalar(didx[i][:], dst[:], 7.0, None, ALU.add))
                    assert s.n == DVE_STEPS
                    dve.wait_ge(sil, g + 1)
                    dve.tensor_tensor(hid[:], silu[:], ps[2][0:I0, :], ALU.mult).then_inc(hrd, 1)
                    dve.wait_ge(down, START + g + 1)
                    dve.tensor_tensor(yo[i][:], ps[3][:].rearrange("p (k d) -> p k d", k=GT),
                                      sr[:, :, 0].unsqueeze(2).broadcast_to([P, GT, D]),
                                      ALU.mult).then_inc(yrd, 1)
H1, DH1 = 4, 32
FF = 4 * D
E1, F1 = 8, 256
KSCALE = DH1 ** -0.25


def rstd_of(pool, t, own, steps, ready):
    pool.wait_ge(own, steps)
    pool.tensor_tensor(t["mv"][:, 1, :], t["mv"][:, 1, :], t["neg_half"][:, 0:NT], ALU.pow).then_inc(ready, 1)


def normalise_chunk(dve, out, src, mv, c):
    for k in range(CH):
        tile = c * CH + k
        last = dve.tensor_scalar(out[:, k, :], src[:, tile, :], mv[:, 0, bass.ds(tile, 1)],
                                 mv[:, 1, bass.ds(tile, 1)], ALU.subtract, ALU.mult)
    return last


def combine(nc, t, sem, ps):
    ctx = ExitStack()
    with ctx:
        def sb(name, shape, dt=F32):
            return ctx.enter_context(nc.sbuf_tensor(name, shape, dt))

        yk = sb("yk", [P, 2, CH, K0 * D])
        ysum = sb("ysumt", [P, CH, D])
        stats, tmp = sb("stats7", [P, NT, 6]), sb("tmp7", [P, 2, NT])
        X, XO, mv = t["X"], t["XO"], t["mv"]
        ld, summed, added, stat, own, var1, nrm = (sem("p7_" + n) for n in (
            "rows_loaded", "summed", "added", "stats", "dve_steps", "rstd_ready", "normed"))
        block = ctx.enter_context(nc.Block())
        y = t["ybuf"].rearrange("(c k p s) d -> c p k (s d)", k=CH, p=P, s=K0)

        @block.sync
        def _(sp):
            for counter in (summed,):
                sp.sem_inc(counter, START)
            with sp.Fori(0, NC // 2) as c2:
                for i in range(2):
                    c = 2 * c2 + i
                    sp.wait_ge(summed, START + c)
                    sp.dma_start(yk[:, i, :, :], y[c]).then_inc(ld, 16)

        @block.gpsimd
        def _(pool):
            rstd_of(pool, t, own, STATS_STEPS, var1)
            rstd_of(pool, t, own, 2 * STATS_STEPS, var1)
            pool.wait_ge(var1, 2)

        @block.vector
        def _(dve):
            with dve.Fori(0, NC // 2) as c2:
                for i in range(2):
                    c = 2 * c2 + i
                    dve.wait_ge(ld, (c + 1) * 16)
                    for k in range(CH):
                        last = dve.reduce_sum(ysum[:, k, :], yk[:, i, k, :].rearrange("p (s d) -> p d s", s=K0),
                                              X_AXIS)
                    last.then_inc(summed, 1)
                    dve.wait_ge(summed, START + c + 1)
                    xc = X[:, bass.ds(c * CH, CH), :]
                    dve.tensor_tensor(xc, xc, ysum[:], ALU.add).then_inc(added, 1)
                    dve.wait_ge(added, c + 1)
                    for k in range(CH):
                        dve.bn_stats(stats[:, c * CH + k, :], X[:, c * CH + k, :]).then_inc(stat, 1)
            dve.wait_ge(stat, NT)
            finish_stats(dve, Steps(dve, own), stats, mv, tmp, NT)
            dve.wait_ge(var1, 1)
            with dve.Fori(0, NC) as c:
                normalise_chunk(dve, XO[:, bass.ds(c * CH, CH), :], X, mv, c).then_inc(nrm, 1)
                dve.wait_ge(nrm, c + 1)
                for k in range(CH):
                    dve.bn_stats(stats[:, c * CH + k, :], XO[:, c * CH + k, :]).then_inc(stat, 1)
            dve.wait_ge(stat, 2 * NT)
            finish_stats(dve, Steps(dve, own, STATS_STEPS), stats, mv, tmp, NT)


def linear_attention(nc, t, sem, ps):
    ctx = ExitStack()
    with ctx:
        def sb(name, shape, dt=F32):
            return ctx.enter_context(nc.sbuf_tensor(name, shape, dt))

        CB = TB // CH
        wk, wqv, wo, bo = sb("wk1", [P, D]), sb("wqv1", [P, 2 * D]), sb("wo1", [P, D]), sb("bo1", [P, D])
        lncol = sb("ln1col", [P, 2])
        block32 = sb("block32", [P, D])
        h = sb("h1", [P, 2, CH, D])
        hT = sb("h1T", [P, 2, CH * P])
        kT, ke = sb("k1T", [P, S]), sb("k1e", [P, S])
        ktok, vtok = sb("ktok", [P, TB, D]), sb("vtok", [P, TB, D])
        qs, qe = sb("qs", [P, CH, D]), sb("qe", [P, CH, D])
        qT = sb("q1T", [P, S])
        qm, qd = sb("qm", [P, CH * H1]), sb("qd", [P, CH * H1])
        km, ksum, krec = sb("km", [P, 2]), sb("ksum", [P, 1]), sb("krec", [P, 1])
        cmat = sb("cmat", [P, D])
        aT = sb("a1T", [P, S])
        stats, tmp = sb("stats8", [P, NT, 6]), sb("tmp8", [P, 2, NT])
        XO, mv = t["XO"], t["mv"]
        ld, own, nrm, act, pe, biased, stat, rst, own2 = (sem("p8_" + n) for n in (
            "loaded", "dve_steps", "normed", "act_steps", "pe_steps", "xo_biased", "stats", "rstd_ready",
            "stat_steps"))
        block = ctx.enter_context(nc.Block())
        DVE_STEPS, ACT_STEPS, PE_STEPS = 6 * CB + 5 + 2, 4 * CB + 1 + 2, 4 * CB + 4

        @block.sync
        def _(sp):
            for dst, n in ((wk[:], "l1_wk"), (wqv[:, 0:D], "l1_wq"), (wqv[:, D:2 * D], "l1_wv"),
                           (wo[:], "l1_wo"), (block32[:], "block32")):
                sp.dma_start(dst, t[n]).then_inc(ld, 16)
            sp.dma_start(bo[:], t["l1_bo"].partition_broadcast(P)).then_inc(ld, 16)
            for i, n in enumerate(("ln1_g", "ln1_b")):
                sp.dma_start(lncol[:, i:i + 1], t[n].rearrange("(p a) -> p a", a=1)).then_inc(ld, 16)
        LOADED = 16 * 8

        @block.gpsimd
        def _(pool):
            pool.wait_ge(ld, LOADED)
            with pool.Fori(0, B) as b:
                pool.wait_ge(nrm, (b + 1) * CB)
                xc = XO[:, bass.ds(b * TB, TB), :]
                pool.tensor_tensor(xc, xc, bo[:].unsqueeze(1).broadcast_to([P, TB, D]), ALU.add)\
                    .then_inc(biased, 1)
            rstd_of(pool, t, own2, STATS_STEPS, rst)
            pool.wait_ge(rst, 1)

        @block.tensor
        def _(e):
            e.wait_ge(ld, LOADED)
            with e.Fori(0, B) as b:
                a0, d0 = b * ACT_STEPS, b * DVE_STEPS
                for c in range(CB):
                    e.wait_ge(nrm, b * CB + c + 1)
                    for k in range(CH):
                        last = e.transpose(ps[0][:, k * P:(k + 1) * P], h[:, c, k, :], t["ident"][:])
                    last.then_inc(pe, 1)
                    e.wait_ge(act, a0 + 4 * c + 1)
                    e.matmul(ps[1][:], wk[:], hT[:, c, :], start=True, stop=True).then_inc(pe, 1)
                    for k in range(CH):
                        last = e.matmul(ps[2 + k // 2][:, (k % 2) * 2 * D:(k % 2 + 1) * 2 * D],
                                        hT[:, c, k * P:(k + 1) * P], wqv[:], start=True, stop=True)
                    last.then_inc(pe, 1)
                    e.wait_ge(own, d0 + 6 * c + 5)
                    for k in range(CH):
                        last = e.transpose(ps[4][:, k * P:(k + 1) * P], qs[:, k, :], t["ident"][:])
                    last.then_inc(pe, 1)
                    e.wait_ge(own, d0 + 6 * c + 6)
                    e.wait_ge(act, a0 + 4 * c + 4)
                e.wait_ge(act, a0 + 4 * CB + 1)
                for k in range(TB):
                    last = e.transpose(ps[k // CH][:, (k % CH) * P:(k % CH + 1) * P], ke[:, k * P:(k + 1) * P],
                                       t["ident"][:])
                last.then_inc(pe, 1)
                e.wait_ge(own, d0 + 6 * CB + 3)
                for k in range(TB):
                    last = e.matmul(ps[5][:, 0:D], ktok[:, k, :], vtok[:, k, :], start=(k == 0),
                                    stop=(k == TB - 1))
                last.then_inc(pe, 1)
                e.wait_ge(own, d0 + 6 * CB + 5)
                for c in range(2):
                    last = e.matmul(ps[2 + c][:], cmat[:], qT[:, c * 512:(c + 1) * 512], start=True, stop=True)
                last.then_inc(pe, 1)
                e.wait_ge(act, a0 + 4 * CB + 3)
                for k in range(TB):
                    last = e.matmul(ps[6 + k // CH][:, (k % CH) * D:(k % CH + 1) * D],
                                    aT[:, k * P:(k + 1) * P], wo[:], start=True, stop=True)
                last.then_inc(pe, 1)
                e.wait_ge(own, d0 + DVE_STEPS)

        @block.scalar
        def _(a):
            a.wait_ge(ld, LOADED)
            with a.Fori(0, B) as b:
                p0, d0 = b * PE_STEPS, b * DVE_STEPS
                s = Steps(a, act, b * ACT_STEPS)
                for c in range(CB):
                    a.wait_ge(pe, p0 + 4 * c + 1)
                    s.done(a.activation(hT[:, c, :], ps[0][:], ACT.Identity, bias=lncol[:, 1:2],
                                        scale=lncol[:, 0:1]))
                    a.wait_ge(pe, p0 + 4 * c + 2)
                    s.done(a.activation(kT[:, c * 512:(c + 1) * 512], ps[1][:], ACT.Copy))
                    a.wait_ge(own, d0 + 6 * c + 2)
                    for j in range(2):
                        last = a.activation(vtok[:, c * CH + 2 * j:c * CH + 2 * j + 2, :],
                                            ps[2 + j][:].rearrange("p (k w d) -> p k w d", k=2, w=2)[:, :, 1, :],
                                            ACT.Copy)
                    s.done(last)
                    s.done(a.activation(qe[:], qs[:], ACT.Exp, scale=KSCALE))
                a.wait_ge(own, d0 + 6 * CB + 2)
                s.done(a.activation(ke[:], kT[:], ACT.Exp, bias=km[:, 1:2], scale=KSCALE,
                                    accum_out=ksum[:]))
                a.wait_ge(pe, p0 + 4 * CB + 3)
                for c in range(2):
                    s.done(a.activation(aT[:, c * 512:(c + 1) * 512], ps[2 + c][:], ACT.Copy))
                assert s.n == ACT_STEPS

        @block.vector
        def _(dve):
            dve.wait_ge(ld, LOADED)
            with dve.Fori(0, B) as b:
                a0, p0 = b * ACT_STEPS, b * PE_STEPS
                s = Steps(dve, own, b * DVE_STEPS)
                for c in range(CB):
                    normalise_chunk(dve, h[:, c, :, :], XO, mv, b * CB + c).then_inc(nrm, 1)
                for c in range(CB):
                    dve.wait_ge(pe, p0 + 4 * c + 3)
                    for j in range(2):
                        v = ps[2 + j][:].rearrange("p (k w h d) -> p k w h d", k=2, w=2, h=H1)[:, :, 0, :, :]
                        last = dve.reduce_max(qm[:, j * 2 * H1:(j + 1) * 2 * H1]
                                              .rearrange("p (k h) -> p k h", k=2), v, X_AXIS)
                    s.do(last)
                    for j in range(2):
                        v = ps[2 + j][:].rearrange("p (k w h d) -> p k w h d", k=2, w=2, h=H1)
                        for k in range(2):
                            m = qm[:, (2 * j + k) * H1:(2 * j + k + 1) * H1]
                            last = dve.tensor_tensor(
                                qs[:, 2 * j + k, :].rearrange("p (h d) -> p h d", h=H1), v[:, k, 0, :, :],
                                m.unsqueeze(2).broadcast_to([P, H1, DH1]), ALU.subtract)
                    s.do(last)
                    dve.wait_ge(act, a0 + 4 * c + 4)
                    q4 = qe[:].rearrange("p k (h d) -> p (k h) d", h=H1)
                    s.do(dve.reduce_sum(qd[:], q4, X_AXIS))
                    s.do(dve.reciprocal(qd[:], qd[:]))
                    s.done(dve.tensor_tensor(qs[:].rearrange("p k (h d) -> p (k h) d", h=H1), q4,
                                             qd[:].unsqueeze(2).broadcast_to([P, CH * H1, DH1]), ALU.mult))
                    dve.wait_ge(pe, p0 + 4 * c + 4)
                    s.do(dve.tensor_copy(qT[:, c * 512:(c + 1) * 512], ps[4][:]))
                dve.wait_ge(act, a0 + 4 * (CB - 1) + 2)
                s.do(dve.reduce_max(km[:, 0:1], kT[:], X_AXIS))
                s.do(dve.tensor_scalar(km[:, 1:2], km[:, 0:1], -KSCALE, None, ALU.mult))
                dve.wait_ge(pe, p0 + 4 * CB + 1)
                s.done(dve.tensor_copy(ktok[:].rearrange("p k d -> p (k d)"), t["bank01"]))
                s.do(dve.reciprocal(krec[:], ksum[:]))
                dve.wait_ge(pe, p0 + 4 * CB + 2)
                s.do(dve.scalar_tensor_tensor(out=cmat[:], in0=ps[5][:, 0:D], scalar=krec[:],
                                              in1=block32[:], op0=ALU.mult, op1=ALU.mult))
                dve.wait_ge(pe, p0 + 4 * CB + 4)
                dve.wait_ge(biased, b + 1)
                for c in range(CB):
                    xc = XO[:, bass.ds(b * TB + c * CH, CH), :]
                    s.done(dve.tensor_tensor(xc, xc, ps[6 + c][:].rearrange("p (k d) -> p k d", k=CH),
                                             ALU.add))
                s.settle()
                for k in range(TB):
                    dve.bn_stats(stats[:, b * TB + k, :], XO[:, b * TB + k, :]).then_inc(stat, 1)
                assert s.n == DVE_STEPS, (s.n, DVE_STEPS)
            dve.wait_ge(stat, NT)
            finish_stats(dve, Steps(dve, own2), stats, mv, tmp, NT)


def feed_forward(nc, t, sem, ps):
    ctx = ExitStack()
    with ctx:
        def sb(name, shape, dt=F32):
            return ctx.enter_context(nc.sbuf_tensor(name, shape, dt))

        NF = FF // P
        wf1, wf2, wd = sb("wf1", [P, FF]), sb("wf2", [P, NF, D]), sb("wd", [P, D])
        lncol, bf1 = sb("ln2col", [P, 2]), sb("bf1", [P, NF])
        bf2, bd = sb("bf2", [P, D]), sb("bd", [P, D])
        h, hT = sb("h2", [P, 2, CH, D]), sb("h2T", [P, CH * P])
        f = sb("f2", [P, NF, CH * P])
        y, yT = sb("y2", [P, CH, D]), sb("y2T", [P, CH * P])
        yb = sb("yb2", [P, 2, CH, D])
        stats, tmp = sb("stats9", [P, NT, 6]), sb("tmp9", [P, 2, NT])
        X, XO, mv = t["X"], t["XO"], t["mv"]
        ld, nrm, turned, hts, f1, gl, f2, ysum, yturned, yts, d1, xs, stat, own, rst, yb_r, xb_r = (
            sem("p9_" + n) for n in (
                "loaded", "normed", "turned", "turned_copied", "ff1_done", "gelu_done", "ff2_done",
                "y_summed", "y_turned", "y_copied", "wd_done", "x_added", "stats", "dve_steps",
                "rstd_ready", "y_biased", "x_biased"))
        block = ctx.enter_context(nc.Block())

        @block.sync
        def _(sp):
            for counter in (ysum, yts, xs, gl, f2, turned, yturned):
                sp.sem_inc(counter, START)
            for dst, n in ((wf1[:], "w_ff1"), (wd[:], "w_d")):
                sp.dma_start(dst, t[n]).then_inc(ld, 16)
            sp.dma_start(wf2[:], t["w_ff2"].rearrange("(f p) d -> p f d", p=P)).then_inc(ld, 16)
            sp.dma_start(bf1[:], t["b_ff1"]).then_inc(ld, 16)
            sp.dma_start(bf2[:], t["b_ff2"].partition_broadcast(P)).then_inc(ld, 16)
            sp.dma_start(bd[:], t["b_d"].partition_broadcast(P)).then_inc(ld, 16)
            for i, n in enumerate(("ln2_g", "ln2_b")):
                sp.dma_start(lncol[:, i:i + 1], t[n].rearrange("(p a) -> p a", a=1)).then_inc(ld, 16)
        LOADED = 16 * 8

        @block.gpsimd
        def _(pool):
            pool.wait_ge(ld, LOADED)
            with pool.Fori(0, NC // 2) as c2:
                for i in range(2):
                    c = 2 * c2 + i
                    cs = bass.ds(c * CH, CH)
                    pool.wait_ge(ysum, START + c)
                    pool.tensor_tensor(yb[:, i, :, :], XO[:, cs, :],
                                       bf2[:].unsqueeze(1).broadcast_to([P, CH, D]), ALU.add).then_inc(yb_r, 1)
                    pool.tensor_tensor(X[:, cs, :], X[:, cs, :],
                                       bd[:].unsqueeze(1).broadcast_to([P, CH, D]), ALU.add).then_inc(xb_r, 1)
            rstd_of(pool, t, own, STATS_STEPS, rst)
            pool.wait_ge(rst, 1)

        @block.tensor
        def _(e):
            e.wait_ge(ld, LOADED)

            def back(c):
                e.wait_ge(gl, START + (c + 1) * NF)
                e.wait_ge(ysum, START + c)
                for k in range(CH):
                    for n in range(NF):
                        last = e.matmul(ps[5][:, k * D:(k + 1) * D], f[:, n, k * P:(k + 1) * P], wf2[:, n, :],
                                        start=(n == 0), stop=(n == NF - 1))
                last.then_inc(f2, 1)
                e.wait_ge(ysum, START + c + 1)
                e.wait_ge(yts, START + c)
                for k in range(CH):
                    last = e.transpose(ps[6][:, k * P:(k + 1) * P], y[:, k, :], t["ident"][:])
                last.then_inc(yturned, 1)
                e.wait_ge(yts, START + c + 1)
                e.wait_ge(xs, START + c)
                for k in range(CH):
                    last = e.matmul(ps[7][:, k * D:(k + 1) * D], yT[:, k * P:(k + 1) * P], wd[:],
                                    start=True, stop=True)
                last.then_inc(d1, 1)

            with e.Fori(0, NC // 2) as c2:
                for i in range(2):
                    c = 2 * c2 + i
                    e.wait_ge(nrm, c + 1)
                    for k in range(CH):
                        last = e.transpose(ps[0][:, k * P:(k + 1) * P], h[:, i, k, :], t["ident"][:])
                    last.then_inc(turned, 1)
                    e.wait_ge(hts, c + 1)
                    for n in range(NF):
                        e.wait_ge(gl, START + c * NF + n)
                        e.matmul(ps[1 + n][:], wf1[:, n * P:(n + 1) * P], hT[:], start=True,
                                 stop=True).then_inc(f1, 1)
                    back(c)

        @block.scalar
        def _(a):
            a.wait_ge(ld, LOADED)
            with a.Fori(0, NC) as c:
                a.wait_ge(turned, START + c + 1)
                a.activation(hT[:], ps[0][:], ACT.Identity, bias=lncol[:, 1:2],
                             scale=lncol[:, 0:1]).then_inc(hts, 1)
                a.wait_ge(f2, START + c)
                for n in range(NF):
                    a.wait_ge(f1, c * NF + n + 1)
                    a.activation(f[:, n, :], ps[1 + n][:], ACT.Gelu_apprx_tanh,
                                 bias=bf1[:, n:n + 1]).then_inc(gl, 1)
                a.wait_ge(yturned, START + c + 1)
                a.activation(yT[:], ps[6][:], ACT.Copy).then_inc(yts, 1)

        @block.vector
        def _(dve):
            with dve.Fori(0, NC // 2) as c2:
                for i in range(2):
                    c = 2 * c2 + i
                    dve.wait_ge(turned, START + c)
                    normalise_chunk(dve, h[:, i, :, :], XO, mv, c).then_inc(nrm, 1)
                    dve.wait_ge(f2, START + c + 1)
                    dve.wait_ge(yb_r, c + 1)
                    dve.wait_ge(yturned, START + c)
                    dve.tensor_tensor(y[:], ps[5][:].rearrange("p (k d) -> p k d", k=CH), yb[:, i, :, :],
                                      ALU.add).then_inc(ysum, 1)
                    dve.wait_ge(d1, c + 1)
                    dve.wait_ge(xb_r, c + 1)
                    xc = X[:, bass.ds(c * CH, CH), :]
                    dve.tensor_tensor(xc, xc, ps[7][:].rearrange("p (k d) -> p k d", k=CH),
                                      ALU.add).then_inc(xs, 1)
                    dve.wait_ge(xs, START + c + 1)
                    for k in range(CH):
                        dve.bn_stats(stats[:, c * CH + k, :], X[:, c * CH + k, :]).then_inc(stat, 1)
            dve.wait_ge(stat, NT)
            finish_stats(dve, Steps(dve, own), stats, mv, tmp, NT)


def experts_of_two(nc, t, sem, ps):
    ctx = ExitStack()
    with ctx:
        def sb(name, shape, dt=F32):
            return ctx.enter_context(nc.sbuf_tensor(name, shape, dt))

        NF = F1 // P
        rw = sb("rw", [P, E1])
        wg, wu = sb("wg7", [P, E1, F1]), sb("wu7", [P, E1, F1])
        wdn = sb("wdn7", [P, E1, NF, D])
        bg, bu = sb("bg7", [P, E1, NF]), sb("bu7", [P, E1, NF])
        bdn = sb("bdn7", [E1, D])
        xf, xT = sb("xf7", [P, 2, CH, D]), sb("xf7T", [P, 2, CH * P])
        sc, rep, top = sb("sc7", [P, CH, E1]), sb("rep7", [P, CH, E1]), sb("top7", [P, CH, 8])
        prob, mx, pw = sb("prob7", [P, CH, E1]), sb("mx7", [P, CH]), sb("pw7", [P, CH, E1])
        pT = sb("pT7", [E1, CH * P])
        sil = sb("sil7", [P, 2, CH * P])
        hid = sb("hid7", [P, 2, NF, CH * P])
        acc = sb("acc7", [P, 2, CH, D])
        X, mv = t["X"], t["mv"]
        ld, nrm, turned, xts, own, ex, rt, pt, ptr, db, gu, sl, hd, dn, ac, st = (sem("p10_" + n) for n in (
            "loaded", "normed", "turned", "turned_copied", "dve_steps", "exp_done", "routed", "p_turned", "p_copied",
            "bias_done", "gate_up_done", "silu_done", "hidden_ready", "down_done", "accumulated", "stored"))
        block = ctx.enter_context(nc.Block())
        DVE_STEPS = 12 + 2 * CH
        UN = E1 * NF
        out = t["out"].rearrange("b (n k p) d -> (b n) p k d", k=CH, p=P)

        @block.sync
        def _(sp):
            for counter in (hd, turned, st):
                sp.sem_inc(counter, START)
            sp.dma_start(rw[:], t["router_wT"]).then_inc(ld, 16)
            for dst, n in ((wg, "gate_w1"), (wu, "up_w1")):
                sp.dma_start(dst[:], t[n].rearrange("e d f -> d e f")).then_inc(ld, 16)
            sp.dma_start(wdn[:].rearrange("p e n d -> p (e n) d"),
                         t["down_w1"].rearrange("e (n p) d -> p (e n) d", p=P)).then_inc(ld, 16)
            for dst, n in ((bg, "gate_b1"), (bu, "up_b1")):
                sp.dma_start(dst[:].rearrange("p e n -> p (e n)"),
                             t[n]).then_inc(ld, 16)
            sp.dma_start(bdn[:], t["down_b1"]).then_inc(ld, 16)
            with sp.Fori(0, NC // 2) as c2:
                for i in range(2):
                    c = 2 * c2 + i
                    sp.wait_ge(ac, (c + 1) * (E1 * CH + 1))
                    sp.dma_start(out[c], acc[:, i, :, :]).then_inc(st, 16)
            sp.wait_ge(st, START + 16 * NC)
        LOADED = 16 * 7

        @block.tensor
        def _(e):
            e.wait_ge(ld, LOADED)
            with e.Fori(0, NC // 2) as c2:
                for i in range(2):
                    c = 2 * c2 + i
                    e.wait_ge(nrm, c + 1)
                    for k in range(CH):
                        last = e.transpose(ps[0][:, k * P:(k + 1) * P], xf[:, i, k, :], t["ident"][:])
                    last.then_inc(turned, 1)
                    e.wait_ge(xts, c + 1)
                    for k in range(CH):
                        last = e.matmul(ps[1][:, k * E1:(k + 1) * E1], xT[:, i, k * P:(k + 1) * P], rw[:],
                                        start=True, stop=True)
                    last.then_inc(rt, 1)

                    def down(x):
                        e.wait_ge(hd, START + c * UN + (x + 1) * NF)
                        e.wait_ge(ac, c * (E1 * CH + 1) + 1 + x * CH)
                        for k in range(CH):
                            for n in range(NF):
                                last = e.matmul(ps[7][:, k * D:(k + 1) * D],
                                                hid[:, x % 2, n, k * P:(k + 1) * P], wdn[:, x, n, :],
                                                start=(n == 0), stop=(n == NF - 1))
                        last.then_inc(dn, 1)

                    for x in range(E1):
                        for n in range(NF):
                            u = x * NF + n
                            e.wait_ge(hd, START + c * UN + max(u - 1, 0))
                            e.matmul(ps[2 + 2 * (u % 2)][:], wg[:, x, n * P:(n + 1) * P], xT[:, i, :],
                                     start=True, stop=True)
                            e.matmul(ps[3 + 2 * (u % 2)][:], wu[:, x, n * P:(n + 1) * P], xT[:, i, :],
                                     start=True, stop=True).then_inc(gu, 1)
                        if x == 0:
                            e.wait_ge(own, (c + 1) * DVE_STEPS)
                            stand_alone(e)
                            for k in range(CH):
                                last = e.transpose(ps[6][0:E1, k * P:(k + 1) * P], pw[:, k, :], t["ident"][:])
                            last.then_inc(pt, 1)
                            e.wait_ge(ptr, c + 1)
                            for k in range(CH):
                                last = e.matmul(ps[7][:, k * D:(k + 1) * D], pT[:, k * P:(k + 1) * P], bdn[:],
                                                start=True, stop=True)
                            last.then_inc(db, 1)
                        if x:
                            down(x - 1)
                    down(E1 - 1)
                    e.wait_ge(ac, (c + 1) * (E1 * CH + 1))

        @block.scalar
        def _(a):
            a.wait_ge(ld, LOADED)
            with a.Fori(0, NC // 2) as c2:
                for i in range(2):
                    c = 2 * c2 + i
                    a.wait_ge(turned, START + c + 1)
                    a.activation(xT[:, i, :], ps[0][:], ACT.Copy).then_inc(xts, 1)
                    a.wait_ge(own, c * DVE_STEPS + 2)
                    a.activation(prob[:], sc[:], ACT.Exp).then_inc(ex, 1)
                    for u in range(UN):
                        a.wait_ge(gu, c * UN + u + 1)
                        a.wait_ge(hd, START + c * UN + max(u - 1, 0))
                        a.activation(sil[:, u % 2, :], ps[2 + 2 * (u % 2)][:], ACT.Silu,
                                     bias=bg[:, u // NF, u % NF:u % NF + 1]).then_inc(sl, 1)

        @block.vector
        def _(dve):
            dve.wait_ge(ld, LOADED)
            with dve.Fori(0, NC // 2) as c2:
                for i in range(2):
                    c = 2 * c2 + i
                    s = Steps(dve, own, c * DVE_STEPS, alone=True)
                    dve.wait_ge(turned, START + c)
                    normalise_chunk(dve, xf[:, i, :, :], X, mv, c).then_inc(nrm, 1)
                    dve.wait_ge(rt, c + 1)
                    lg = ps[1][:, 0:CH * E1].rearrange("p (k e) -> p k e", k=CH)
                    bc = lambda ap: ap.unsqueeze(2).broadcast_to([P, CH, E1])
                    s.do(dve.reduce_max(mx[:], lg, X_AXIS))
                    s.do(dve.tensor_tensor(sc[:], lg, bc(mx[:]), ALU.subtract))
                    dve.wait_ge(ex, c + 1)
                    s.do(dve.reduce_sum(mx[:], prob[:], X_AXIS))
                    s.do(dve.reciprocal(mx[:], mx[:]))
                    s.do(dve.tensor_tensor(prob[:], prob[:], bc(mx[:]), ALU.mult))
                    for k in range(CH):
                        s.done(dve.max(top[:, k, :], prob[:, k, :]))
                    s.settle()
                    s.do(dve.tensor_tensor(mx[:], top[:, :, 0], top[:, :, 1], ALU.add))
                    s.done(dve.tensor_scalar(mx[:], mx[:], 1e-9, None, ALU.add))
                    s.do(dve.memset(top[:, :, 2:8], 3.0e38))
                    for k in range(CH):
                        s.done(dve.match_replace(rep[:, k, :], top[:, k, :], prob[:, k, :], -3.0e38))
                    s.settle()
                    s.done(dve.tensor_tensor(rep[:], rep[:], prob[:], ALU.not_equal))
                    s.do(dve.reciprocal(mx[:], mx[:]))
                    s.do(dve.tensor_tensor(pw[:], prob[:], rep[:], ALU.mult))
                    s.do(dve.tensor_tensor(pw[:], pw[:], bc(mx[:]), ALU.mult))
                    assert s.n == DVE_STEPS, s.n
                    n_acc = c * (E1 * CH + 1)

                    def add_expert(x):
                        dve.wait_ge(dn, c * E1 + x + 1)
                        for k in range(CH):
                            dve.wait_ge(ac, n_acc + 1 + x * CH)
                            dve.scalar_tensor_tensor(out=acc[:, i, k, :], in0=ps[7][:, k * D:(k + 1) * D],
                                                     scalar=pw[:, k, x:x + 1], in1=acc[:, i, k, :],
                                                     op0=ALU.mult, op1=ALU.add).then_inc(ac, 1)

                    for x in range(E1):
                        for n in range(NF):
                            u = x * NF + n
                            dve.wait_ge(sl, c * UN + u + 1)
                            dve.scalar_tensor_tensor(out=hid[:, x % 2, n, :], in0=ps[3 + 2 * (u % 2)][:],
                                                     scalar=bu[:, x, n:n + 1], in1=sil[:, u % 2, :],
                                                     op0=ALU.add, op1=ALU.mult).then_inc(hd, 1)
                        if x == 0:
                            dve.wait_ge(pt, c + 1)
                            dve.tensor_copy(pT[:], ps[6][0:E1, :]).then_inc(ptr, 1)
                            dve.wait_ge(db, c + 1)
                            dve.wait_ge(st, START + 16 * c)
                            dve.tensor_tensor(acc[:, i, :, :], X[:, bass.ds(c * CH, CH), :],
                                              ps[7][:].rearrange("p (k d) -> p k d", k=CH),
                                              ALU.add).then_inc(ac, 1)
                        if x:
                            add_expert(x - 1)
                    add_expert(E1 - 1)
def network(nc, t):
    with ExitStack() as ctx:
        def sb(name, shape, dt=F32, c=ctx):
            return c.enter_context(nc.sbuf_tensor(name, shape, dt))

        def sem(name):
            return ctx.enter_context(nc.semaphore(name))

        psum = ctx.enter_context(nc.psum_tensor("psum", [P, 4096], F32))
        ps = [psum[:, i * 512:(i + 1) * 512] for i in range(8)]
        t["tp"] = t["bank01"] = psum[:, 0:1024]
        t["bank23"], t["bank45"], t["tp2"] = psum[:, 1024:2048], psum[:, 2048:3072], psum[:, 3072:4096]
        t["scores"] = psum[:, 0:2048].rearrange("p (a b c) -> p a b c", a=2, b=2)
        ident = sb("ident", [P, P])
        t["X"] = sb("X", [P, NT, D])
        t["mv"] = sb("mv_all", [P, 2, NT])
        t["neg_half"] = sb("neg_half", [P, NT])
        t["stat_sem"], t["keys_in"] = sem("p3_stats"), sem("p4_keys_in")
        consts = sem("constants")
        with nc.Block() as block:
            @block.sync
            def _(sp):
                sp.dma_start(ident[:], t["ident"]).then_inc(consts, 16)
                sp.wait_ge(consts, 16)

            @block.gpsimd
            def _(pool):
                pool.memset(t["neg_half"][:], -0.5)
        t["ident"] = ident
        with ExitStack() as c:
            t["att"] = sb("att", [P, NT, D], F32, c)
            with ExitStack() as c2:
                t["qkv"] = sb("qkv", [P, NT, 3 * D], F32, c2)
                t["gco"] = sb("gco", [P, NT, 2, H0], F32, c2)
                project_batches(nc, t, sem, ps)
                attend(nc, t, sem, ps)
            output_projection(nc, t, sem, ps)
        with ExitStack() as c:
            for n, dt in (("slotv", F32), ("tok", F32), ("full", F32), ("gidx", I32)):
                t[n] = sb(n, [P, E0 // 2], dt, c)
            with ExitStack() as c2:
                t["keys"] = sb("keys", [E0, N_TOK], F32, c2)
                gate_and_shared(nc, t, sem, ps)
                pick_slots(nc, t, sem, ps)
            routed_experts(nc, t, sem, ps)
        t["XO"] = sb("XO", [P, NT, D])
        combine(nc, t, sem, ps)
        linear_attention(nc, t, sem, ps)
        feed_forward(nc, t, sem, ps)
        experts_of_two(nc, t, sem, ps)


def constants(np):
    u = np.arange(S, dtype=np.float64) - S // 2
    u2_low = np.mod(u * u, 128)
    one = np.ones(S)
    krows = np.stack([u * u - u2_low, u2_low, u * u - u2_low, u2_low, u, u, -one, -one], -1)
    part = np.arange(P)
    return {
        "ident": np.eye(P, dtype=np.float32),
        "kconst": np.ascontiguousarray(krows.reshape(TB, P, 8).transpose(1, 0, 2).astype(np.float32)),
        "hmask": (part[:, None] // DH0 == np.arange(H0)[None]).astype(np.float32),
        "block32": (part[:, None] // DH1 == part[None] // DH1).astype(np.float32),
        "tokv": (N_TOK - P * np.arange(NT)[None] - part[:, None]).astype(np.float32),
    }


def kernel(**inputs):
    import numpy as np
    import concourse.bacc as bacc
    from concourse.bass_utils import run_bass_kernel_spmd

    a = {k: np.asarray(v) for k, v in inputs.items()}
    l0, f0, l1, f1 = ({k[len(p):]: v for k, v in a.items() if k.startswith(p)}
                      for p in ("L0_attn_", "L0_ffn_", "L1_attn_", "L1_ffn_"))
    arrays = constants(np)
    arrays["x"] = l0["hidden_states"]
    for n in ("wq", "wk", "wv", "wo", "wfq", "wfg", "bq", "bk", "bv", "bo", "bfq", "bfg", "up", "uz"):
        arrays[n] = l0[n]
    arrays["gate_wT"], arrays["gate_b0"] = f0["gate_w"].T, f0["gate_b"]
    arrays["ws1T"], arrays["ws3T"] = f0["ws1"].T, f0["ws3"].T
    arrays["ws2T"] = f0["ws2"].T.reshape(2, I0, D).transpose(1, 0, 2)
    arrays["w1T"] = f0["w1"].transpose(2, 0, 1).reshape(D, E0 * I0)
    arrays["w3T"] = f0["w3"].transpose(2, 0, 1).reshape(D, E0 * I0)
    arrays["w2T"] = f0["w2"].transpose(2, 0, 1).reshape(I0, E0 * D)
    for n in ("wq", "wk", "wv", "wo", "bo"):
        arrays["l1_" + n] = l1[n]
    for n in ("ln1_g", "ln1_b", "ln2_g", "ln2_b", "w_ff1", "b_ff1", "w_ff2", "b_ff2", "w_d", "b_d"):
        arrays[n] = l1[n]
    arrays["router_wT"] = f1["router_w"].T
    arrays["b_ff1"] = l1["b_ff1"].reshape(FF // P, P).T
    for n in ("gate_w", "up_w", "down_w", "down_b"):
        arrays[n + "1"] = f1[n]
    for n in ("gate_b", "up_b"):
        arrays[n + "1"] = f1[n].reshape(E1 * F1 // P, P).T

    nc = bacc.Bacc("TRN2", target_bir_lowering=False, num_devices=1)
    arrays = {f"in_{n}": np.ascontiguousarray(v) for n, v in arrays.items()}
    t = {n[3:]: nc.dram_tensor(n, v.shape, F32, kind="ExternalInput").ap() for n, v in arrays.items()}
    t["out"] = nc.dram_tensor("out", (B, S, D), F32, kind="ExternalOutput").ap()
    t["rows"] = nc.dram_tensor("token_rows", (N_TOK, ROW), F32, kind="Internal").ap()
    t["ybuf"] = nc.dram_tensor("pick_rows", (N_TOK * K0, D), F32, kind="Internal").ap()
    network(nc, t)
    r = run_bass_kernel_spmd(nc, [arrays], core_ids=[0])
    return r.results[0]["out"]
```

```python
from contextlib import ExitStack

import concourse.bass as bass
from concourse import mybir

F32 = mybir.dt.float32
F32R = mybir.dt.float32r
BF16 = mybir.dt.bfloat16
I32 = mybir.dt.int32
U32 = mybir.dt.uint32
ALU = mybir.AluOpType
ACT = mybir.ActivationFunctionType
X_AXIS = mybir.AxisListType.X

P = 128
D = 128
B, S = 4, 1024
NT = B * S // P
TB = S // P
H0, DH0 = 16, 8
GH = 4
NG = H0 // GH
R = 32
EPS = 1e-5
START = 1


def stand_alone(eng):
    eng.nop(nofuse=True)


class Steps:

    def __init__(self, eng, sem, base=0, alone=False):
        self.eng, self.sem, self.base, self.alone, self.n = eng, sem, base, alone, 0

    def done(self, ins):
        ins.then_inc(self.sem, 1)
        self.n += 1

    def settle(self):
        self.eng.wait_ge(self.sem, self.base + self.n)
        if self.alone:
            stand_alone(self.eng)

    def do(self, ins):
        self.done(ins)
        self.settle()
def project_batches(nc, t, sem, ps):
    ctx = ExitStack()
    with ctx:
        def sb(name, shape, dt=F32):
            return ctx.enter_context(nc.sbuf_tensor(name, shape, dt))

        wqkv = sb("wqkv", [P, 3 * D])
        wfq, wfg = sb("wfq", [P, D]), sb("wfg", [P, D])
        cols = sb("cols", [P, 5])
        biases = sb("biases", [P, 3 * D])
        hmask = sb("hmask", [P, H0])
        upz = sb("upz", [P, 2, H0])
        stats = sb("stats", [P, TB, 6])
        mv = sb("mv", [P, TB, 2])
        rstd = sb("rstd", [P, TB])
        half = sb("half", [P, TB])
        xn = sb("xn", [P, TB, D])
        xT = sb("xT", [P, S])
        qT = sb("qT", [P, S])
        cT = sb("cT", [P, S])
        glo = sb("glo", [P, 2])
        cbias = sb("cbias", [P, 3])
        ez = sb("ez", [P, TB, 2, H0])
        g1 = sb("g1", [P, TB, 2, H0])
        g2 = sb("g2", [P, TB, H0])
        g3 = sb("g3", [P, TB, H0])
        X, qkv, gco = t["X"], t["qkv"], t["gco"]

        loaded, own, rst, trd, act, pe = (sem(n) for n in (
            "p1_loaded", "p1_dve_steps", "p1_rstd_ready", "p1_xn_ready", "p1_act_steps", "p1_pe_steps"))
        tok, evac = sem("p1_qkv_ready"), sem("p1_qkv_taken")
        halfs = sem("p1_half_ready")
        block = ctx.enter_context(nc.Block())

        @block.sync
        def _(sp):
            for b in range(B):
                sp.dma_start(X[:, b * TB:(b + 1) * TB, :],
                             t["x"][b].rearrange("(t p) d -> p t d", p=P)).then_inc(loaded, 16)
            for i, n in enumerate(("wq", "wk", "wv")):
                sp.dma_start(wqkv[:, i * D:(i + 1) * D], t[n]).then_inc(loaded, 16)
            sp.dma_start(wfq[:], t["wfq"]).then_inc(loaded, 16)
            sp.dma_start(wfg[:], t["wfg"]).then_inc(loaded, 16)
            sp.dma_start(hmask[:], t["hmask"]).then_inc(loaded, 16)
            for i, n in enumerate(("bq", "bk", "bv")):
                sp.dma_start(biases[:, i * D:(i + 1) * D],
                             t[n].partition_broadcast(P)).then_inc(loaded, 16)
            for i, n in enumerate(("bq", "bfq", "bfg", "up", "uz")):
                v = t[n] if n[0] == "b" else t[n].rearrange("h a d -> (h a d)")
                sp.dma_start(cols[:, i:i + 1], v.rearrange("(p a) -> p a", a=1)).then_inc(loaded, 16)
        N_LOADED = 16 * (B + 3 + 3 + 3 + 5)

        DVE_STEPS = TB + 11
        ACT_STEPS = 2 + 1 + 2 + 1
        PE_STEPS = 5

        @block.gpsimd
        def _(pool):
            pool.memset(half[:], -0.5).then_inc(halfs, 1)
            pool.wait_ge(halfs, 1)
            with pool.Fori(0, B) as b:
                pool.wait_ge(own, 3 + b * DVE_STEPS + TB + 2)
                pool.tensor_tensor(rstd[:], rstd[:], half[:], ALU.pow).then_inc(rst, 1)

        @block.vector
        def _(dve):
            dve.wait_ge(loaded, N_LOADED)
            s0 = Steps(dve, own)
            for i in range(2):
                s0.done(dve.tensor_scalar(upz[:, i, :], hmask[:], cols[:, 3 + i:4 + i], None, ALU.mult))
            s0.do(dve.tensor_tensor(cbias[:, 0:1], cols[:, 1:2], cols[:, 2:3], ALU.add))
            with dve.Fori(0, B) as b:
                s = Steps(dve, own, 3 + b * DVE_STEPS, alone=True)
                for i in range(TB):
                    s.done(dve.bn_stats(stats[:, i, :], X[:, b * TB + i, :]))
                s.settle()
                for i in range(TB):
                    last = dve.bn_aggr(mv[:, i, :], stats[:, i, :])
                s.do(last)
                s.do(dve.tensor_scalar(rstd[:], mv[:, :, 1], EPS, None, ALU.add))
                dve.wait_ge(rst, b + 1)
                for i in range(TB):
                    last = dve.tensor_scalar(xn[:, i, :], X[:, b * TB + i, :], mv[:, i, 0:1],
                                             rstd[:, i:i + 1], ALU.subtract, ALU.mult)
                last.then_inc(trd, 1)
                dve.wait_ge(act, b * ACT_STEPS + 3)
                s.do(dve.reduce_sum(glo[:, 0:1], qT[:], X_AXIS))
                s.do(dve.tensor_scalar(glo[:, 1:2], glo[:, 0:1], 1.0 / S, None, ALU.mult))
                for i in range(TB):
                    dve.wait_ge(tok, b * TB + i + 1)
                    dve.tensor_tensor(qkv[:, b * TB + i, :], ps[4 + i % 2][:, 0:3 * D], biases[:],
                                      ALU.add).then_inc(evac, 1)
                dve.wait_ge(pe, b * PE_STEPS + 3)
                s.do(dve.tensor_tensor(cbias[:, 1:2], ps[6][:, 0:1], cbias[:, 0:1], ALU.add))
                dve.wait_ge(act, b * ACT_STEPS + 6)
                s.do(dve.tensor_scalar(g1[:], ez[:], 1.0, None, ALU.add))
                s.do(dve.reciprocal(g2[:], g1[:, :, 0, :]))
                s.do(dve.tensor_scalar(g2[:], g2[:], float(S), -float(S // 2), ALU.mult, ALU.add))
                s.do(dve.tensor_tensor(g3[:], g1[:, :, 1, :], g1[:, :, 1, :], ALU.mult))
                s.done(dve.tensor_scalar(gco[:, bass.ds(b * TB, TB), 0, :], g3[:], -2.0 / S ** 2, None,
                                         ALU.mult))
                s.do(dve.scalar_tensor_tensor(out=gco[:, bass.ds(b * TB, TB), 1, :], in0=g3[:],
                                              scalar=4.0 / S ** 2, in1=g2[:], op0=ALU.mult, op1=ALU.mult))
                assert s.n == DVE_STEPS, s.n

        @block.scalar
        def _(a):
            a.wait_ge(loaded, N_LOADED)
            with a.Fori(0, B) as b:
                s = Steps(a, act, b * ACT_STEPS)
                a.wait_ge(pe, b * PE_STEPS + 1)
                s.do(a.activation(xT[:], t["tp"][:], ACT.Copy))
                for c in range(2):
                    a.wait_ge(pe, b * PE_STEPS + 2)
                    s.done(a.activation(qT[:, c * 512:(c + 1) * 512], ps[2 + c][:], ACT.Identity,
                                        bias=cols[:, 0:1]))
                a.wait_ge(pe, b * PE_STEPS + 4)
                a.wait_ge(own, 3 + b * DVE_STEPS + TB + 5)
                for c in range(2):
                    s.done(a.activation(cT[:, c * 512:(c + 1) * 512], ps[2 + c][:], ACT.Tanh,
                                        bias=cbias[:, 1:2]))
                a.wait_ge(pe, b * PE_STEPS + 5)
                s.done(a.activation(ez[:].rearrange("p t a h -> p (t a h)"), ps[7][:, 0:2 * H0 * TB],
                                    ACT.Exp, scale=-1.0))
                assert s.n == ACT_STEPS

        @block.tensor
        def _(e):
            e.wait_ge(loaded, N_LOADED)
            with e.Fori(0, B) as b:
                e.wait_ge(trd, b + 1)
                for i in range(TB):
                    last = e.transpose(t["tp"][:, i * P:(i + 1) * P], xn[:, i, :], t["ident"][:])
                last.then_inc(pe, 1)
                e.wait_ge(act, b * ACT_STEPS + 1)
                for c in range(2):
                    last = e.matmul(ps[2 + c][:], wqkv[:, 0:D], xT[:, c * 512:(c + 1) * 512],
                                    start=True, stop=True)
                last.then_inc(pe, 1)
                for i in range(TB):
                    if i >= 2:
                        e.wait_ge(evac, b * TB + i - 1)
                    e.matmul(ps[4 + i % 2][:, 0:3 * D], xT[:, i * P:(i + 1) * P], wqkv[:],
                             start=True, stop=True).then_inc(tok, 1)
                e.wait_ge(own, 3 + b * DVE_STEPS + TB + 4)
                e.matmul(ps[6][:, 0:1], wfg[:], glo[:, 1:2], start=True, stop=True).then_inc(pe, 1)
                for c in range(2):
                    last = e.matmul(ps[2 + c][:], wfq[:], qT[:, c * 512:(c + 1) * 512],
                                    start=True, stop=True)
                last.then_inc(pe, 1)
                e.wait_ge(act, b * ACT_STEPS + 5)
                for i in range(TB):
                    last = e.matmul(ps[7][:, i * 2 * H0:(i + 1) * 2 * H0], cT[:, i * P:(i + 1) * P],
                                    upz[:].rearrange("p a h -> p (a h)"), start=True, stop=True)
                last.then_inc(pe, 1)
                e.wait_ge(act, b * ACT_STEPS + 6)
                e.wait_ge(evac, b * TB + TB)


def attend(nc, t, sem, ps):
    ctx = ExitStack()
    with ctx:
        def sb(name, shape, dt=F32):
            return ctx.enter_context(nc.sbuf_tensor(name, shape, dt))

        STEPS = 16
        BS = NG * STEPS
        QH = S // 2
        SCALE = DH0 ** -0.5
        INIT = 4 + 2 * NG
        NB = 3
        qrow = sb("qrow", [P, TB, GH, R], F32R)
        krow = sb("krow", [P, TB, GH, R], F32R)
        vaug = [sb(f"vaug{i}", [P, TB, GH, R]) for i in range(NG)]
        qT = [sb(f"aqT{i}", [P, S], F32R) for i in range(NG)]
        kT = [sb(f"akT{i}", [P, GH, S], F32R) for i in range(NG)]
        probs = sb("probs", [P, 4, 2, QH])
        mx, rowmax = sb("mx", [P, TB, GH, 2]), sb("rowmax", [P, TB, GH])
        mrow = sb("mrow", [P, TB, GH, R], F32R)
        scaled = sb("scaled", [P, TB, R])
        kconst = sb("kconst", [P, TB, 8])
        ctxT = [sb(f"ctxT{i}", [P, QH]) for i in range(2)]
        zeros = sb("zeros", [P, 512])
        qscale = sb("qscale", [P, TB])
        rden = sb("rden", [P, 2, 4, GH])
        qkv, gco, att = t["qkv"], t["gco"], t["att"]
        scores, ctxp, tp = t["scores"], ps[4], [ps[5], ps[6], ps[7]]
        f32 = lambda ap: ap.bitcast(F32)

        (ld, pool_own, s_ready, p_ready, pv_done, half_copied,
         tp_full, tp_free, qk_copied, dve_own, dve_c, init, zeroed) = (sem("p2_" + n) for n in (
             "loaded", "pool_steps", "scores_ready", "probs_ready", "pv_done", "half_copied",
             "tp_full", "tp_free", "operands_copied", "dve_steps", "den_ready", "init_done", "rows_zeroed"))
        block = ctx.enter_context(nc.Block())

        def halves(at, kind, u):
            return [(at, kind, u, c) for c in range(2)]

        def maxima(at, u):
            return [(at + (2 * j + c) * 0.225, "X", u, (j // TB, j % TB, c))
                    for j in range(GH * TB) for c in range(2)]\
                + halves(at + 14.8, "M", u)

        FIRST = sorted(halves(0, "Q", 0) + halves(0, "K", 0) + maxima(0.1, 0) + halves(5.2, "Q", 1)
                       + halves(7.4, "K", 1), key=lambda x: x[0])

        def batch_events(last):
            out = []
            for g in range(NG):
                k = g * STEPS
                if not (last and g + 1 == NG):
                    out += maxima(k + 0.1, g + 1)
                if not (last and g + 2 >= NG):
                    out += halves(k + 5.2, "Q", g + 2) + halves(k + 7.4, "K", g + 2)
                if g:
                    out.append((k + 3.3, "C", 2 * g - 1, None))
                out.append((k + 11.3, "C", 2 * g, None))
            return sorted(out, key=lambda x: x[0]) + [(BS + 1, "C", 2 * NG - 1, None)]

        by_dve = lambda events: sum(x[1] not in "QK" for x in events)
        NF, NE = len(FIRST), len(batch_events(False))
        NFD, NED = by_dve(FIRST), by_dve(batch_events(False))
        assert NE % NB == 0

        class Events:

            def __init__(self, events, b=None):
                self.events, self.follows = events, b is not None
                self.base = 0 if b is None else NF + b * NE
                self.dve_base = 0 if b is None else NFD + b * NED

            def passed(self, n):
                return self.base + n

            def bank(self, n):
                return tp[(n + (NF if self.follows else 0)) % NB]

            def emptied(self, n):
                return START + self.dve_base + by_dve(self.events[:n])

        @block.sync
        def _(sp):
            for counter in (tp_full, pv_done, tp_free, p_ready, half_copied, qk_copied):
                sp.sem_inc(counter, START)
            sp.dma_start(kconst[:], t["kconst"]).then_inc(ld, 16)
            sp.wait_ge(init, INIT)
            rows = t["ybuf"].rearrange("(p n) d -> p (n d)", p=P)
            n = rows.shape[1] // zeros.shape[1]
            for i in range(n):
                sp.dma_start(rows[:, bass.ts(i, zeros.shape[1])], zeros[:]).then_inc(zeroed, 16)
            sp.wait_ge(zeroed, 16 * n)

        POOL_STEPS = 14
        M_STEPS = 3
        POOL_FIRST = GH + NG

        @block.gpsimd
        def _(pool):
            for v in vaug:
                pool.memset(v[:], 0.0).then_inc(init, 1)
            pool.memset(f32(qrow[:]), 0.0)
            pool.memset(f32(mrow[:]), 0.0).then_inc(init, 1)
            pool.memset(zeros[:], 0.0).then_inc(init, 1)
            pool.memset(qscale[:], SCALE).then_inc(init, 1)
            pool.memset(mx[:], 0.0).then_inc(init, 1)
            pool.wait_ge(ld, 16)
            pool.wait_ge(init, INIT)
            s = Steps(pool, pool_own)
            for h in range(GH):
                s.done(pool.tensor_copy(krow[:, :, h, 24:32], kconst[:]))
            for v in vaug:
                s.done(pool.memset(v[:, :, :, DH0:DH0 + 1], 1.0))
            s.settle()
            assert s.n == POOL_FIRST

            def build(b, u):
                g = u % NG
                unit = b * NG + u
                s = Steps(pool, pool_own, POOL_FIRST + unit * POOL_STEPS, alone=True)
                tiles = bass.ds((b + u // NG) * TB, TB)
                part = lambda w: qkv[:, tiles, w * D + g * R:w * D + (g + 1) * R]\
                    .rearrange("p t (h d) -> p t h d", h=GH)
                co = lambda w: gco[:, tiles, w, g * GH:(g + 1) * GH]
                tmp = scaled[:].rearrange("p t (h d) -> p t h d", h=GH)
                s.settle()
                if u == 1:
                    pool.wait_ge(qk_copied, START + 4)
                if u >= 2:
                    pool.wait_ge(dve_own, M_STEPS * (unit - 1))
                    pool.wait_ge(pv_done, START + (b * NG + max(u - NG + 1, 0)) * STEPS)
                    stand_alone(pool)
                q, k, v = qrow, krow, vaug[g]
                s.done(pool.tensor_tensor(scaled[:], qkv[:, tiles, g * R:(g + 1) * R],
                                          qscale[:].unsqueeze(2).broadcast_to([P, TB, R]), ALU.mult))
                s.done(pool.tensor_copy(k[:, :, :, 0:8], part(1)))
                s.done(pool.tensor_copy(q[:, :, :, 24], co(0)))
                s.done(pool.tensor_copy(q[:, :, :, 28], co(1)))
                s.done(pool.tensor_copy(v[:, :, :, 0:DH0], part(2)))
                s.settle()
                s.done(pool.tensor_copy(q[:, :, :, 0:8], tmp))
                s.done(pool.tensor_copy(k[:, :, :, 16:24], f32(k[:, :, :, 0:8])))
                s.done(pool.tensor_tensor(k[:, :, :, 8:16], part(1), f32(k[:, :, :, 0:8]), ALU.subtract))
                s.done(pool.tensor_copy(q[:, :, :, 25], f32(q[:, :, :, 24])))
                s.done(pool.tensor_tensor(q[:, :, :, 26], co(0), f32(q[:, :, :, 24]), ALU.subtract))
                s.settle()
                s.done(pool.tensor_copy(q[:, :, :, 27], f32(q[:, :, :, 26])))
                s.done(pool.tensor_tensor(q[:, :, :, 29], co(1), f32(q[:, :, :, 28]), ALU.subtract))
                s.done(pool.tensor_copy(q[:, :, :, 8:16], f32(q[:, :, :, 0:8])))
                s.done(pool.tensor_tensor(q[:, :, :, 16:24], tmp, f32(q[:, :, :, 0:8]), ALU.subtract))
                assert s.n == POOL_STEPS, s.n

            for u in range(2):
                build(0, u)
            with pool.Fori(0, B - 1) as b:
                for u in range(2, NG + 2):
                    build(b, u)
            for u in range(2, NG):
                build(B - 1, u)

        @block.tensor
        def _(e):
            def turned(b, kind, u, c):
                return START + (b * NG + u) * 4 + (2 if kind == "K" else 0) + c + 1

            def event(b, ev, n):
                _, kind, u, at = ev.events[n]
                bank = ev.bank(n)
                if n < NB:
                    if ev.follows:
                        e.wait_ge(tp_free, ev.emptied(0))
                        e.wait_ge(qk_copied, START + (b * NG + 2) * 4)
                elif ev.events[n - NB][1] in "QK":
                    e.wait_ge(qk_copied, turned(b, *ev.events[n - NB][1:]))
                else:
                    e.wait_ge(tp_free, ev.emptied(n - NB + 1))
                if kind == "C":
                    e.wait_ge(half_copied, START + b * 2 * NG + u + 1)
                    for i in range(4):
                        last = e.transpose(bank[:, i * P:(i + 1) * P], ctxT[u % 2][:, i * P:(i + 1) * P],
                                           t["ident"][:])
                elif kind == "X":
                    h, i, c = at
                    if (h, i, c) == (0, 0, 0):
                        e.wait_ge(qk_copied, START + (b * NG + u + 1) * 4)
                    last = e.matmul(bank[:], qT[u % NG][:, i * P:(i + 1) * P],
                                    kT[u % NG][:, h, c * 512:(c + 1) * 512], start=True, stop=True)
                else:
                    if kind == "M":
                        e.wait_ge(dve_own, (b * NG + u + 1) * M_STEPS)
                    else:
                        e.wait_ge(pool_own, POOL_FIRST + (b * NG + u + 1) * POOL_STEPS)
                    src = {"Q": qrow, "K": krow, "M": mrow}[kind]
                    for i in range(4):
                        last = e.transpose(bank[:, i * P:(i + 1) * P],
                                           f32(src[:, 4 * at + i, :, :]).rearrange("p h r -> p (h r)"),
                                           t["ident"][:])
                last.then_inc(tp_full, 1)

            def score_step(b, n):
                g, hf, kt, pair = n // 32, n // 16 % 2, n // 2 % 8, n % 2
                if n:
                    e.wait_ge(p_ready, START + b * 2 * BS + max(n - 1, 0))
                for j in range(2):
                    h = 2 * pair + j
                    last = e.matmul(scores[:, n % 2, j, :],
                                    kT[g][:, h, kt * P:(kt + 1) * P], qT[g][:, hf * QH:(hf + 1) * QH],
                                    start=True, stop=True)
                last.then_inc(s_ready, 1)

            def values_step(b, k):
                g, hf, kt = k // STEPS, k // 8 % 2, k % 8
                e.wait_ge(p_ready, START + b * 2 * BS + 2 * k + 2)
                if kt == 0:
                    e.wait_ge(half_copied, START + b * 2 * NG + 2 * g + hf)
                for h in range(GH):
                    last = e.matmul(ctxp[h * R:(h + 1) * R, :], vaug[g][:, kt, h, :],
                                    probs[:, (2 * k + h // 2) % 4, h % 2, :],
                                    start=(kt == 0), stop=(kt == 7))
                last.then_inc(pv_done, 1)

            def batch(b, last):
                ev = Events(batch_events(last), b)
                seen = [0]

                def events_to(place):
                    while seen[0] < len(ev.events) and ev.events[seen[0]][0] < place:
                        event(b, ev, seen[0])
                        seen[0] += 1

                for k in range(BS + 1):
                    if k < BS:
                        if k % STEPS == 0:
                            m = [x[1:3] for x in ev.events].index(("M", k // STEPS)) + 2 if k else 0
                            e.wait_ge(tp_free, ev.emptied(m))
                        score_step(b, 2 * k)
                        events_to(k + 0.3)
                        score_step(b, 2 * k + 1)
                    events_to(k + 0.6)
                    if k:
                        values_step(b, k - 1)
                    events_to(k + 1)
                events_to(BS + 2)

            first = Events(FIRST)
            for n in range(NF):
                event(0, first, n)
            with e.Fori(0, B - 1) as b:
                batch(b, False)
            batch(B - 1, True)

        @block.scalar
        def _(a):
            def operands(b, ev, n):
                _, kind, u, c = ev.events[n]
                bank, half = ev.bank(n), slice(c * 512, (c + 1) * 512)
                a.wait_ge(tp_full, START + ev.passed(n) + 1)
                if kind == "Q":
                    last = a.activation(qT[u % NG][:, half], bank[:], ACT.Copy)
                else:
                    for h in range(GH):
                        r = slice(h * R, (h + 1) * R)
                        last = a.activation(kT[u % NG][r, h, half], bank[r, :], ACT.Copy)
                last.then_inc(qk_copied, 1)

            def context(b, u):
                a.wait_ge(pv_done, START + b * BS + 8 * (u + 1))
                a.activation(ctxT[u % 2][:], ctxp[:], ACT.Copy).then_inc(half_copied, 1)

            def batch(b, last):
                ev = Events(batch_events(last), b)
                turns = [n for n, x in enumerate(ev.events) if x[1] in "QK"]
                for n in range(2 * BS):
                    a.wait_ge(s_ready, b * 2 * BS + n + 1)
                    if n % 2 == 0:
                        a.wait_ge(pv_done, START + b * BS + max(n // 2 - 1, 0))
                    a.activation(probs[:, n % 4, :, :], scores[:, n % 2, :, :], ACT.Exp)\
                        .then_inc(p_ready, 1)
                    while turns and n % 2 and ev.events[turns[0]][0] < n // 2 + 1:
                        operands(b, ev, turns.pop(0))
                    if n % 2 and n // 2 % 8 == 0 and n > 1:
                        context(b, n // 16 - 1)
                context(b, 2 * NG - 1)

            a.wait_ge(init, INIT)
            first = Events(FIRST)
            for n, x in enumerate(FIRST):
                if x[1] in "QK":
                    operands(0, first, n)
            with a.Fori(0, B - 1) as b:
                batch(b, False)
            batch(B - 1, True)

        @block.vector
        def _(dve):
            for k in kT:
                dve.memset(f32(k[:]), 0.0).then_inc(init, 1)
            dve.wait_ge(init, INIT)

            def event(b, ev, n):
                _, kind, u, at = ev.events[n]
                bank = ev.bank(n)
                if kind in "QK":
                    return
                if kind == "M":
                    if at == 0:
                        dve.wait_ge(tp_free, ev.emptied(n))
                        s = Steps(dve, dve_own, (b * NG + u) * M_STEPS)
                        s.do(dve.tensor_tensor(rowmax[:], mx[:, :, :, 0], mx[:, :, :, 1], ALU.max))
                        s.do(dve.tensor_copy(mrow[:, :, :, 30], rowmax[:]))
                        s.do(dve.tensor_tensor(mrow[:, :, :, 31], rowmax[:], f32(mrow[:, :, :, 30]),
                                               ALU.subtract))
                        assert s.n == M_STEPS
                dve.wait_ge(tp_full, START + ev.passed(n) + 1)
                if kind == "C":
                    v = bank[:].rearrange("p (i h r) -> p i h r", i=4, h=GH)
                    dve.reciprocal(rden[:, u % 2], v[:, :, :, DH0]).then_inc(dve_c, 1)
                    dve.wait_ge(dve_c, b * 2 * NG + u + 1)
                    g, hf = u // 2, u % 2
                    o = att[:, bass.ds(b * TB + 4 * hf, 4), g * R:(g + 1) * R]\
                        .rearrange("p i (h d) -> p i h d", h=GH)
                    dve.tensor_tensor(o, v[:, :, :, 0:DH0],
                                      rden[:, u % 2].unsqueeze(3).broadcast_to([P, 4, GH, DH0]),
                                      ALU.mult).then_inc(tp_free, 1)
                elif kind == "X":
                    h, i, c = at
                    dve.reduce_max(mx[:, i, h, c:c + 1], bank[:], X_AXIS).then_inc(tp_free, 1)
                else:
                    q = qT[u % NG][:, at * 512:(at + 1) * 512]
                    dve.tensor_tensor(q, f32(q), bank[:], ALU.add).then_inc(tp_free, 1)

            def batch(b, last):
                ev = Events(batch_events(last), b)
                for n in range(len(ev.events)):
                    event(b, ev, n)

            first = Events(FIRST)
            for n in range(NF):
                event(0, first, n)
            with dve.Fori(0, B - 1) as b:
                batch(b, False)
            batch(B - 1, True)
CH = 4
NC = NT // CH
E0, K0, CAP, I0 = 64, 6, 64, 88
SI = 2 * I0
ROW = 2 * D
N_TOK = B * S


def finish_stats(dve, s, stats, mv, tmp, n):
    s.done(dve.tensor_tensor(mv[:, 0, :], stats[:, :, 1], stats[:, :, 4], ALU.add))
    s.done(dve.tensor_tensor(tmp[:, 0, :], stats[:, :, 1], stats[:, :, 4], ALU.subtract))
    s.do(dve.tensor_tensor(tmp[:, 1, :], stats[:, :, 2], stats[:, :, 5], ALU.add))
    s.done(dve.tensor_scalar(mv[:, 0, :], mv[:, 0, :], 0.5, None, ALU.mult))
    s.done(dve.tensor_scalar(tmp[:, 1, :], tmp[:, 1, :], 1.0 / D, EPS, ALU.mult, ALU.add))
    s.do(dve.scalar_tensor_tensor(out=tmp[:, 0, :], in0=tmp[:, 0, :], scalar=0.25, in1=tmp[:, 0, :],
                                  op0=ALU.mult, op1=ALU.mult))
    s.do(dve.tensor_tensor(mv[:, 1, :], tmp[:, 0, :], tmp[:, 1, :], ALU.add))


STATS_STEPS = 7


def output_projection(nc, t, sem, ps):
    ctx = ExitStack()
    with ctx:
        def sb(name, shape, dt=F32):
            return ctx.enter_context(nc.sbuf_tensor(name, shape, dt))

        wo, bo = sb("wo0", [P, D]), sb("bo0", [P, D])
        ctile = sb("ctile", [P, 2, CH, D])
        cT = sb("ctxTt", [P, 2, CH * P])
        stats, tmp = sb("stats3", [P, NT, 6]), sb("tmp3", [P, 2, NT])
        X, att, mv = t["X"], t["att"], t["mv"]
        loaded, biased, taken, turned, turned_sb, proj, added, own, varr = (sem("p3_" + n) for n in (
            "loaded", "x_biased", "ctx_taken", "turned", "turned_copied", "projected", "added",
            "dve_steps", "var_ready"))
        block = ctx.enter_context(nc.Block())

        @block.sync
        def _(sp):
            for counter in (turned, added):
                sp.sem_inc(counter, START)
            sp.dma_start(wo[:], t["wo"]).then_inc(loaded, 16)
            sp.dma_start(bo[:], t["bo"].partition_broadcast(P)).then_inc(loaded, 16)

        @block.gpsimd
        def _(pool):
            pool.wait_ge(loaded, 32)
            with pool.Fori(0, NC) as c:
                pool.tensor_tensor(X[:, bass.ds(c * CH, CH), :], X[:, bass.ds(c * CH, CH), :],
                                   bo[:].unsqueeze(1).broadcast_to([P, CH, D]), ALU.add).then_inc(biased, 1)
            pool.wait_ge(own, STATS_STEPS)
            pool.tensor_tensor(mv[:, 1, :], mv[:, 1, :], t["neg_half"][:, 0:NT], ALU.pow).then_inc(varr, 1)
            pool.wait_ge(varr, 1)

        @block.scalar
        def _(a):
            with a.Fori(0, NC // 2) as c2:
                for i in range(2):
                    c = 2 * c2 + i
                    a.wait_ge(turned, START + c)
                    a.activation(ctile[:, i, :, :], att[:, bass.ds(c * CH, CH), :], ACT.Copy).then_inc(taken, 1)
                    a.wait_ge(turned, START + c + 1)
                    a.activation(cT[:, i, :], ps[i][:], ACT.Copy).then_inc(turned_sb, 1)

        @block.tensor
        def _(e):
            e.wait_ge(loaded, 32)
            with e.Fori(0, NC // 2) as c2:
                for i in range(2):
                    c = 2 * c2 + i
                    e.wait_ge(taken, c + 1)
                    for k in range(CH):
                        last = e.transpose(ps[i][:, k * P:(k + 1) * P], ctile[:, i, k, :], t["ident"][:])
                    last.then_inc(turned, 1)
                    e.wait_ge(turned_sb, c + 1)
                    e.wait_ge(added, START + c)
                    for k in range(CH):
                        last = e.matmul(ps[2 + i][:, k * D:(k + 1) * D], cT[:, i, k * P:(k + 1) * P], wo[:],
                                        start=True, stop=True)
                    last.then_inc(proj, 1)

        @block.vector
        def _(dve):
            with dve.Fori(0, NC // 2) as c2:
                for i in range(2):
                    c = 2 * c2 + i
                    dve.wait_ge(proj, c + 1)
                    dve.wait_ge(biased, c + 1)
                    xc = X[:, bass.ds(c * CH, CH), :]
                    dve.tensor_tensor(xc, xc, ps[2 + i][:].rearrange("p (k d) -> p k d", k=CH),
                                      ALU.add).then_inc(added, 1)
                    dve.wait_ge(added, START + c + 1)
                    for k in range(CH):
                        dve.bn_stats(stats[:, c * CH + k, :], X[:, c * CH + k, :]).then_inc(t["stat_sem"], 1)
            dve.wait_ge(t["stat_sem"], NT)
            finish_stats(dve, Steps(dve, own), stats, mv, tmp, NT)


def gate_and_shared(nc, t, sem, ps):
    ctx = ExitStack()
    with ctx:
        def sb(name, shape, dt=F32):
            return ctx.enter_context(nc.sbuf_tensor(name, shape, dt))

        gw, gb = sb("gw", [P, E0]), sb("gb", [P, E0])
        ws1, ws3 = sb("ws1", [P, SI]), sb("ws3", [P, SI])
        ws2 = sb("ws2", [I0, 2, D])
        tokv = sb("tokv", [P, NT])
        xrow = sb("xrow", [P, 2, CH, ROW])
        xnT = sb("xnT", [P, 2, CH * P])
        mx, den = sb("gmx", [P, 2, CH]), sb("gden", [P, 2, CH])
        sc = sb("gsc", [P, CH, E0])
        sel, rep, mask = sb("sel", [P, CH, E0]), sb("rep", [P, CH, E0]), sb("mask", [P, CH, E0])
        top = sb("top", [P, CH, 8])
        keyrow = sb("keyrow", [P, CH, E0])
        zero = sb("gzero", [P, E0])
        silu = sb("silu", [I0, 2 * CH * P])
        hid = sb("hid", [I0, 2, 2 * CH * P])
        X, mv, keys = t["X"], t["mv"], t["keys"]
        (loaded, norm, turned, turned_sb, up, sil, hrd, down, gat, ex, own, kt, stored, ysum) = (
            sem("p4_" + n) for n in ("loaded", "x_normed", "turned", "turned_copied", "up_done", "silu_done",
                                     "hidden_ready", "down_done", "gate_done", "exp_done", "dve_steps",
                                     "keys_turned", "rows_stored", "z_added"))
        block = ctx.enter_context(nc.Block())
        rows = t["rows"].rearrange("(c k p) r -> c p k r", k=CH, p=P)
        DVE_STEPS = 9 + 3 * CH
        FIRST = 2

        @block.sync
        def _(sp):
            for counter in (stored, hrd, ysum, kt):
                sp.sem_inc(counter, START)
            for dst, src in ((gw[:], "gate_wT"), (ws1[:], "ws1T"), (ws3[:], "ws3T"), (ws2[:], "ws2T"),
                             (tokv[:], "tokv")):
                sp.dma_start(dst, t[src]).then_inc(loaded, 16)
            sp.dma_start(gb[:], t["gate_b0"].partition_broadcast(P)).then_inc(loaded, 16)
            with sp.Fori(0, NC // 2) as c2:
                for i in range(2):
                    c = 2 * c2 + i
                    sp.wait_ge(own, FIRST + (c + 1) * DVE_STEPS)
                    sp.dma_start(rows[c], xrow[:, i, :, :]).then_inc(stored, 16)
            sp.wait_ge(stored, START + 16 * NC)

        @block.scalar
        def _(a):
            with a.Fori(0, NC // 2) as c2:
                for i in range(2):
                    c = 2 * c2 + i
                    a.wait_ge(turned, c + 1)
                    a.activation(xnT[:, i, :], ps[0][:], ACT.Copy).then_inc(turned_sb, 1)
                    a.wait_ge(own, FIRST + c * DVE_STEPS + 2)
                    a.activation(xrow[:, i, :, D:D + E0], sc[:], ACT.Exp).then_inc(ex, 1)
                    a.wait_ge(up, c + 1)
                    a.wait_ge(hrd, START + c)
                    a.activation(silu[:], t["bank23"][0:I0, :], ACT.Silu).then_inc(sil, 1)

        @block.tensor
        def _(e):
            e.wait_ge(loaded, 16 * 6)
            with e.Fori(0, NC // 2) as c2:
                for i in range(2):
                    c = 2 * c2 + i
                    e.wait_ge(norm, c + 1)
                    for k in range(CH):
                        last = e.transpose(ps[0][:, k * P:(k + 1) * P], xrow[:, i, k, 0:D], t["ident"][:])
                    last.then_inc(turned, 1)
                    e.wait_ge(turned_sb, c + 1)
                    for k in range(CH):
                        last = e.matmul(ps[1][:, k * E0:(k + 1) * E0], xnT[:, i, k * P:(k + 1) * P], gw[:],
                                        start=True, stop=True)
                    last.then_inc(gat, 1)
                    e.wait_ge(hrd, START + c)
                    for w, bank in ((ws1, 2), (ws3, 4)):
                        for f in range(2):
                            last = e.matmul(ps[bank + f][0:I0, :], w[:, f * I0:(f + 1) * I0], xnT[:, i, :],
                                            start=True, stop=True)
                    last.then_inc(up, 1)
                    e.wait_ge(hrd, START + c + 1)
                    e.wait_ge(ysum, START + c)
                    for k in range(CH):
                        for f in range(2):
                            last = e.matmul(ps[6][:, k * D:(k + 1) * D],
                                            hid[:, i, f * CH * P + k * P:f * CH * P + (k + 1) * P],
                                            ws2[:, f, :], start=(f == 0), stop=(f == 1))
                    last.then_inc(down, 1)
                    e.wait_ge(own, FIRST + (c + 1) * DVE_STEPS)
                    stand_alone(e)
                    for k in range(CH):
                        last = e.transpose(ps[7][0:E0, k * P:(k + 1) * P], keyrow[:, k, :], t["ident"][:])
                    last.then_inc(kt, 1)

        @block.vector
        def _(dve):
            dve.wait_ge(loaded, 16 * 6)
            s = Steps(dve, own)
            s.done(dve.memset(zero[:], 0.0))
            s.do(dve.memset(xrow[:], 0.0))

            def normalise(c, i):
                for k in range(CH):
                    tile = c * CH + k
                    last = dve.tensor_scalar(xrow[:, i, k, 0:D], X[:, tile, :], mv[:, 0, bass.ds(tile, 1)],
                                             mv[:, 1, bass.ds(tile, 1)], ALU.subtract, ALU.mult)
                last.then_inc(norm, 1)

            with dve.Fori(0, NC // 2) as c2:
                for i in range(2):
                    c = 2 * c2 + i
                    s = Steps(dve, own, FIRST + c * DVE_STEPS, alone=True)
                    dve.wait_ge(stored, START + 16 * c)
                    normalise(c, i)
                    dve.wait_ge(gat, c + 1)
                    g = ps[1][:, 0:CH * E0].rearrange("p (k e) -> p k e", k=CH)
                    bc = lambda ap: ap.unsqueeze(2).broadcast_to([P, CH, E0])
                    score, rank = xrow[:, i, :, D:D + E0], xrow[:, i, :, D + E0:ROW]
                    s.do(dve.reduce_max(mx[:, i, :], g, X_AXIS))
                    s.do(dve.tensor_tensor(sc[:], g, bc(mx[:, i, :]), ALU.subtract))
                    dve.wait_ge(sil, c + 1)
                    dve.tensor_tensor(hid[:, i, :], silu[:], t["bank45"][0:I0, :], ALU.mult).then_inc(hrd, 1)
                    dve.wait_ge(ex, c + 1)
                    s.do(dve.reduce_sum(den[:, i, :], score, X_AXIS))
                    s.do(dve.reciprocal(den[:, i, :], den[:, i, :]))
                    s.do(dve.tensor_tensor(score, score, bc(den[:, i, :]), ALU.mult))
                    s.do(dve.tensor_tensor(sel[:], score, gb[:].unsqueeze(1).broadcast_to([P, CH, E0]),
                                           ALU.add))
                    for k in range(CH):
                        s.done(dve.max(top[:, k, :], sel[:, k, :]))
                    s.settle()
                    s.do(dve.memset(top[:, :, K0:8], 3.0e38))
                    for k in range(CH):
                        s.done(dve.match_replace(rep[:, k, :], top[:, k, :], sel[:, k, :], -3.0e38))
                    s.settle()
                    s.do(dve.tensor_tensor(mask[:], rep[:], sel[:], ALU.not_equal))
                    for k in range(CH):
                        s.done(dve.tensor_tensor_scan(xrow[:, i, k, D + E0:ROW], mask[:, k, :], zero[:],
                                                      0.0, ALU.add, ALU.add))
                    dve.wait_ge(kt, START + c)
                    s.do(dve.tensor_tensor(keyrow[:], mask[:], bc(tokv[:, bass.ds(c * CH, CH)]), ALU.mult))
                    assert s.n == DVE_STEPS
                    dve.wait_ge(down, c + 1)
                    xc = X[:, bass.ds(c * CH, CH), :]
                    dve.tensor_tensor(xc, xc, ps[6][:].rearrange("p (k d) -> p k d", k=CH),
                                      ALU.add).then_inc(ysum, 1)
                    dve.wait_ge(kt, START + c + 1)
                    dve.tensor_copy(keys[:, bass.ds(c * CH * P, CH * P)], ps[7][0:E0, :]).then_inc(t["keys_in"], 1)
            dve.wait_ge(t["keys_in"], NC)


def pick_slots(nc, t, sem, ps):
    ctx = ExitStack()
    with ctx:
        def sb(name, shape, dt=F32):
            return ctx.enter_context(nc.sbuf_tensor(name, shape, dt))

        half = N_TOK // 2
        fold = sb("fold", [P, half])
        work = sb("work", [P, half])
        first = sb("firstk", [P, CAP])
        both = sb("bothk", [E0, 2 * CAP])
        both2 = sb("bothk2", [E0, 2 * CAP])
        found = sb("found", [E0, CAP])
        keys, slotv = t["keys"], t["slotv"]
        own, turned = sem("p5_dve_steps"), sem("p5_turned")
        block = ctx.enter_context(nc.Block())

        @block.vector
        def _(dve):
            s = Steps(dve, own)
            s.done(dve.tensor_copy(fold[0:E0, :], keys[:, 0:half]))
            s.do(dve.tensor_copy(fold[E0:P, :], keys[:, half:N_TOK]))

            def largest(out, a, b):
                for r in range(CAP // 8):
                    s.do(dve.max(out[:, r * 8:(r + 1) * 8], a[:]))
                    s.do(dve.match_replace(b[:], out[:, r * 8:(r + 1) * 8], a[:], 0.0))
                    a, b = b, a
            largest(first, fold, work)
            s.done(dve.tensor_copy(both[:, 0:CAP], first[0:E0, :]))
            s.do(dve.tensor_copy(both[:, CAP:2 * CAP], first[E0:P, :]))
            largest(found, both, both2)
            dve.wait_ge(turned, 1)
            v = ps[0][0:CAP, 0:E0].rearrange("p (j o) -> p j o", o=2)
            s.done(dve.tensor_copy(slotv[0:CAP, :], v[:, :, 0]))
            s.do(dve.tensor_copy(slotv[CAP:P, :], v[:, :, 1]))
            s.do(dve.tensor_scalar(t["tok"][:], slotv[:], -1.0, float(N_TOK), ALU.mult, ALU.add))
            s.do(dve.tensor_scalar(t["gidx"][:], t["tok"][:], float(N_TOK - 1), None, ALU.min))
            s.do(dve.tensor_scalar(t["full"][:], slotv[:], 0.0, None, ALU.is_gt))
            t["pick_steps"] = s.n

        @block.tensor
        def _(e):
            e.wait_ge(own, t["pick_steps"] - 5)
            e.transpose(ps[0][0:CAP, 0:E0], found[:], t["ident"][0:E0, 0:E0]).then_inc(turned, 1)


def routed_experts(nc, t, sem, ps):
    ctx = ExitStack()
    with ctx:
        def sb(name, shape, dt=F32):
            return ctx.enter_context(nc.sbuf_tensor(name, shape, dt))

        GT = 4
        NGR = E0 // 2 // GT
        EG = 2 * GT
        w1 = sb("w1b", [P, 2, EG * I0])
        w3 = sb("w3b", [P, 2, EG * I0])
        w2 = sb("w2b", [I0, 2, EG * D])
        xg = [sb(f"xg{i}", [P, GT, ROW]) for i in range(2)]
        sidx = [sb(f"sidx{i}", [P, GT], I32) for i in range(2)]
        didx = [sb(f"didx{i}", [P, GT], I32) for i in range(2)]
        yo = [sb(f"yo{i}", [P, GT, D]) for i in range(2)]
        xT = sb("xgT", [P, GT * P])
        silu = sb("silu5", [I0, GT * P])
        hid = sb("hid5", [I0, GT * P])
        sr = sb("scorerank", [P, GT, 2])
        dst = sb("dstf", [P, GT])
        wl, ixr, gth, turned, turned_sb, up, sil, hrd, down, own, sct, yrd = (sem("p6_" + n) for n in (
            "weights", "index_ready", "gathered", "turned", "turned_copied", "up_done", "silu_done",
            "hidden_ready", "down_done", "dve_steps", "scattered", "y_ready"))
        block = ctx.enter_context(nc.Block())
        DVE_STEPS = EG + 4
        tok, full, gidx = t["tok"], t["full"], t["gidx"]

        @block.sync
        def _(sp):
            for counter in (down, yrd, hrd):
                sp.sem_inc(counter, START)
            with sp.Fori(0, NGR // 2) as g2:
                for i in range(2):
                    g = 2 * g2 + i
                    sp.wait_ge(down, START + g)
                    sp.dma_start(w1[:, i, :], t["w1T"][:, bass.ds(g * EG * I0, EG * I0)]).then_inc(wl, 16)
                    sp.dma_start(w3[:, i, :], t["w3T"][:, bass.ds(g * EG * I0, EG * I0)]).then_inc(wl, 16)
                    sp.dma_start(w2[:, i, :], t["w2T"][:, bass.ds(g * EG * D, EG * D)]).then_inc(wl, 16)

        @block.gpsimd
        def _(pool):
            def scatter(g, i):
                pool.wait_ge(yrd, START + g + 1)
                stand_alone(pool)
                for k in range(GT):
                    pool.indirect_dma_start(
                        out=t["ybuf"], out_offset=bass.IndirectOffsetOnAxis(ap=didx[i][:, k:k + 1], axis=0),
                        in_=yo[i][:, k, :], in_offset=None, bounds_check=N_TOK * K0 - 1,
                        oob_is_err=False).then_inc(sct, 16)

            with pool.Fori(0, NGR // 2) as g2:
                for i in range(2):
                    g = 2 * g2 + i
                    pool.wait_ge(yrd, START + g)
                    stand_alone(pool)
                    pool.tensor_copy(sidx[i][:], gidx[:, bass.ds(g * GT, GT)]).then_inc(ixr, 1)
                    pool.wait_ge(ixr, g + 1)
                    stand_alone(pool)
                    for k in range(GT):
                        pool.indirect_dma_start(
                            out=xg[i][:, k, :], out_offset=None, in_=t["rows"],
                            in_offset=bass.IndirectOffsetOnAxis(ap=sidx[i][:, k:k + 1], axis=0)
                        ).then_inc(gth, 16)
                    scatter(g, i)
                pool.wait_ge(sct, 16 * GT * 2 * (g2 + 1))
                stand_alone(pool)
            pool.wait_ge(sct, 16 * GT * NGR)

        @block.scalar
        def _(a):
            with a.Fori(0, NGR // 2) as g2:
                for i in range(2):
                    g = 2 * g2 + i
                    a.wait_ge(turned, g + 1)
                    a.activation(xT[:], ps[0][:], ACT.Copy).then_inc(turned_sb, 1)
                    a.wait_ge(up, g + 1)
                    a.activation(silu[:], ps[1][0:I0, :], ACT.Silu).then_inc(sil, 1)

        @block.tensor
        def _(e):
            with e.Fori(0, NGR // 2) as g2:
                for i in range(2):
                    g = 2 * g2 + i
                    e.wait_ge(gth, (g + 1) * 16 * GT)
                    for k in range(GT):
                        last = e.transpose(ps[0][:, k * P:(k + 1) * P], xg[i][:, k, 0:D], t["ident"][:])
                    last.then_inc(turned, 1)
                    e.wait_ge(turned_sb, g + 1)
                    e.wait_ge(wl, (g + 1) * 48)
                    e.wait_ge(hrd, START + g)
                    for w, bank in ((w1, 1), (w3, 2)):
                        for x in range(EG):
                            last = e.matmul(ps[bank][0:I0, x * CAP:(x + 1) * CAP],
                                            w[:, i, x * I0:(x + 1) * I0], xT[:, x * CAP:(x + 1) * CAP],
                                            start=True, stop=True)
                    last.then_inc(up, 1)
                    e.wait_ge(hrd, START + g + 1)
                    e.wait_ge(yrd, START + g)
                    for x in range(EG):
                        last = e.matmul(ps[3][(x % 2) * CAP:(x % 2 + 1) * CAP, (x // 2) * D:(x // 2 + 1) * D],
                                        hid[:, x * CAP:(x + 1) * CAP], w2[:, i, x * D:(x + 1) * D],
                                        start=True, stop=True)
                    last.then_inc(down, 1)

        @block.vector
        def _(dve):
            with dve.Fori(0, NGR // 2) as g2:
                for i in range(2):
                    g = 2 * g2 + i
                    s = Steps(dve, own, g * DVE_STEPS)
                    dve.wait_ge(gth, (g + 1) * 16 * GT)
                    dve.wait_ge(yrd, START + g)
                    for k in range(GT):
                        v = xg[i][:, k, D:ROW].rearrange("p (a e) -> p a e", a=2)
                        for o in range(2):
                            h = slice(o * CAP, (o + 1) * CAP)
                            s.done(dve.tensor_copy(sr[h, k, :], v[h, :, bass.ds(g * EG + 2 * k + o, 1)]
                                                   .squeeze(2)))
                    s.settle()
                    s.do(dve.tensor_tensor(sr[:, :, 0], sr[:, :, 0], full[:, bass.ds(g * GT, GT)], ALU.mult))
                    s.do(dve.scalar_tensor_tensor(out=dst[:], in0=tok[:, bass.ds(g * GT, GT)],
                                                  scalar=float(K0), in1=sr[:, :, 1], op0=ALU.mult,
                                                  op1=ALU.add))
                    s.do(dve.scalar_tensor_tensor(out=dst[:], in0=full[:, bass.ds(g * GT, GT)],
                                                  scalar=-8.0, in1=dst[:], op0=ALU.mult, op1=ALU.add))
                    s.do(dve.tensor_scalar(didx[i][:], dst[:], 7.0, None, ALU.add))
                    assert s.n == DVE_STEPS
                    dve.wait_ge(sil, g + 1)
                    dve.tensor_tensor(hid[:], silu[:], ps[2][0:I0, :], ALU.mult).then_inc(hrd, 1)
                    dve.wait_ge(down, START + g + 1)
                    dve.tensor_tensor(yo[i][:], ps[3][:].rearrange("p (k d) -> p k d", k=GT),
                                      sr[:, :, 0].unsqueeze(2).broadcast_to([P, GT, D]),
                                      ALU.mult).then_inc(yrd, 1)
H1, DH1 = 4, 32
FF = 4 * D
E1, F1 = 8, 256
KSCALE = DH1 ** -0.25


def rstd_of(pool, t, own, steps, ready):
    pool.wait_ge(own, steps)
    pool.tensor_tensor(t["mv"][:, 1, :], t["mv"][:, 1, :], t["neg_half"][:, 0:NT], ALU.pow).then_inc(ready, 1)


def normalise_chunk(dve, out, src, mv, c):
    for k in range(CH):
        tile = c * CH + k
        last = dve.tensor_scalar(out[:, k, :], src[:, tile, :], mv[:, 0, bass.ds(tile, 1)],
                                 mv[:, 1, bass.ds(tile, 1)], ALU.subtract, ALU.mult)
    return last


def combine(nc, t, sem, ps):
    ctx = ExitStack()
    with ctx:
        def sb(name, shape, dt=F32):
            return ctx.enter_context(nc.sbuf_tensor(name, shape, dt))

        yk = sb("yk", [P, 2, CH, K0 * D])
        ysum = sb("ysumt", [P, CH, D])
        stats, tmp = sb("stats7", [P, NT, 6]), sb("tmp7", [P, 2, NT])
        X, XO, mv = t["X"], t["XO"], t["mv"]
        ld, summed, added, stat, own, var1, nrm = (sem("p7_" + n) for n in (
            "rows_loaded", "summed", "added", "stats", "dve_steps", "rstd_ready", "normed"))
        block = ctx.enter_context(nc.Block())
        y = t["ybuf"].rearrange("(c k p s) d -> c p k (s d)", k=CH, p=P, s=K0)

        @block.sync
        def _(sp):
            for counter in (summed,):
                sp.sem_inc(counter, START)
            with sp.Fori(0, NC // 2) as c2:
                for i in range(2):
                    c = 2 * c2 + i
                    sp.wait_ge(summed, START + c)
                    sp.dma_start(yk[:, i, :, :], y[c]).then_inc(ld, 16)

        @block.gpsimd
        def _(pool):
            rstd_of(pool, t, own, STATS_STEPS, var1)
            rstd_of(pool, t, own, 2 * STATS_STEPS, var1)
            pool.wait_ge(var1, 2)

        @block.vector
        def _(dve):
            with dve.Fori(0, NC // 2) as c2:
                for i in range(2):
                    c = 2 * c2 + i
                    dve.wait_ge(ld, (c + 1) * 16)
                    for k in range(CH):
                        last = dve.reduce_sum(ysum[:, k, :], yk[:, i, k, :].rearrange("p (s d) -> p d s", s=K0),
                                              X_AXIS)
                    last.then_inc(summed, 1)
                    dve.wait_ge(summed, START + c + 1)
                    xc = X[:, bass.ds(c * CH, CH), :]
                    dve.tensor_tensor(xc, xc, ysum[:], ALU.add).then_inc(added, 1)
                    dve.wait_ge(added, c + 1)
                    for k in range(CH):
                        dve.bn_stats(stats[:, c * CH + k, :], X[:, c * CH + k, :]).then_inc(stat, 1)
            dve.wait_ge(stat, NT)
            finish_stats(dve, Steps(dve, own), stats, mv, tmp, NT)
            dve.wait_ge(var1, 1)
            with dve.Fori(0, NC) as c:
                normalise_chunk(dve, XO[:, bass.ds(c * CH, CH), :], X, mv, c).then_inc(nrm, 1)
                dve.wait_ge(nrm, c + 1)
                for k in range(CH):
                    dve.bn_stats(stats[:, c * CH + k, :], XO[:, c * CH + k, :]).then_inc(stat, 1)
            dve.wait_ge(stat, 2 * NT)
            finish_stats(dve, Steps(dve, own, STATS_STEPS), stats, mv, tmp, NT)


def linear_attention(nc, t, sem, ps):
    ctx = ExitStack()
    with ctx:
        def sb(name, shape, dt=F32):
            return ctx.enter_context(nc.sbuf_tensor(name, shape, dt))

        CB = TB // CH
        wk, wqv, wo, bo = sb("wk1", [P, D]), sb("wqv1", [P, 2 * D]), sb("wo1", [P, D]), sb("bo1", [P, D])
        lncol = sb("ln1col", [P, 2])
        block32 = sb("block32", [P, D])
        h = sb("h1", [P, 2, CH, D])
        hT = sb("h1T", [P, 2, CH * P])
        kT, ke = sb("k1T", [P, S]), sb("k1e", [P, S])
        ktok, vtok = sb("ktok", [P, TB, D]), sb("vtok", [P, TB, D])
        qs, qe = sb("qs", [P, CH, D]), sb("qe", [P, CH, D])
        qT = sb("q1T", [P, S])
        qm, qd = sb("qm", [P, CH * H1]), sb("qd", [P, CH * H1])
        km, ksum, krec = sb("km", [P, 2]), sb("ksum", [P, 1]), sb("krec", [P, 1])
        cmat = sb("cmat", [P, D])
        aT = sb("a1T", [P, S])
        stats, tmp = sb("stats8", [P, NT, 6]), sb("tmp8", [P, 2, NT])
        XO, mv = t["XO"], t["mv"]
        ld, own, nrm, act, pe, biased, stat, rst, own2 = (sem("p8_" + n) for n in (
            "loaded", "dve_steps", "normed", "act_steps", "pe_steps", "xo_biased", "stats", "rstd_ready",
            "stat_steps"))
        block = ctx.enter_context(nc.Block())
        DVE_STEPS, ACT_STEPS, PE_STEPS = 6 * CB + 5 + 2, 4 * CB + 1 + 2, 4 * CB + 4

        @block.sync
        def _(sp):
            for dst, n in ((wk[:], "l1_wk"), (wqv[:, 0:D], "l1_wq"), (wqv[:, D:2 * D], "l1_wv"),
                           (wo[:], "l1_wo"), (block32[:], "block32")):
                sp.dma_start(dst, t[n]).then_inc(ld, 16)
            sp.dma_start(bo[:], t["l1_bo"].partition_broadcast(P)).then_inc(ld, 16)
            for i, n in enumerate(("ln1_g", "ln1_b")):
                sp.dma_start(lncol[:, i:i + 1], t[n].rearrange("(p a) -> p a", a=1)).then_inc(ld, 16)
        LOADED = 16 * 8

        @block.gpsimd
        def _(pool):
            pool.wait_ge(ld, LOADED)
            with pool.Fori(0, B) as b:
                pool.wait_ge(nrm, (b + 1) * CB)
                xc = XO[:, bass.ds(b * TB, TB), :]
                pool.tensor_tensor(xc, xc, bo[:].unsqueeze(1).broadcast_to([P, TB, D]), ALU.add)\
                    .then_inc(biased, 1)
            rstd_of(pool, t, own2, STATS_STEPS, rst)
            pool.wait_ge(rst, 1)

        @block.tensor
        def _(e):
            e.wait_ge(ld, LOADED)
            with e.Fori(0, B) as b:
                a0, d0 = b * ACT_STEPS, b * DVE_STEPS
                for c in range(CB):
                    e.wait_ge(nrm, b * CB + c + 1)
                    for k in range(CH):
                        last = e.transpose(ps[0][:, k * P:(k + 1) * P], h[:, c, k, :], t["ident"][:])
                    last.then_inc(pe, 1)
                    e.wait_ge(act, a0 + 4 * c + 1)
                    e.matmul(ps[1][:], wk[:], hT[:, c, :], start=True, stop=True).then_inc(pe, 1)
                    for k in range(CH):
                        last = e.matmul(ps[2 + k // 2][:, (k % 2) * 2 * D:(k % 2 + 1) * 2 * D],
                                        hT[:, c, k * P:(k + 1) * P], wqv[:], start=True, stop=True)
                    last.then_inc(pe, 1)
                    e.wait_ge(own, d0 + 6 * c + 5)
                    for k in range(CH):
                        last = e.transpose(ps[4][:, k * P:(k + 1) * P], qs[:, k, :], t["ident"][:])
                    last.then_inc(pe, 1)
                    e.wait_ge(own, d0 + 6 * c + 6)
                    e.wait_ge(act, a0 + 4 * c + 4)
                e.wait_ge(act, a0 + 4 * CB + 1)
                for k in range(TB):
                    last = e.transpose(ps[k // CH][:, (k % CH) * P:(k % CH + 1) * P], ke[:, k * P:(k + 1) * P],
                                       t["ident"][:])
                last.then_inc(pe, 1)
                e.wait_ge(own, d0 + 6 * CB + 3)
                for k in range(TB):
                    last = e.matmul(ps[5][:, 0:D], ktok[:, k, :], vtok[:, k, :], start=(k == 0),
                                    stop=(k == TB - 1))
                last.then_inc(pe, 1)
                e.wait_ge(own, d0 + 6 * CB + 5)
                for c in range(2):
                    last = e.matmul(ps[2 + c][:], cmat[:], qT[:, c * 512:(c + 1) * 512], start=True, stop=True)
                last.then_inc(pe, 1)
                e.wait_ge(act, a0 + 4 * CB + 3)
                for k in range(TB):
                    last = e.matmul(ps[6 + k // CH][:, (k % CH) * D:(k % CH + 1) * D],
                                    aT[:, k * P:(k + 1) * P], wo[:], start=True, stop=True)
                last.then_inc(pe, 1)
                e.wait_ge(own, d0 + DVE_STEPS)

        @block.scalar
        def _(a):
            a.wait_ge(ld, LOADED)
            with a.Fori(0, B) as b:
                p0, d0 = b * PE_STEPS, b * DVE_STEPS
                s = Steps(a, act, b * ACT_STEPS)
                for c in range(CB):
                    a.wait_ge(pe, p0 + 4 * c + 1)
                    s.done(a.activation(hT[:, c, :], ps[0][:], ACT.Identity, bias=lncol[:, 1:2],
                                        scale=lncol[:, 0:1]))
                    a.wait_ge(pe, p0 + 4 * c + 2)
                    s.done(a.activation(kT[:, c * 512:(c + 1) * 512], ps[1][:], ACT.Copy))
                    a.wait_ge(own, d0 + 6 * c + 2)
                    for j in range(2):
                        last = a.activation(vtok[:, c * CH + 2 * j:c * CH + 2 * j + 2, :],
                                            ps[2 + j][:].rearrange("p (k w d) -> p k w d", k=2, w=2)[:, :, 1, :],
                                            ACT.Copy)
                    s.done(last)
                    s.done(a.activation(qe[:], qs[:], ACT.Exp, scale=KSCALE))
                a.wait_ge(own, d0 + 6 * CB + 2)
                s.done(a.activation(ke[:], kT[:], ACT.Exp, bias=km[:, 1:2], scale=KSCALE,
                                    accum_out=ksum[:]))
                a.wait_ge(pe, p0 + 4 * CB + 3)
                for c in range(2):
                    s.done(a.activation(aT[:, c * 512:(c + 1) * 512], ps[2 + c][:], ACT.Copy))
                assert s.n == ACT_STEPS

        @block.vector
        def _(dve):
            dve.wait_ge(ld, LOADED)
            with dve.Fori(0, B) as b:
                a0, p0 = b * ACT_STEPS, b * PE_STEPS
                s = Steps(dve, own, b * DVE_STEPS)
                for c in range(CB):
                    normalise_chunk(dve, h[:, c, :, :], XO, mv, b * CB + c).then_inc(nrm, 1)
                for c in range(CB):
                    dve.wait_ge(pe, p0 + 4 * c + 3)
                    for j in range(2):
                        v = ps[2 + j][:].rearrange("p (k w h d) -> p k w h d", k=2, w=2, h=H1)[:, :, 0, :, :]
                        last = dve.reduce_max(qm[:, j * 2 * H1:(j + 1) * 2 * H1]
                                              .rearrange("p (k h) -> p k h", k=2), v, X_AXIS)
                    s.do(last)
                    for j in range(2):
                        v = ps[2 + j][:].rearrange("p (k w h d) -> p k w h d", k=2, w=2, h=H1)
                        for k in range(2):
                            m = qm[:, (2 * j + k) * H1:(2 * j + k + 1) * H1]
                            last = dve.tensor_tensor(
                                qs[:, 2 * j + k, :].rearrange("p (h d) -> p h d", h=H1), v[:, k, 0, :, :],
                                m.unsqueeze(2).broadcast_to([P, H1, DH1]), ALU.subtract)
                    s.do(last)
                    dve.wait_ge(act, a0 + 4 * c + 4)
                    q4 = qe[:].rearrange("p k (h d) -> p (k h) d", h=H1)
                    s.do(dve.reduce_sum(qd[:], q4, X_AXIS))
                    s.do(dve.reciprocal(qd[:], qd[:]))
                    s.done(dve.tensor_tensor(qs[:].rearrange("p k (h d) -> p (k h) d", h=H1), q4,
                                             qd[:].unsqueeze(2).broadcast_to([P, CH * H1, DH1]), ALU.mult))
                    dve.wait_ge(pe, p0 + 4 * c + 4)
                    s.do(dve.tensor_copy(qT[:, c * 512:(c + 1) * 512], ps[4][:]))
                dve.wait_ge(act, a0 + 4 * (CB - 1) + 2)
                s.do(dve.reduce_max(km[:, 0:1], kT[:], X_AXIS))
                s.do(dve.tensor_scalar(km[:, 1:2], km[:, 0:1], -KSCALE, None, ALU.mult))
                dve.wait_ge(pe, p0 + 4 * CB + 1)
                s.done(dve.tensor_copy(ktok[:].rearrange("p k d -> p (k d)"), t["bank01"]))
                s.do(dve.reciprocal(krec[:], ksum[:]))
                dve.wait_ge(pe, p0 + 4 * CB + 2)
                s.do(dve.scalar_tensor_tensor(out=cmat[:], in0=ps[5][:, 0:D], scalar=krec[:],
                                              in1=block32[:], op0=ALU.mult, op1=ALU.mult))
                dve.wait_ge(pe, p0 + 4 * CB + 4)
                dve.wait_ge(biased, b + 1)
                for c in range(CB):
                    xc = XO[:, bass.ds(b * TB + c * CH, CH), :]
                    s.done(dve.tensor_tensor(xc, xc, ps[6 + c][:].rearrange("p (k d) -> p k d", k=CH),
                                             ALU.add))
                s.settle()
                for k in range(TB):
                    dve.bn_stats(stats[:, b * TB + k, :], XO[:, b * TB + k, :]).then_inc(stat, 1)
                assert s.n == DVE_STEPS, (s.n, DVE_STEPS)
            dve.wait_ge(stat, NT)
            finish_stats(dve, Steps(dve, own2), stats, mv, tmp, NT)


def feed_forward(nc, t, sem, ps):
    ctx = ExitStack()
    with ctx:
        def sb(name, shape, dt=F32):
            return ctx.enter_context(nc.sbuf_tensor(name, shape, dt))

        NF = FF // P
        wf1, wf2, wd = sb("wf1", [P, FF]), sb("wf2", [P, NF, D]), sb("wd", [P, D])
        lncol, bf1 = sb("ln2col", [P, 2]), sb("bf1", [P, NF])
        bf2, bd = sb("bf2", [P, D]), sb("bd", [P, D])
        h, hT = sb("h2", [P, 2, CH, D]), sb("h2T", [P, CH * P])
        f = sb("f2", [P, NF, CH * P])
        y, yT = sb("y2", [P, CH, D]), sb("y2T", [P, CH * P])
        yb = sb("yb2", [P, 2, CH, D])
        stats, tmp = sb("stats9", [P, NT, 6]), sb("tmp9", [P, 2, NT])
        X, XO, mv = t["X"], t["XO"], t["mv"]
        ld, nrm, turned, hts, f1, gl, f2, ysum, yturned, yts, d1, xs, stat, own, rst, yb_r, xb_r = (
            sem("p9_" + n) for n in (
                "loaded", "normed", "turned", "turned_copied", "ff1_done", "gelu_done", "ff2_done",
                "y_summed", "y_turned", "y_copied", "wd_done", "x_added", "stats", "dve_steps",
                "rstd_ready", "y_biased", "x_biased"))
        block = ctx.enter_context(nc.Block())

        @block.sync
        def _(sp):
            for counter in (ysum, yts, xs, gl, f2, turned, yturned):
                sp.sem_inc(counter, START)
            for dst, n in ((wf1[:], "w_ff1"), (wd[:], "w_d")):
                sp.dma_start(dst, t[n]).then_inc(ld, 16)
            sp.dma_start(wf2[:], t["w_ff2"].rearrange("(f p) d -> p f d", p=P)).then_inc(ld, 16)
            sp.dma_start(bf1[:], t["b_ff1"]).then_inc(ld, 16)
            sp.dma_start(bf2[:], t["b_ff2"].partition_broadcast(P)).then_inc(ld, 16)
            sp.dma_start(bd[:], t["b_d"].partition_broadcast(P)).then_inc(ld, 16)
            for i, n in enumerate(("ln2_g", "ln2_b")):
                sp.dma_start(lncol[:, i:i + 1], t[n].rearrange("(p a) -> p a", a=1)).then_inc(ld, 16)
            t["w7"]["load"](sp)
        LOADED = 16 * 8

        @block.gpsimd
        def _(pool):
            pool.wait_ge(ld, LOADED)
            with pool.Fori(0, NC // 2) as c2:
                for i in range(2):
                    c = 2 * c2 + i
                    cs = bass.ds(c * CH, CH)
                    pool.wait_ge(ysum, START + c)
                    pool.tensor_tensor(yb[:, i, :, :], XO[:, cs, :],
                                       bf2[:].unsqueeze(1).broadcast_to([P, CH, D]), ALU.add).then_inc(yb_r, 1)
                    pool.tensor_tensor(X[:, cs, :], X[:, cs, :],
                                       bd[:].unsqueeze(1).broadcast_to([P, CH, D]), ALU.add).then_inc(xb_r, 1)
            t["w7"]["do_split"](pool)
            rstd_of(pool, t, own, STATS_STEPS, rst)
            pool.wait_ge(rst, 1)

        @block.tensor
        def _(e):
            e.wait_ge(ld, LOADED)

            def back(c):
                e.wait_ge(gl, START + (c + 1) * NF)
                e.wait_ge(ysum, START + c)
                for k in range(CH):
                    for n in range(NF):
                        last = e.matmul(ps[5][:, k * D:(k + 1) * D], f[:, n, k * P:(k + 1) * P], wf2[:, n, :],
                                        start=(n == 0), stop=(n == NF - 1))
                last.then_inc(f2, 1)
                e.wait_ge(ysum, START + c + 1)
                e.wait_ge(yts, START + c)
                for k in range(CH):
                    last = e.transpose(ps[6][:, k * P:(k + 1) * P], y[:, k, :], t["ident"][:])
                last.then_inc(yturned, 1)
                e.wait_ge(yts, START + c + 1)
                e.wait_ge(xs, START + c)
                for k in range(CH):
                    last = e.matmul(ps[7][:, k * D:(k + 1) * D], yT[:, k * P:(k + 1) * P], wd[:],
                                    start=True, stop=True)
                last.then_inc(d1, 1)

            with e.Fori(0, NC // 2) as c2:
                for i in range(2):
                    c = 2 * c2 + i
                    e.wait_ge(nrm, c + 1)
                    for k in range(CH):
                        last = e.transpose(ps[0][:, k * P:(k + 1) * P], h[:, i, k, :], t["ident"][:])
                    last.then_inc(turned, 1)
                    e.wait_ge(hts, c + 1)
                    for n in range(NF):
                        e.wait_ge(gl, START + c * NF + n)
                        e.matmul(ps[1 + n][:], wf1[:, n * P:(n + 1) * P], hT[:], start=True,
                                 stop=True).then_inc(f1, 1)
                    back(c)

        @block.scalar
        def _(a):
            a.wait_ge(ld, LOADED)
            with a.Fori(0, NC) as c:
                a.wait_ge(turned, START + c + 1)
                a.activation(hT[:], ps[0][:], ACT.Identity, bias=lncol[:, 1:2],
                             scale=lncol[:, 0:1]).then_inc(hts, 1)
                a.wait_ge(f2, START + c)
                for n in range(NF):
                    a.wait_ge(f1, c * NF + n + 1)
                    a.activation(f[:, n, :], ps[1 + n][:], ACT.Gelu_apprx_tanh,
                                 bias=bf1[:, n:n + 1]).then_inc(gl, 1)
                a.wait_ge(yturned, START + c + 1)
                a.activation(yT[:], ps[6][:], ACT.Copy).then_inc(yts, 1)

        @block.vector
        def _(dve):
            with dve.Fori(0, NC // 2) as c2:
                for i in range(2):
                    c = 2 * c2 + i
                    dve.wait_ge(turned, START + c)
                    normalise_chunk(dve, h[:, i, :, :], XO, mv, c).then_inc(nrm, 1)
                    dve.wait_ge(f2, START + c + 1)
                    dve.wait_ge(yb_r, c + 1)
                    dve.wait_ge(yturned, START + c)
                    dve.tensor_tensor(y[:], ps[5][:].rearrange("p (k d) -> p k d", k=CH), yb[:, i, :, :],
                                      ALU.add).then_inc(ysum, 1)
                    dve.wait_ge(d1, c + 1)
                    dve.wait_ge(xb_r, c + 1)
                    xc = X[:, bass.ds(c * CH, CH), :]
                    dve.tensor_tensor(xc, xc, ps[7][:].rearrange("p (k d) -> p k d", k=CH),
                                      ALU.add).then_inc(xs, 1)
                    dve.wait_ge(xs, START + c + 1)
                    for k in range(CH):
                        dve.bn_stats(stats[:, c * CH + k, :], X[:, c * CH + k, :]).then_inc(stat, 1)
            dve.wait_ge(stat, NT)
            finish_stats(dve, Steps(dve, own), stats, mv, tmp, NT)


def chunks(eng, body):
    body(0, 0, True, False)
    with eng.Fori(0, NC // 2 - 1) as c2:
        for i in range(2):
            body(2 * c2 + 1 + i, (1 + i) % 2, False, False)
    body(NC - 1, 1, False, True)


def expert_weights(nc, t, sb, sem):
    NF = F1 // P
    w = {n: sb(n, [P, E1, F1]) for n in ("gate7", "up7")}
    for n in ("gate7", "up7"):
        w[n + "_high"], w[n + "_low"] = sb(n + "h", [P, E1, F1], F32R), sb(n + "l", [P, E1, F1], F32R)
    w["down7"] = sb("down7", [P, E1, NF, D])
    w["loaded"], w["split_high"], w["split"] = (sem("w7_" + n) for n in ("loaded", "high_parts", "low_parts"))

    def load(sp):
        for dst, n in (("gate7", "gate_w1"), ("up7", "up_w1")):
            sp.dma_start(w[dst][:], t[n].rearrange("e d f -> d e f")).then_inc(w["loaded"], 16)
        sp.dma_start(w["down7"][:].rearrange("p e n d -> p (e n) d"),
                     t["down_w1"].rearrange("e (n p) d -> p (e n) d", p=P)).then_inc(w["loaded"], 16)

    def split(pool):
        pool.wait_ge(w["loaded"], 48)
        for n in ("gate7", "up7"):
            pool.tensor_copy(w[n + "_high"][:], w[n][:]).then_inc(w["split_high"], 1)
        pool.wait_ge(w["split_high"], 2)
        for n in ("gate7", "up7"):
            pool.tensor_tensor(w[n + "_low"][:], w[n][:], w[n + "_high"][:].bitcast(F32), ALU.subtract)\
                .then_inc(w["split"], 1)
        pool.wait_ge(w["split"], 2)
    w["load"], w["do_split"] = load, split
    return w


def experts_of_two(nc, t, sem, ps):
    ctx = ExitStack()
    with ctx:
        def sb(name, shape, dt=F32):
            return ctx.enter_context(nc.sbuf_tensor(name, shape, dt))

        NF = F1 // P
        w = t["w7"]
        wdn = w["down7"]
        gate, upw = ([w[n + "_high"], w[n + "_low"]] for n in ("gate7", "up7"))
        rw = sb("rw", [P, E1])
        bg, bu = sb("bg7", [P, E1, NF]), sb("bu7", [P, E1, NF])
        bdn = sb("bdn7", [E1, D])
        xf, xT = sb("xf7", [P, CH, D]), sb("xf7T", [P, CH * P])
        xh, xl = sb("xf7h", [P, 2, CH * P], F32R), sb("xf7l", [P, 2, CH * P], F32R)
        sc, rep, top = sb("sc7", [P, CH, E1]), sb("rep7", [P, CH, E1]), sb("top7", [P, CH, 8])
        prob, mx, pw = sb("prob7", [P, CH, E1]), sb("mx7", [P, CH]), sb("pw7", [P, 2, CH, E1])
        pT = sb("pT7", [E1, CH * P])
        sil = sb("sil7", [P, 2, CH * P])
        hid = sb("hid7", [P, 2, NF, CH * P])
        acc = sb("acc7", [P, 2, CH, D])
        X, mv = t["X"], t["mv"]
        ld, nrm, turned, xts, xls, own, ex, rt, pt, ptr, db, ini, gu, sl, hd, dn, ac, st = (
            sem("p10_" + n) for n in (
                "loaded", "normed", "turned", "turned_copied", "low_ready", "dve_steps", "exp_done", "routed",
                "p_turned", "p_copied", "bias_done", "acc_begun", "gate_up_done", "silu_done",
                "hidden_ready", "down_done", "accumulated", "stored"))
        block = ctx.enter_context(nc.Block())
        DVE_STEPS = 12 + 2 * CH
        UN = E1 * NF
        ADDS = E1 * CH
        out = t["out"].rearrange("b (n k p) d -> (b n) p k d", k=CH, p=P)

        @block.sync
        def _(sp):
            for counter in (hd, turned, st, ac, ini, rt):
                sp.sem_inc(counter, START)
            sp.dma_start(rw[:], t["router_wT"]).then_inc(ld, 16)
            for dst, n in ((bg, "gate_b1"), (bu, "up_b1")):
                sp.dma_start(dst[:].rearrange("p e n -> p (e n)"), t[n]).then_inc(ld, 16)
            sp.dma_start(bdn[:], t["down_b1"]).then_inc(ld, 16)
            with sp.Fori(0, NC // 2) as c2:
                for i in range(2):
                    c = 2 * c2 + i
                    sp.wait_ge(ac, START + (c + 1) * ADDS)
                    sp.dma_start(out[c], acc[:, i, :, :]).then_inc(st, 16)
            sp.wait_ge(st, START + 16 * NC)
        LOADED = 16 * 4

        @block.tensor
        def _(e):
            e.wait_ge(ld, LOADED)

            def turn(c, i):
                e.wait_ge(nrm, c + 1)
                e.wait_ge(ini, START + c)
                for k in range(CH):
                    last = e.transpose(ps[0][:, k * P:(k + 1) * P], xf[:, k, :], t["ident"][:])
                last.then_inc(turned, 1)

            def router(c, i):
                e.wait_ge(xts, 2 * c + 1)
                for k in range(CH):
                    last = e.matmul(ps[1][:, k * E1:(k + 1) * E1], xT[:, k * P:(k + 1) * P], rw[:],
                                    start=True, stop=True)
                last.then_inc(rt, 1)

            def turn_weights(c, i):
                e.wait_ge(own, (c + 1) * DVE_STEPS)
                stand_alone(e)
                for k in range(CH):
                    last = e.transpose(ps[6][0:E1, k * P:(k + 1) * P], pw[:, i, k, :], t["ident"][:])
                last.then_inc(pt, 1)

            def bias(c, i):
                e.wait_ge(ptr, c + 1)
                e.wait_ge(xts, 2 * c + 2)
                for k in range(CH):
                    last = e.matmul(ps[0][:, k * D:(k + 1) * D], pT[:, k * P:(k + 1) * P], bdn[:],
                                    start=True, stop=True)
                last.then_inc(db, 1)

            def down(c, x):
                e.wait_ge(hd, START + c * UN + (x + 1) * NF)
                e.wait_ge(ac, START + c * ADDS + x * CH)
                for k in range(CH):
                    for n in range(NF):
                        last = e.matmul(ps[7][:, k * D:(k + 1) * D], hid[:, x % 2, n, k * P:(k + 1) * P],
                                        wdn[:, x, n, :], start=(n == 0), stop=(n == NF - 1))
                last.then_inc(dn, 1)

            def body(c, i, first, last_chunk):
                for x in range(E1):
                    for n in range(NF):
                        u = x * NF + n
                        if u == 0:
                            e.wait_ge(xls, c + 1)
                        e.wait_ge(hd, START + c * UN + max(u - 1, 0))
                        for bank, wt in ((2, gate), (3, upw)):
                            terms = ((0, xh), (0, xl), (1, xh))
                            for j, (part, rows) in enumerate(terms):
                                m = e.matmul(ps[bank + 2 * (u % 2)][:], wt[part][:, x, n * P:(n + 1) * P],
                                             rows[:, i, :], start=(j == 0), stop=(j == len(terms) - 1))
                        m.then_inc(gu, 1)
                        if not last_chunk:
                            if u == 2:
                                turn(c + 1, 1 - i)
                            elif u == 4:
                                router(c + 1, 1 - i)
                            elif u == 14:
                                turn_weights(c + 1, 1 - i)
                            elif u == 15:
                                bias(c + 1, 1 - i)
                    if x:
                        down(c, x - 1)
                    elif not first:
                        down(c - 1, E1 - 1)
                if last_chunk:
                    down(c, E1 - 1)

            for step in (turn, router, turn_weights, bias):
                step(0, 0)
            chunks(e, body)

        @block.scalar
        def _(a):
            a.wait_ge(ld, LOADED)

            def turned_rows(c, i):
                a.wait_ge(turned, START + c + 1)
                a.wait_ge(rt, START + c)
                a.activation(xT[:], ps[0][:], ACT.Copy).then_inc(xts, 1)
                a.activation(xh[:, i, :], ps[0][:], ACT.Copy).then_inc(xts, 1)

            def exponentials(c):
                a.wait_ge(own, c * DVE_STEPS + 2)
                a.activation(prob[:], sc[:], ACT.Exp).then_inc(ex, 1)

            def body(c, i, first, last_chunk):
                for u in range(UN):
                    a.wait_ge(gu, c * UN + u + 1)
                    a.wait_ge(hd, START + c * UN + max(u - 1, 0))
                    a.activation(sil[:, u % 2, :], ps[2 + 2 * (u % 2)][:], ACT.Silu,
                                 bias=bg[:, u // NF, u % NF:u % NF + 1]).then_inc(sl, 1)
                    if not last_chunk:
                        if u == 2:
                            turned_rows(c + 1, 1 - i)
                        elif u == 7:
                            exponentials(c + 1)

            turned_rows(0, 0)
            exponentials(0)
            chunks(a, body)

        @block.vector
        def _(dve):
            dve.wait_ge(ld, LOADED)

            def bc(ap):
                return ap.unsqueeze(2).broadcast_to([P, CH, E1])

            def route(c, i, u, first=False):
                at = {1: 0, 4: 0, 6: 0, 9: 2, 10: 5, 11: 5 + CH, 12: 7 + CH, 13: 8 + 2 * CH}
                s = Steps(dve, own, c * DVE_STEPS + at.get(u, 0), alone=True)
                if u == 1:
                    dve.wait_ge(turned, START + c)
                    normalise_chunk(dve, xf, X, mv, c).then_inc(nrm, 1)
                elif u == 4:
                    dve.wait_ge(xts, 2 * c + 2)
                    dve.tensor_tensor(xl[:, i, :], xT[:], xh[:, i, :].bitcast(F32), ALU.subtract)\
                        .then_inc(xls, 1)
                elif u == 6:
                    dve.wait_ge(rt, START + c + 1)
                    lg = ps[1][:, 0:CH * E1].rearrange("p (k e) -> p k e", k=CH)
                    s.do(dve.reduce_max(mx[:], lg, X_AXIS))
                    s.do(dve.tensor_tensor(sc[:], lg, bc(mx[:]), ALU.subtract))
                elif u == 9:
                    dve.wait_ge(ex, c + 1)
                    s.do(dve.reduce_sum(mx[:], prob[:], X_AXIS))
                    s.do(dve.reciprocal(mx[:], mx[:]))
                    s.do(dve.tensor_tensor(prob[:], prob[:], bc(mx[:]), ALU.mult))
                elif u == 10:
                    for k in range(CH):
                        s.done(dve.max(top[:, k, :], prob[:, k, :]))
                    s.settle()
                elif u == 11:
                    s.do(dve.tensor_tensor(mx[:], top[:, :, 0], top[:, :, 1], ALU.add))
                    s.done(dve.tensor_scalar(mx[:], mx[:], 1e-9, None, ALU.add))
                elif u == 12:
                    s.do(dve.memset(top[:, :, 2:8], 3.0e38))
                    for k in range(CH):
                        s.done(dve.match_replace(rep[:, k, :], top[:, k, :], prob[:, k, :], -3.0e38))
                    s.settle()
                elif u == 13:
                    s.done(dve.tensor_tensor(rep[:], rep[:], prob[:], ALU.not_equal))
                    s.do(dve.reciprocal(mx[:], mx[:]))
                    s.do(dve.tensor_tensor(pw[:, i, :, :], prob[:], rep[:], ALU.mult))
                    s.do(dve.tensor_tensor(pw[:, i, :, :], pw[:, i, :, :], bc(mx[:]), ALU.mult))
                elif u == 14:
                    dve.wait_ge(pt, c + 1)
                    dve.tensor_copy(pT[:], ps[6][0:E1, :]).then_inc(ptr, 1)
                elif u == 15:
                    dve.wait_ge(db, c + 1)
                    if not first:
                        dve.wait_ge(st, START + 16 * (c - 1))
                    dve.tensor_tensor(acc[:, i, :, :], X[:, bass.ds(c * CH, CH), :],
                                      ps[0][:].rearrange("p (k d) -> p k d", k=CH),
                                      ALU.add).then_inc(ini, 1)

            def add_expert(c, i, x):
                dve.wait_ge(dn, c * E1 + x + 1)
                for k in range(CH):
                    if x:
                        dve.wait_ge(ac, START + c * ADDS + (x - 1) * CH + k + 1)
                    else:
                        dve.wait_ge(ini, START + c + 1)
                    dve.scalar_tensor_tensor(out=acc[:, i, k, :], in0=ps[7][:, k * D:(k + 1) * D],
                                             scalar=pw[:, i, k, x:x + 1], in1=acc[:, i, k, :],
                                             op0=ALU.mult, op1=ALU.add).then_inc(ac, 1)

            def body(c, i, first, last_chunk):
                for x in range(E1):
                    for n in range(NF):
                        u = x * NF + n
                        dve.wait_ge(sl, c * UN + u + 1)
                        dve.scalar_tensor_tensor(out=hid[:, x % 2, n, :], in0=ps[3 + 2 * (u % 2)][:],
                                                 scalar=bu[:, x, n:n + 1], in1=sil[:, u % 2, :],
                                                 op0=ALU.add, op1=ALU.mult).then_inc(hd, 1)
                        if not last_chunk:
                            route(c + 1, 1 - i, u)
                    if x:
                        add_expert(c, i, x - 1)
                    elif not first:
                        add_expert(c - 1, 1 - i, E1 - 1)
                if last_chunk:
                    add_expert(c, i, E1 - 1)

            for u in range(UN):
                route(0, 0, u, first=True)
            chunks(dve, body)
def network(nc, t):
    with ExitStack() as ctx:
        def sb(name, shape, dt=F32, c=ctx):
            return c.enter_context(nc.sbuf_tensor(name, shape, dt))

        def sem(name):
            return ctx.enter_context(nc.semaphore(name))

        psum = ctx.enter_context(nc.psum_tensor("psum", [P, 4096], F32))
        ps = [psum[:, i * 512:(i + 1) * 512] for i in range(8)]
        t["tp"] = t["bank01"] = psum[:, 0:1024]
        t["bank23"], t["bank45"], t["tp2"] = psum[:, 1024:2048], psum[:, 2048:3072], psum[:, 3072:4096]
        t["scores"] = psum[:, 0:2048].rearrange("p (a b c) -> p a b c", a=2, b=2)
        ident = sb("ident", [P, P])
        t["X"] = sb("X", [P, NT, D])
        t["mv"] = sb("mv_all", [P, 2, NT])
        t["neg_half"] = sb("neg_half", [P, NT])
        t["stat_sem"], t["keys_in"] = sem("p3_stats"), sem("p4_keys_in")
        consts = sem("constants")
        with nc.Block() as block:
            @block.sync
            def _(sp):
                sp.dma_start(ident[:], t["ident"]).then_inc(consts, 16)
                sp.wait_ge(consts, 16)

            @block.gpsimd
            def _(pool):
                pool.memset(t["neg_half"][:], -0.5)
        t["ident"] = ident
        with ExitStack() as c:
            t["qkv"] = sb("qkv", [P, NT, 3 * D], F32, c)
            t["att"] = t["qkv"][:, :, 0:D]
            with ExitStack() as c2:
                t["gco"] = sb("gco", [P, NT, 2, H0], F32, c2)
                project_batches(nc, t, sem, ps)
                attend(nc, t, sem, ps)
            output_projection(nc, t, sem, ps)
        with ExitStack() as c:
            for n, dt in (("slotv", F32), ("tok", F32), ("full", F32), ("gidx", I32)):
                t[n] = sb(n, [P, E0 // 2], dt, c)
            with ExitStack() as c2:
                t["keys"] = sb("keys", [E0, N_TOK], F32, c2)
                gate_and_shared(nc, t, sem, ps)
                pick_slots(nc, t, sem, ps)
            routed_experts(nc, t, sem, ps)
        t["XO"] = sb("XO", [P, NT, D])
        combine(nc, t, sem, ps)
        linear_attention(nc, t, sem, ps)
        t["w7"] = expert_weights(nc, t, sb, sem)
        feed_forward(nc, t, sem, ps)
        experts_of_two(nc, t, sem, ps)


def constants(np):
    u = np.arange(S, dtype=np.float64) - S // 2
    u2_low = np.mod(u * u, 128)
    one = np.ones(S)
    krows = np.stack([u * u - u2_low, u2_low, u * u - u2_low, u2_low, u, u, -one, -one], -1)
    part = np.arange(P)
    return {
        "ident": np.eye(P, dtype=np.float32),
        "kconst": np.ascontiguousarray(krows.reshape(TB, P, 8).transpose(1, 0, 2).astype(np.float32)),
        "hmask": (part[:, None] // DH0 == np.arange(H0)[None]).astype(np.float32),
        "block32": (part[:, None] // DH1 == part[None] // DH1).astype(np.float32),
        "tokv": (N_TOK - P * np.arange(NT)[None] - part[:, None]).astype(np.float32),
    }


def kernel(**inputs):
    import numpy as np
    import concourse.bacc as bacc
    from concourse.bass_utils import run_bass_kernel_spmd

    a = {k: np.asarray(v) for k, v in inputs.items()}
    l0, f0, l1, f1 = ({k[len(p):]: v for k, v in a.items() if k.startswith(p)}
                      for p in ("L0_attn_", "L0_ffn_", "L1_attn_", "L1_ffn_"))
    arrays = constants(np)
    arrays["x"] = l0["hidden_states"]
    for n in ("wq", "wk", "wv", "wo", "wfq", "wfg", "bq", "bk", "bv", "bo", "bfq", "bfg", "up", "uz"):
        arrays[n] = l0[n]
    arrays["gate_wT"], arrays["gate_b0"] = f0["gate_w"].T, f0["gate_b"]
    arrays["ws1T"], arrays["ws3T"] = f0["ws1"].T, f0["ws3"].T
    arrays["ws2T"] = f0["ws2"].T.reshape(2, I0, D).transpose(1, 0, 2)
    arrays["w1T"] = f0["w1"].transpose(2, 0, 1).reshape(D, E0 * I0)
    arrays["w3T"] = f0["w3"].transpose(2, 0, 1).reshape(D, E0 * I0)
    arrays["w2T"] = f0["w2"].transpose(2, 0, 1).reshape(I0, E0 * D)
    for n in ("wq", "wk", "wv", "wo", "bo"):
        arrays["l1_" + n] = l1[n]
    for n in ("ln1_g", "ln1_b", "ln2_g", "ln2_b", "w_ff1", "b_ff1", "w_ff2", "b_ff2", "w_d", "b_d"):
        arrays[n] = l1[n]
    arrays["router_wT"] = f1["router_w"].T
    arrays["b_ff1"] = l1["b_ff1"].reshape(FF // P, P).T
    for n in ("gate_w", "up_w", "down_w", "down_b"):
        arrays[n + "1"] = f1[n]
    for n in ("gate_b", "up_b"):
        arrays[n + "1"] = f1[n].reshape(E1 * F1 // P, P).T

    nc = bacc.Bacc("TRN2", target_bir_lowering=False, num_devices=1)
    arrays = {f"in_{n}": np.ascontiguousarray(v) for n, v in arrays.items()}
    t = {n[3:]: nc.dram_tensor(n, v.shape, F32, kind="ExternalInput").ap() for n, v in arrays.items()}
    t["out"] = nc.dram_tensor("out", (B, S, D), F32, kind="ExternalOutput").ap()
    t["rows"] = nc.dram_tensor("token_rows", (N_TOK, ROW), F32, kind="Internal").ap()
    t["ybuf"] = nc.dram_tensor("pick_rows", (N_TOK * K0, D), F32, kind="Internal").ap()
    network(nc, t)
    r = run_bass_kernel_spmd(nc, [arrays], core_ids=[0])
    return r.results[0]["out"]
```

```python
from contextlib import ExitStack

import concourse.bass as bass
from concourse import mybir

F32 = mybir.dt.float32
F32R = mybir.dt.float32r
BF16 = mybir.dt.bfloat16
I32 = mybir.dt.int32
U32 = mybir.dt.uint32
ALU = mybir.AluOpType
ACT = mybir.ActivationFunctionType
X_AXIS = mybir.AxisListType.X

P = 128
D = 128
B, S = 4, 1024
NT = B * S // P
TB = S // P
H0, DH0 = 16, 8
GH = 4
NG = H0 // GH
R = 32
EPS = 1e-5
START = 1


def stand_alone(eng):
    eng.nop(nofuse=True)


class Steps:

    def __init__(self, eng, sem, base=0, alone=False):
        self.eng, self.sem, self.base, self.alone, self.n = eng, sem, base, alone, 0

    def done(self, ins):
        ins.then_inc(self.sem, 1)
        self.n += 1

    def settle(self):
        self.eng.wait_ge(self.sem, self.base + self.n)
        if self.alone:
            stand_alone(self.eng)

    def do(self, ins):
        self.done(ins)
        self.settle()
def project_batches(nc, t, sem, ps):
    ctx = ExitStack()
    with ctx:
        def sb(name, shape, dt=F32):
            return ctx.enter_context(nc.sbuf_tensor(name, shape, dt))

        wqkv = sb("wqkv", [P, 3 * D])
        wfq, wfg = sb("wfq", [P, D]), sb("wfg", [P, D])
        cols = sb("cols", [P, 5])
        biases = sb("biases", [P, 3 * D])
        hmask = sb("hmask", [P, H0])
        upz = sb("upz", [P, 2, H0])
        stats = sb("stats", [P, TB, 6])
        mv = sb("mv", [P, TB, 2])
        rstd = sb("rstd", [P, TB])
        half = sb("half", [P, TB])
        xn = sb("xn", [P, TB, D])
        xT = sb("xT", [P, S])
        qT = sb("qT", [P, S])
        cT = sb("cT", [P, S])
        glo = sb("glo", [P, 2])
        cbias = sb("cbias", [P, 3])
        ez = sb("ez", [P, TB, 2, H0])
        g1 = sb("g1", [P, TB, 2, H0])
        g2 = sb("g2", [P, TB, H0])
        g3 = sb("g3", [P, TB, H0])
        X, qkv, gco = t["X"], t["qkv"], t["gco"]

        first_rows, more_rows = sem("p1_first_rows"), sem("p1_more_rows")
        loaded, st_own, own, rst, trd, turned, xts, act, pe = (sem("p1_" + n) for n in (
            "loaded", "stat_steps", "dve_steps", "rstd_ready", "xn_ready", "xn_turned", "xn_copied",
            "act_steps", "pe_steps"))
        tok, evac = sem("p1_qkv_ready"), sem("p1_qkv_taken")
        halfs = sem("p1_half_ready")
        block = ctx.enter_context(nc.Block())

        @block.sync
        def _(sp):
            for counter in t["attention_counters"].values():
                sp.sem_inc(counter, START)
            def rows(b, counter):
                sp.dma_start(X[:, b * TB:(b + 1) * TB, :],
                             t["x"][b].rearrange("(t p) d -> p t d", p=P)).then_inc(counter, 16)
            rows(0, first_rows)
            for i, n in enumerate(("wq", "wk", "wv")):
                sp.dma_start(wqkv[:, i * D:(i + 1) * D], t[n]).then_inc(loaded, 16)
            sp.dma_start(wfq[:], t["wfq"]).then_inc(loaded, 16)
            sp.dma_start(wfg[:], t["wfg"]).then_inc(loaded, 16)
            sp.dma_start(hmask[:], t["hmask"]).then_inc(loaded, 16)
            sp.dma_start(t["kconst_sb"][:], t["kconst"]).then_inc(loaded, 16)
            for i, n in enumerate(("bq", "bk", "bv")):
                sp.dma_start(biases[:, i * D:(i + 1) * D],
                             t[n].partition_broadcast(P)).then_inc(loaded, 16)
            for i, n in enumerate(("bq", "bfq", "bfg", "up", "uz")):
                v = t[n] if n[0] == "b" else t[n].rearrange("h a d -> (h a d)")
                sp.dma_start(cols[:, i:i + 1], v.rearrange("(p a) -> p a", a=1)).then_inc(loaded, 16)
            for b in range(1, B):
                rows(b, more_rows)
        N_LOADED = 16 * (3 + 3 + 1 + 3 + 5)

        STAT_STEPS, DVE_STEPS = TB + 2, 9
        ACT_STEPS = 2 + 2 + 1
        PE_STEPS = 4

        def batches(eng, body):
            body(0, True, False)
            with eng.Fori(1, B - 1) as b:
                body(b, False, False)
            body(B - 1, False, True)

        @block.gpsimd
        def _(pool):
            pool.memset(half[:], -0.5).then_inc(halfs, 1)
            pool.wait_ge(halfs, 1)
            with pool.Fori(0, B) as b:
                pool.wait_ge(st_own, (b + 1) * STAT_STEPS)
                pool.tensor_tensor(rstd[:], rstd[:], half[:], ALU.pow).then_inc(rst, 1)
            for buf, value in t["cleared"]:
                pool.memset(buf, value).then_inc(halfs, 1)
            pool.wait_ge(halfs, 1 + len(t["cleared"]))
            pool.wait_ge(loaded, N_LOADED)
            for v in t["vaug"]:
                pool.memset(v[:, :, :, DH0:DH0 + 1], 1.0).then_inc(halfs, 1)
            for h in range(GH):
                pool.tensor_copy(t["krow"][:, :, h, 24:32], t["kconst_sb"][:]).then_inc(halfs, 1)
            pool.wait_ge(halfs, 1 + len(t["cleared"]) + NG + GH)
            pool.wait_ge(evac, TB)
            pool.wait_ge(own, 3 + DVE_STEPS)
            build_rows(pool, t, slice(0, TB), 0, Steps(pool, t["rows_steps"]))

        @block.vector
        def _(dve):
            def statistics(b):
                s = Steps(dve, st_own, b * STAT_STEPS, alone=True)
                for i in range(TB):
                    s.done(dve.bn_stats(stats[:, i, :], X[:, b * TB + i, :]))
                s.settle()
                for i in range(TB):
                    last = dve.bn_aggr(mv[:, i, :], stats[:, i, :])
                s.do(last)
                s.do(dve.tensor_scalar(rstd[:], mv[:, :, 1], EPS, None, ALU.add))
                assert s.n == STAT_STEPS

            def normalise(b):
                dve.wait_ge(rst, b + 1)
                for i in range(TB):
                    last = dve.tensor_scalar(xn[:, i, :], X[:, b * TB + i, :], mv[:, i, 0:1],
                                             rstd[:, i:i + 1], ALU.subtract, ALU.mult)
                last.then_inc(trd, 1)

            def body(b, first, last):
                s = Steps(dve, own, 3 + b * DVE_STEPS, alone=True)
                dve.wait_ge(act, b * ACT_STEPS + 2)
                s.do(dve.reduce_sum(glo[:, 0:1], qT[:], X_AXIS))
                s.do(dve.tensor_scalar(glo[:, 1:2], glo[:, 0:1], 1.0 / S, None, ALU.mult))
                if not last:
                    statistics(b + 1)
                dve.wait_ge(pe, b * PE_STEPS + 2)
                s.do(dve.tensor_tensor(cbias[:, 1:2], ps[6][:, 0:1], cbias[:, 0:1], ALU.add))
                for i in range(TB):
                    dve.wait_ge(tok, b * TB + i + 1)
                    dve.tensor_tensor(qkv[:, b * TB + i, :], ps[4 + i % 2][:, 0:3 * D], biases[:],
                                      ALU.add).then_inc(evac, 1)
                if not last:
                    normalise(b + 1)
                dve.wait_ge(act, (b + 1) * ACT_STEPS)
                s.do(dve.tensor_scalar(g1[:], ez[:], 1.0, None, ALU.add))
                s.do(dve.reciprocal(g2[:], g1[:, :, 0, :]))
                s.do(dve.tensor_scalar(g2[:], g2[:], float(S), -float(S // 2), ALU.mult, ALU.add))
                s.do(dve.tensor_tensor(g3[:], g1[:, :, 1, :], g1[:, :, 1, :], ALU.mult))
                s.done(dve.tensor_scalar(gco[:, bass.ds(b * TB, TB), 0, :], g3[:], -2.0 / S ** 2, None,
                                         ALU.mult))
                s.do(dve.scalar_tensor_tensor(out=gco[:, bass.ds(b * TB, TB), 1, :], in0=g3[:],
                                              scalar=4.0 / S ** 2, in1=g2[:], op0=ALU.mult, op1=ALU.mult))
                assert s.n == DVE_STEPS, s.n

            dve.wait_ge(first_rows, 16)
            statistics(0)
            dve.wait_ge(loaded, N_LOADED)
            s0 = Steps(dve, own)
            for i in range(2):
                s0.done(dve.tensor_scalar(upz[:, i, :], hmask[:], cols[:, 3 + i:4 + i], None, ALU.mult))
            s0.do(dve.tensor_tensor(cbias[:, 0:1], cols[:, 1:2], cols[:, 2:3], ALU.add))
            normalise(0)
            dve.wait_ge(more_rows, 16 * (B - 1))
            batches(dve, body)

        @block.scalar
        def _(a):
            a.wait_ge(loaded, N_LOADED)

            def turned_rows(b):
                a.wait_ge(turned, b + 1)
                a.activation(xT[:], t["tp"][:], ACT.Copy).then_inc(xts, 1)

            def body(b, first, last):
                s = Steps(a, act, b * ACT_STEPS)
                a.wait_ge(pe, b * PE_STEPS + 1)
                for c in range(2):
                    s.done(a.activation(qT[:, c * 512:(c + 1) * 512], ps[2 + c][:], ACT.Identity,
                                        bias=cols[:, 0:1]))
                a.wait_ge(pe, b * PE_STEPS + 3)
                a.wait_ge(own, 3 + b * DVE_STEPS + 3)
                for c in range(2):
                    s.done(a.activation(cT[:, c * 512:(c + 1) * 512], ps[2 + c][:], ACT.Tanh,
                                        bias=cbias[:, 1:2]))
                a.wait_ge(own, 3 + b * DVE_STEPS)
                a.wait_ge(pe, b * PE_STEPS + 4)
                s.done(a.activation(ez[:].rearrange("p t a h -> p (t a h)"), ps[7][:, 0:2 * H0 * TB],
                                    ACT.Exp, scale=-1.0))
                assert s.n == ACT_STEPS
                if not last:
                    turned_rows(b + 1)

            turned_rows(0)
            batches(a, body)

        @block.tensor
        def _(e):
            e.wait_ge(loaded, N_LOADED)

            def turn(b):
                e.wait_ge(trd, b + 1)
                for i in range(TB):
                    last = e.transpose(t["tp"][:, i * P:(i + 1) * P], xn[:, i, :], t["ident"][:])
                last.then_inc(turned, 1)

            def tokens(b, tiles, first):
                for i in tiles:
                    if i >= 2 or not first:
                        e.wait_ge(evac, b * TB + i - 1)
                    e.matmul(ps[4 + i % 2][:, 0:3 * D], xT[:, i * P:(i + 1) * P], wqkv[:],
                             start=True, stop=True).then_inc(tok, 1)

            def body(b, first, last_batch):
                e.wait_ge(xts, b + 1)
                for c in range(2):
                    last = e.matmul(ps[2 + c][:], wqkv[:, 0:D], xT[:, c * 512:(c + 1) * 512],
                                    start=True, stop=True)
                last.then_inc(pe, 1)
                tokens(b, range(2), first)
                e.wait_ge(own, 3 + b * DVE_STEPS + 2)
                e.matmul(ps[6][:, 0:1], wfg[:], glo[:, 1:2], start=True, stop=True).then_inc(pe, 1)
                for c in range(2):
                    last = e.matmul(ps[2 + c][:], wfq[:], qT[:, c * 512:(c + 1) * 512],
                                    start=True, stop=True)
                last.then_inc(pe, 1)
                tokens(b, range(2, 6), first)
                e.wait_ge(act, b * ACT_STEPS + 4)
                for i in range(TB):
                    last = e.matmul(ps[7][:, i * 2 * H0:(i + 1) * 2 * H0], cT[:, i * P:(i + 1) * P],
                                    upz[:].rearrange("p a h -> p (a h)"), start=True, stop=True)
                last.then_inc(pe, 1)
                tokens(b, range(6, TB), first)
                if not last_batch:
                    turn(b + 1)

            turn(0)
            batches(e, body)


ATTENTION_COUNTERS = ("probs_ready", "pv_done", "half_copied", "tp_full", "tp_free", "operands_copied",
                      "keys_spread")
POOL_STEPS = 14


def build_rows(pool, t, tiles, g, s):
    f32 = lambda ap: ap.bitcast(F32)
    qkv, gco, scaled = t["qkv"], t["gco"], t["scaled"]
    q, k, v = t["qrow"], t["krow"], t["vaug"][g]
    part = lambda w: qkv[:, tiles, w * D + g * R:w * D + (g + 1) * R].rearrange("p t (h d) -> p t h d", h=GH)
    co = lambda w: gco[:, tiles, w, g * GH:(g + 1) * GH]
    tmp = scaled[:].rearrange("p t (h d) -> p t h d", h=GH)
    s.done(pool.tensor_tensor(scaled[:], qkv[:, tiles, g * R:(g + 1) * R],
                              t["qscale"][:].unsqueeze(2).broadcast_to([P, TB, R]), ALU.mult))
    s.done(pool.tensor_copy(k[:, :, :, 0:8], part(1)))
    s.done(pool.tensor_copy(q[:, :, :, 24], co(0)))
    s.done(pool.tensor_copy(q[:, :, :, 28], co(1)))
    s.done(pool.tensor_copy(v[:, :, :, 0:DH0], part(2)))
    s.settle()
    s.done(pool.tensor_copy(q[:, :, :, 0:8], tmp))
    s.done(pool.tensor_copy(k[:, :, :, 16:24], f32(k[:, :, :, 0:8])))
    s.done(pool.tensor_tensor(k[:, :, :, 8:16], part(1), f32(k[:, :, :, 0:8]), ALU.subtract))
    s.done(pool.tensor_copy(q[:, :, :, 25], f32(q[:, :, :, 24])))
    s.done(pool.tensor_tensor(q[:, :, :, 26], co(0), f32(q[:, :, :, 24]), ALU.subtract))
    s.settle()
    s.done(pool.tensor_copy(q[:, :, :, 27], f32(q[:, :, :, 26])))
    s.done(pool.tensor_tensor(q[:, :, :, 29], co(1), f32(q[:, :, :, 28]), ALU.subtract))
    s.done(pool.tensor_copy(q[:, :, :, 8:16], f32(q[:, :, :, 0:8])))
    s.done(pool.tensor_tensor(q[:, :, :, 16:24], tmp, f32(q[:, :, :, 0:8]), ALU.subtract))
    assert s.n == POOL_STEPS, s.n


def attention_buffers(t, sb, sem):
    f32 = lambda ap: ap.bitcast(F32)
    t["attention_counters"] = {n: sem("p2_" + n) for n in ATTENTION_COUNTERS}
    t["qrow"] = sb("qrow", [P, TB, GH, R], F32R)
    t["krow"] = sb("krow", [P, TB, GH, R], F32R)
    t["kconst_sb"] = sb("kconst", [P, TB, 8])
    t["scaled"] = sb("scaled", [P, TB, R])
    t["vaug"] = [sb(f"vaug{i}", [P, TB, GH, R]) for i in range(NG)]
    t["kT"] = [sb(f"akT{i}", [P, GH, S], F32R) for i in range(NG)]
    t["mrow"] = sb("mrow", [P, TB, GH, R], F32R)
    t["zeros"] = sb("zeros", [P, 512])
    t["qscale"] = sb("qscale", [P, TB])
    t["cleared"] = [(f32(t["qrow"][:]), 0.0), (t["qscale"][:], DH0 ** -0.5), (f32(t["mrow"][:]), 0.0),
                    (t["zeros"][:], 0.0), *((v[:], 0.0) for v in t["vaug"]),
                    *((f32(k[:]), 0.0) for k in t["kT"])]


def attend(nc, t, sem, ps):
    ctx = ExitStack()
    with ctx:
        def sb(name, shape, dt=F32):
            return ctx.enter_context(nc.sbuf_tensor(name, shape, dt))

        STEPS = 16
        BS = NG * STEPS
        QH = S // 2
        NB = 3
        qT = [sb(f"aqT{i}", [P, S], F32R) for i in range(NG)]
        kstage = sb("kstage", [P, 2, 512])
        probs = sb("probs", [P, 4, 2, QH])
        mx, rowmax = sb("mx", [P, TB, GH, 2]), sb("rowmax", [P, TB, GH])
        ctxT = [sb(f"ctxT{i}", [P, QH]) for i in range(2)]
        rden = sb("rden", [P, 2, 4, GH])
        att = t["att"]
        qrow, krow, vaug, kT, mrow, zeros = (t[n] for n in ("qrow", "krow", "vaug", "kT", "mrow", "zeros"))
        pool_own = t["rows_steps"]
        scores, ctxp, tp = t["scores"], ps[4], [ps[5], ps[6], ps[7]]
        f32 = lambda ap: ap.bitcast(F32)

        s_ready, dve_own, dve_c, zeroed = (sem("p2_" + n) for n in (
            "scores_ready", "dve_steps", "den_ready", "rows_zeroed"))
        p_ready, pv_done, half_copied, tp_full, tp_free, qk_copied, k_spread = (
            t["attention_counters"][n] for n in ATTENTION_COUNTERS)
        block = ctx.enter_context(nc.Block())

        def halves(at, kind, u, apart=0):
            return [(at + c * apart, kind, u, c) for c in range(2)]

        def maxima(at, u):
            return [(at + (2 * j + c) * 0.23, "X", u, (j // TB, j % TB, c))
                    for j in range(GH * TB) for c in range(2)]\
                + halves(at + 14.9, "M", u)

        FIRST = sorted(halves(0, "Q", 0) + halves(0, "K", 0) + maxima(0.1, 0) + halves(8.2, "Q", 1, 1)
                       + halves(10.2, "K", 1, 1), key=lambda x: x[0])

        def batch_events(last):
            out = []
            for g in range(NG):
                k = g * STEPS
                if not (last and g + 1 == NG):
                    out += maxima(k + 0.1, g + 1)
                if not (last and g + 2 >= NG):
                    out += halves(k + 4.2, "Q", g + 2, 1) + halves(k + 6.2, "K", g + 2, 1)
                if g:
                    out.append((k + 3.3, "C", 2 * g - 1, None))
                out.append((k + 11.3, "C", 2 * g, None))
            return sorted(out, key=lambda x: x[0]) + [(BS + 1, "C", 2 * NG - 1, None)]

        by_dve = lambda events: sum(x[1] not in "QK" for x in events)
        NF, NE = len(FIRST), len(batch_events(False))
        NFD, NED = by_dve(FIRST), by_dve(batch_events(False))
        assert NE % NB == 0

        class Events:

            def __init__(self, events, b=None):
                self.events, self.follows = events, b is not None
                self.base = 0 if b is None else NF + b * NE
                self.dve_base = 0 if b is None else NFD + b * NED

            def passed(self, n):
                return self.base + n

            def bank(self, n):
                return tp[(n + (NF if self.follows else 0)) % NB]

            def emptied(self, n):
                return START + self.dve_base + by_dve(self.events[:n])

        @block.sync
        def _(sp):
            rows = t["ybuf"].rearrange("(p n) d -> p (n d)", p=P)
            n = rows.shape[1] // zeros.shape[1]
            for i in range(n):
                sp.dma_start(rows[:, bass.ts(i, zeros.shape[1])], zeros[:]).then_inc(zeroed, 16)
            sp.wait_ge(zeroed, 16 * n)

        M_STEPS = 3

        @block.gpsimd
        def _(pool):
            def build(b, u):
                unit = b * NG + u
                s = Steps(pool, pool_own, unit * POOL_STEPS, alone=True)
                s.settle()
                if u == 1:
                    pool.wait_ge(qk_copied, START + 4)
                if u >= 2:
                    pool.wait_ge(dve_own, M_STEPS * (unit - 1))
                    pool.wait_ge(pv_done, START + (b * NG + max(u - NG + 1, 0)) * STEPS)
                    stand_alone(pool)
                build_rows(pool, t, bass.ds((b + u // NG) * TB, TB), u % NG, s)

            def spread(b, u):
                pool.wait_ge(pool_own, (b * NG + u + 1) * POOL_STEPS)
                s = Steps(pool, k_spread, START + (b * NG + u) * 2 * GH, alone=True)
                for c in range(2):
                    pool.wait_ge(qk_copied, START + (b * NG + u) * 4 + 2 + c + 1)
                    stand_alone(pool)
                    for h in range(GH):
                        r = slice(h * R, (h + 1) * R)
                        s.done(pool.tensor_copy(kT[u % NG][r, h, c * 512:(c + 1) * 512], kstage[r, c, :]))
                    s.settle()

            build(0, 1)
            spread(0, 1)
            with pool.Fori(0, B - 1) as b:
                for u in range(2, NG + 2):
                    build(b, u)
                    spread(b, u)
            for u in range(2, NG):
                build(B - 1, u)
                spread(B - 1, u)

        @block.tensor
        def _(e):
            def turned(b, kind, u, c):
                return START + (b * NG + u) * 4 + (2 if kind == "K" else 0) + c + 1

            def event(b, ev, n):
                _, kind, u, at = ev.events[n]
                bank = ev.bank(n)
                if n < NB:
                    if ev.follows:
                        e.wait_ge(tp_free, ev.emptied(0))
                        e.wait_ge(qk_copied, START + (b * NG + 2) * 4)
                elif ev.events[n - NB][1] in "QK":
                    e.wait_ge(qk_copied, turned(b, *ev.events[n - NB][1:]))
                else:
                    e.wait_ge(tp_free, ev.emptied(n - NB + 1))
                if kind == "C":
                    e.wait_ge(half_copied, START + b * 2 * NG + u + 1)
                    for i in range(4):
                        last = e.transpose(bank[:, i * P:(i + 1) * P], ctxT[u % 2][:, i * P:(i + 1) * P],
                                           t["ident"][:])
                elif kind == "X":
                    h, i, c = at
                    if (h, i, c) == (0, 0, 0):
                        e.wait_ge(qk_copied, START + (b * NG + u) * 4 + 2)
                        e.wait_ge(k_spread, START + (b * NG + u + 1) * 2 * GH)
                    last = e.matmul(bank[:], qT[u % NG][:, i * P:(i + 1) * P],
                                    kT[u % NG][:, h, c * 512:(c + 1) * 512], start=True, stop=True)
                else:
                    if kind == "M":
                        e.wait_ge(dve_own, (b * NG + u + 1) * M_STEPS)
                    else:
                        e.wait_ge(pool_own, (b * NG + u + 1) * POOL_STEPS)
                    src = {"Q": qrow, "K": krow, "M": mrow}[kind]
                    for i in range(4):
                        last = e.transpose(bank[:, i * P:(i + 1) * P],
                                           f32(src[:, 4 * at + i, :, :]).rearrange("p h r -> p (h r)"),
                                           t["ident"][:])
                last.then_inc(tp_full, 1)

            def score_step(b, n):
                g, hf, kt, pair = n // 32, n // 16 % 2, n // 2 % 8, n % 2
                if n:
                    e.wait_ge(p_ready, START + b * 2 * BS + max(n - 1, 0))
                for j in range(2):
                    h = 2 * pair + j
                    last = e.matmul(scores[:, n % 2, j, :],
                                    kT[g][:, h, kt * P:(kt + 1) * P], qT[g][:, hf * QH:(hf + 1) * QH],
                                    start=True, stop=True)
                last.then_inc(s_ready, 1)

            def values_step(b, k):
                g, hf, kt = k // STEPS, k // 8 % 2, k % 8
                e.wait_ge(p_ready, START + b * 2 * BS + 2 * k + 2)
                if kt == 0:
                    e.wait_ge(half_copied, START + b * 2 * NG + 2 * g + hf)
                for h in range(GH):
                    last = e.matmul(ctxp[h * R:(h + 1) * R, :], vaug[g][:, kt, h, :],
                                    probs[:, (2 * k + h // 2) % 4, h % 2, :],
                                    start=(kt == 0), stop=(kt == 7))
                last.then_inc(pv_done, 1)

            def batch(b, last):
                ev = Events(batch_events(last), b)
                seen = [0]

                def events_to(place):
                    while seen[0] < len(ev.events) and ev.events[seen[0]][0] < place:
                        event(b, ev, seen[0])
                        seen[0] += 1

                for k in range(BS + 1):
                    if k < BS:
                        if k % STEPS == 0:
                            m = [x[1:3] for x in ev.events].index(("M", k // STEPS)) + 2 if k else 0
                            e.wait_ge(tp_free, ev.emptied(m))
                        score_step(b, 2 * k)
                        events_to(k + 0.25)
                        score_step(b, 2 * k + 1)
                    events_to(k + 0.6)
                    if k:
                        values_step(b, k - 1)
                    events_to(k + 1)
                events_to(BS + 2)

            first = Events(FIRST)
            for n in range(NF):
                event(0, first, n)
            with e.Fori(0, B - 1) as b:
                batch(b, False)
            batch(B - 1, True)

        @block.scalar
        def _(a):
            def operands(b, ev, n):
                _, kind, u, c = ev.events[n]
                bank, half = ev.bank(n), slice(c * 512, (c + 1) * 512)
                a.wait_ge(tp_full, START + ev.passed(n) + 1)
                if kind == "Q":
                    last = a.activation(qT[u % NG][:, half], bank[:], ACT.Copy)
                else:
                    if not ev.follows and u == 0:
                        for h in range(GH):
                            r = slice(h * R, (h + 1) * R)
                            a.activation(kT[0][r, h, half], bank[r, :], ACT.Copy).then_inc(k_spread, 1)
                    a.wait_ge(k_spread, START + (b * NG + u) * 2 * GH)
                    last = a.activation(kstage[:, c, :], bank[:], ACT.Copy)
                last.then_inc(qk_copied, 1)

            def context(b, u):
                a.wait_ge(pv_done, START + b * BS + 8 * (u + 1))
                a.activation(ctxT[u % 2][:], ctxp[:], ACT.Copy).then_inc(half_copied, 1)

            def batch(b, last):
                ev = Events(batch_events(last), b)
                turns = [n for n, x in enumerate(ev.events) if x[1] in "QK"]
                for n in range(2 * BS):
                    a.wait_ge(s_ready, b * 2 * BS + n + 1)
                    if n % 2 == 0:
                        a.wait_ge(pv_done, START + b * BS + max(n // 2 - 1, 0))
                    a.activation(probs[:, n % 4, :, :], scores[:, n % 2, :, :], ACT.Exp)\
                        .then_inc(p_ready, 1)
                    while turns and ev.events[turns[0]][0] < n // 2 + (1 if n % 2 else 0.25):
                        operands(b, ev, turns.pop(0))
                    if n % 2 and n // 2 % 8 == 0 and n > 1:
                        context(b, n // 16 - 1)
                context(b, 2 * NG - 1)

            first = Events(FIRST)
            for n, x in enumerate(FIRST):
                if x[1] in "QK":
                    operands(0, first, n)
            with a.Fori(0, B - 1) as b:
                batch(b, False)
            batch(B - 1, True)

        @block.vector
        def _(dve):
            def event(b, ev, n):
                _, kind, u, at = ev.events[n]
                bank = ev.bank(n)
                if kind in "QK":
                    return
                if kind == "M":
                    if at == 0:
                        dve.wait_ge(tp_free, ev.emptied(n))
                        s = Steps(dve, dve_own, (b * NG + u) * M_STEPS)
                        s.do(dve.tensor_tensor(rowmax[:], mx[:, :, :, 0], mx[:, :, :, 1], ALU.max))
                        s.do(dve.tensor_copy(mrow[:, :, :, 30], rowmax[:]))
                        s.do(dve.tensor_tensor(mrow[:, :, :, 31], rowmax[:], f32(mrow[:, :, :, 30]),
                                               ALU.subtract))
                        assert s.n == M_STEPS
                dve.wait_ge(tp_full, START + ev.passed(n) + 1)
                if kind == "C":
                    v = bank[:].rearrange("p (i h r) -> p i h r", i=4, h=GH)
                    dve.reciprocal(rden[:, u % 2], v[:, :, :, DH0]).then_inc(dve_c, 1)
                    dve.wait_ge(dve_c, b * 2 * NG + u + 1)
                    g, hf = u // 2, u % 2
                    o = att[:, bass.ds(b * TB + 4 * hf, 4), g * R:(g + 1) * R]\
                        .rearrange("p i (h d) -> p i h d", h=GH)
                    dve.tensor_tensor(o, v[:, :, :, 0:DH0],
                                      rden[:, u % 2].unsqueeze(3).broadcast_to([P, 4, GH, DH0]),
                                      ALU.mult).then_inc(tp_free, 1)
                elif kind == "X":
                    h, i, c = at
                    dve.reduce_max(mx[:, i, h, c:c + 1], bank[:], X_AXIS).then_inc(tp_free, 1)
                else:
                    q = qT[u % NG][:, at * 512:(at + 1) * 512]
                    dve.tensor_tensor(q, f32(q), bank[:], ALU.add).then_inc(tp_free, 1)

            def batch(b, last):
                ev = Events(batch_events(last), b)
                for n in range(len(ev.events)):
                    event(b, ev, n)

            first = Events(FIRST)
            for n in range(NF):
                event(0, first, n)
            with dve.Fori(0, B - 1) as b:
                batch(b, False)
            batch(B - 1, True)
CH = 4
NC = NT // CH
E0, K0, CAP, I0 = 64, 6, 64, 88
SI = 2 * I0
ROW = 2 * D
N_TOK = B * S


def chunks(eng, body):
    body(0, 0, True, False)
    with eng.Fori(0, NC // 2 - 1) as c2:
        for i in range(2):
            body(2 * c2 + 1 + i, (1 + i) % 2, False, False)
    body(NC - 1, 1, False, True)


def normalise_chunk(dve, out, src, mv, c):
    for k in range(CH):
        tile = c * CH + k
        last = dve.tensor_scalar(out[:, k, :], src[:, tile, :], mv[:, 0, bass.ds(tile, 1)],
                                 mv[:, 1, bass.ds(tile, 1)], ALU.subtract, ALU.mult)
    return last


def finish_stats(dve, s, stats, mv, tmp, n):
    s.done(dve.tensor_tensor(mv[:, 0, :], stats[:, :, 1], stats[:, :, 4], ALU.add))
    s.done(dve.tensor_tensor(tmp[:, 0, :], stats[:, :, 1], stats[:, :, 4], ALU.subtract))
    s.do(dve.tensor_tensor(tmp[:, 1, :], stats[:, :, 2], stats[:, :, 5], ALU.add))
    s.done(dve.tensor_scalar(mv[:, 0, :], mv[:, 0, :], 0.5, None, ALU.mult))
    s.done(dve.tensor_scalar(tmp[:, 1, :], tmp[:, 1, :], 1.0 / D, EPS, ALU.mult, ALU.add))
    s.do(dve.scalar_tensor_tensor(out=tmp[:, 0, :], in0=tmp[:, 0, :], scalar=0.25, in1=tmp[:, 0, :],
                                  op0=ALU.mult, op1=ALU.mult))
    s.do(dve.tensor_tensor(mv[:, 1, :], tmp[:, 0, :], tmp[:, 1, :], ALU.add))


STATS_STEPS = 7


def output_projection(nc, t, sem, ps):
    ctx = ExitStack()
    with ctx:
        def sb(name, shape, dt=F32):
            return ctx.enter_context(nc.sbuf_tensor(name, shape, dt))

        wo, bo = sb("wo0", [P, D]), sb("bo0", [P, D])
        ctile = sb("ctile", [P, 2, CH, D])
        cT = sb("ctxTt", [P, 2, CH * P])
        stats, tmp = sb("stats3", [P, NT, 6]), sb("tmp3", [P, 2, NT])
        X, att, mv = t["X"], t["att"], t["mv"]
        loaded, biased, taken, turned, turned_sb, proj, added, own, varr = (sem("p3_" + n) for n in (
            "loaded", "x_biased", "ctx_taken", "turned", "turned_copied", "projected", "added",
            "dve_steps", "var_ready"))
        block = ctx.enter_context(nc.Block())

        @block.sync
        def _(sp):
            for counter in (turned, added):
                sp.sem_inc(counter, START)
            sp.dma_start(wo[:], t["wo"]).then_inc(loaded, 16)
            sp.dma_start(bo[:], t["bo"].partition_broadcast(P)).then_inc(loaded, 16)
            load_weights(sp, t["w4"])

        @block.gpsimd
        def _(pool):
            pool.wait_ge(loaded, 32)
            with pool.Fori(0, NC) as c:
                pool.tensor_tensor(X[:, bass.ds(c * CH, CH), :], X[:, bass.ds(c * CH, CH), :],
                                   bo[:].unsqueeze(1).broadcast_to([P, CH, D]), ALU.add).then_inc(biased, 1)
            pool.wait_ge(own, STATS_STEPS)
            pool.tensor_tensor(mv[:, 1, :], mv[:, 1, :], t["neg_half"][:, 0:NT], ALU.pow).then_inc(varr, 1)
            pool.wait_ge(varr, 1)

        @block.scalar
        def _(a):
            def take(c, i):
                a.activation(ctile[:, i, :, :], att[:, bass.ds(c * CH, CH), :], ACT.Copy).then_inc(taken, 1)

            def body(c, i, first, last):
                if not last:
                    a.wait_ge(turned, START + c)
                    take(c + 1, 1 - i)
                a.wait_ge(turned, START + c + 1)
                a.activation(cT[:, i, :], ps[i][:], ACT.Copy).then_inc(turned_sb, 1)

            take(0, 0)
            chunks(a, body)

        @block.tensor
        def _(e):
            e.wait_ge(loaded, 32)

            def turn(c, i):
                e.wait_ge(taken, c + 1)
                for k in range(CH):
                    last = e.transpose(ps[i][:, k * P:(k + 1) * P], ctile[:, i, k, :], t["ident"][:])
                last.then_inc(turned, 1)

            def body(c, i, first, last_chunk):
                if not last_chunk:
                    turn(c + 1, 1 - i)
                e.wait_ge(turned_sb, c + 1)
                if not first:
                    e.wait_ge(added, START + c - 1)
                for k in range(CH):
                    last = e.matmul(ps[2 + i][:, k * D:(k + 1) * D], cT[:, i, k * P:(k + 1) * P], wo[:],
                                    start=True, stop=True)
                last.then_inc(proj, 1)

            turn(0, 0)
            chunks(e, body)

        @block.vector
        def _(dve):
            def statistics(c):
                for k in range(CH):
                    dve.bn_stats(stats[:, c * CH + k, :], X[:, c * CH + k, :]).then_inc(t["stat_sem"], 1)

            def body(c, i, first, last):
                dve.wait_ge(proj, c + 1)
                dve.wait_ge(biased, c + 1)
                xc = X[:, bass.ds(c * CH, CH), :]
                dve.tensor_tensor(xc, xc, ps[2 + i][:].rearrange("p (k d) -> p k d", k=CH),
                                  ALU.add).then_inc(added, 1)
                if not first:
                    dve.wait_ge(added, START + c)
                    statistics(c - 1)

            chunks(dve, body)
            dve.wait_ge(added, START + NC)
            statistics(NC - 1)
            dve.wait_ge(t["stat_sem"], NT)
            finish_stats(dve, Steps(dve, own), stats, mv, tmp, NT)


def load_weights(sp, w):
    for dst, src in w["transfers"]:
        sp.dma_start(dst, src).then_inc(w["loaded"], 16)


def gate_weights(t, sb, sem):
    shapes = {"gw": [P, E0], "gb": [P, E0], "ws1": [P, SI], "ws3": [P, SI], "ws2": [I0, 2, D], "tokv": [P, NT]}
    w = {n: sb(n, shape) for n, shape in shapes.items()}
    w["loaded"] = sem("p4_loaded")
    w["transfers"] = [(w["gw"][:], t["gate_wT"]), (w["ws1"][:], t["ws1T"]), (w["ws3"][:], t["ws3T"]),
                      (w["ws2"][:], t["ws2T"]), (w["tokv"][:], t["tokv"]),
                      (w["gb"][:], t["gate_b0"].partition_broadcast(P))]
    return w


def gate_and_shared(nc, t, sem, ps):
    ctx = ExitStack()
    with ctx:
        def sb(name, shape, dt=F32):
            return ctx.enter_context(nc.sbuf_tensor(name, shape, dt))

        gw, gb, ws1, ws3, ws2, tokv, loaded = (t["w4"][n] for n in ("gw", "gb", "ws1", "ws3", "ws2", "tokv",
                                                                    "loaded"))
        LOADED = 16 * len(t["w4"]["transfers"])
        xrow = sb("xrow", [P, 2, CH, ROW])
        xnT = sb("xnT", [P, 2, CH * P])
        mx, den = sb("gmx", [P, 2, CH]), sb("gden", [P, 2, CH])
        sc = sb("gsc", [P, CH, E0])
        sel, rep, mask = sb("sel", [P, CH, E0]), sb("rep", [P, CH, E0]), sb("mask", [P, CH, E0])
        top = sb("top", [P, CH, 8])
        keyrow = sb("keyrow", [P, CH, E0])
        zero = sb("gzero", [P, E0])
        silu = sb("silu", [I0, 2 * CH * P])
        hid = sb("hid", [I0, 2, 2 * CH * P])
        X, mv, keys = t["X"], t["mv"], t["keys"]
        (pool_own, norm, turned, turned_sb, up, sil, hrd, down, gat, ex, own, kt, stored, ysum) = (
            sem("p4_" + n) for n in ("pool_steps", "x_normed", "turned", "turned_copied", "up_done", "silu_done",
                                     "hidden_ready", "down_done", "gate_done", "exp_done", "dve_steps",
                                     "keys_turned", "rows_stored", "z_added"))
        block = ctx.enter_context(nc.Block())
        rows = t["rows"].rearrange("(c k p) r -> c p k r", k=CH, p=P)
        DVE_STEPS, POOL_CHUNK = 6 + 3 * CH, 3
        FIRST = 1

        @block.sync
        def _(sp):
            for counter in (stored, hrd, ysum, kt, t["keys_in"]):
                sp.sem_inc(counter, START)
            with sp.Fori(0, NC // 2) as c2:
                for i in range(2):
                    c = 2 * c2 + i
                    sp.wait_ge(own, FIRST + (c + 1) * DVE_STEPS)
                    sp.dma_start(rows[c], xrow[:, i, :, :]).then_inc(stored, 16)
            sp.wait_ge(stored, START + 16 * NC)

        @block.gpsimd
        def _(pool):
            pool.wait_ge(loaded, LOADED)

            def bc(ap):
                return ap.unsqueeze(2).broadcast_to([P, CH, E0])

            def body(c, i, first, last):
                s = Steps(pool, pool_own, c * POOL_CHUNK, alone=True)
                score = xrow[:, i, :, D:D + E0]
                pool.wait_ge(own, FIRST + c * DVE_STEPS + 4)
                stand_alone(pool)
                s.do(pool.tensor_tensor(score, score, bc(den[:, i, :]), ALU.mult))
                s.do(pool.tensor_tensor(sel[:], score, gb[:].unsqueeze(1).broadcast_to([P, CH, E0]),
                                        ALU.add))
                pool.wait_ge(own, FIRST + c * DVE_STEPS + 6 + 2 * CH)
                stand_alone(pool)
                if not first:
                    pool.wait_ge(kt, START + c)
                    stand_alone(pool)
                s.do(pool.tensor_tensor(keyrow[:], mask[:], bc(tokv[:, bass.ds(c * CH, CH)]), ALU.mult))
                assert s.n == POOL_CHUNK

            chunks(pool, body)

        @block.scalar
        def _(a):
            def exponentials(c, i):
                a.wait_ge(own, FIRST + c * DVE_STEPS + 2)
                a.activation(xrow[:, i, :, D:D + E0], sc[:], ACT.Exp).then_inc(ex, 1)

            def body(c, i, first, last):
                a.wait_ge(up, c + 1)
                a.wait_ge(hrd, START + c)
                a.activation(silu[:], t["bank23"][0:I0, :], ACT.Silu).then_inc(sil, 1)
                if not last:
                    exponentials(c + 1, 1 - i)

            exponentials(0, 0)
            chunks(a, body)

        @block.tensor
        def _(e):
            e.wait_ge(loaded, LOADED)

            def turn(c, i):
                e.wait_ge(norm, c + 1)
                for k in range(CH):
                    last = e.transpose(ps[0][:, k * P:(k + 1) * P], xrow[:, i, k, 0:D], t["ident"][:])
                last.then_inc(turned, 1)

            def gate(c, i, first=False):
                e.wait_ge(turned_sb, c + 1)
                if not first:
                    e.wait_ge(own, FIRST + (c - 1) * DVE_STEPS + 2)
                    stand_alone(e)
                for k in range(CH):
                    last = e.matmul(ps[1][:, k * E0:(k + 1) * E0], xnT[:, i, k * P:(k + 1) * P], gw[:],
                                    start=True, stop=True)
                last.then_inc(gat, 1)

            def turn_keys(c):
                e.wait_ge(pool_own, (c + 1) * POOL_CHUNK)
                e.wait_ge(t["keys_in"], START + c)
                stand_alone(e)
                for k in range(CH):
                    last = e.transpose(ps[7][0:E0, k * P:(k + 1) * P], keyrow[:, k, :], t["ident"][:])
                last.then_inc(kt, 1)

            def down_rows(c, i):
                e.wait_ge(hrd, START + c + 1)
                e.wait_ge(ysum, START + c)
                for k in range(CH):
                    for f in range(2):
                        last = e.matmul(ps[6][:, k * D:(k + 1) * D],
                                        hid[:, i, f * CH * P + k * P:f * CH * P + (k + 1) * P],
                                        ws2[:, f, :], start=(f == 0), stop=(f == 1))
                last.then_inc(down, 1)

            def body(c, i, first, last_chunk):
                e.wait_ge(turned_sb, c + 1)
                e.wait_ge(hrd, START + c)
                for w, bank in ((ws1, 2), (ws3, 4)):
                    for f in range(2):
                        last = e.matmul(ps[bank + f][0:I0, :], w[:, f * I0:(f + 1) * I0], xnT[:, i, :],
                                        start=True, stop=True)
                last.then_inc(up, 1)
                if not last_chunk:
                    turn(c + 1, 1 - i)
                if not first:
                    turn_keys(c - 1)
                    down_rows(c - 1, 1 - i)
                if not last_chunk:
                    gate(c + 1, 1 - i)
                else:
                    turn_keys(c)
                    down_rows(c, i)

            turn(0, 0)
            gate(0, 0, first=True)
            chunks(e, body)

        @block.vector
        def _(dve):
            Steps(dve, own).do(dve.memset(zero[:], 0.0))

            def bc(ap):
                return ap.unsqueeze(2).broadcast_to([P, CH, E0])

            def normalise(c, i):
                normalise_chunk(dve, xrow[:, i, :, 0:D], X, mv, c).then_inc(norm, 1)

            def turned_rows(c, i):
                dve.wait_ge(turned, c + 1)
                dve.tensor_copy(xnT[:, i, :], ps[0][:]).then_inc(turned_sb, 1)

            def logits(c, i):
                s = Steps(dve, own, FIRST + c * DVE_STEPS, alone=True)
                dve.wait_ge(gat, c + 1)
                g = ps[1][:, 0:CH * E0].rearrange("p (k e) -> p k e", k=CH)
                s.do(dve.reduce_max(mx[:, i, :], g, X_AXIS))
                s.do(dve.tensor_tensor(sc[:], g, bc(mx[:, i, :]), ALU.subtract))

            def sums(c, i):
                s = Steps(dve, own, FIRST + c * DVE_STEPS + 2, alone=True)
                dve.wait_ge(ex, c + 1)
                s.do(dve.reduce_sum(den[:, i, :], xrow[:, i, :, D:D + E0], X_AXIS))
                s.done(dve.reciprocal(den[:, i, :], den[:, i, :]))

            def picks(c, i):
                s = Steps(dve, own, FIRST + c * DVE_STEPS + 4, alone=True)
                dve.wait_ge(pool_own, c * POOL_CHUNK + 2)
                stand_alone(dve)
                for k in range(CH):
                    s.done(dve.max(top[:, k, :], sel[:, k, :]))
                s.settle()
                s.do(dve.memset(top[:, :, K0:8], 3.0e38))
                for k in range(CH):
                    s.done(dve.match_replace(rep[:, k, :], top[:, k, :], sel[:, k, :], -3.0e38))

            def masks(c, first):
                s = Steps(dve, own, FIRST + c * DVE_STEPS + 5 + 2 * CH, alone=True)
                s.settle()
                if not first:
                    dve.wait_ge(pool_own, c * POOL_CHUNK)
                    stand_alone(dve)
                s.done(dve.tensor_tensor(mask[:], rep[:], sel[:], ALU.not_equal))

            def ranks(c, i):
                s = Steps(dve, own, FIRST + c * DVE_STEPS + 6 + 2 * CH, alone=True)
                s.settle()
                for k in range(CH):
                    s.done(dve.tensor_tensor_scan(xrow[:, i, k, D + E0:ROW], mask[:, k, :], zero[:],
                                                  0.0, ALU.add, ALU.add))
                assert 6 + 2 * CH + s.n == DVE_STEPS

            def hidden(c, i):
                dve.wait_ge(sil, c + 1)
                dve.tensor_tensor(hid[:, i, :], silu[:], t["bank45"][0:I0, :], ALU.mult).then_inc(hrd, 1)

            def finish(c):
                dve.wait_ge(kt, START + c + 1)
                dve.tensor_copy(keys[:, bass.ds(c * CH * P, CH * P)], ps[7][0:E0, :])\
                    .then_inc(t["keys_in"], 1)
                dve.wait_ge(down, c + 1)
                xc = X[:, bass.ds(c * CH, CH), :]
                dve.tensor_tensor(xc, xc, ps[6][:].rearrange("p (k d) -> p k d", k=CH),
                                  ALU.add).then_inc(ysum, 1)

            def body(c, i, first, last):
                sums(c, i)
                if not last:
                    if not first:
                        dve.wait_ge(stored, START + 16 * c)
                    normalise(c + 1, 1 - i)
                picks(c, i)
                if not last:
                    turned_rows(c + 1, 1 - i)
                masks(c, first)
                hidden(c, i)
                ranks(c, i)
                if not last:
                    logits(c + 1, 1 - i)
                if not first:
                    finish(c - 1)
                if last:
                    finish(c)

            normalise(0, 0)
            dve.wait_ge(loaded, LOADED)
            turned_rows(0, 0)
            logits(0, 0)
            chunks(dve, body)
            dve.wait_ge(t["keys_in"], START + NC)


def pick_slots(nc, t, sem, ps):
    ctx = ExitStack()
    with ctx:
        def sb(name, shape, dt=F32):
            return ctx.enter_context(nc.sbuf_tensor(name, shape, dt))

        half = N_TOK // 2
        fold = sb("fold", [P, half])
        work = sb("work", [P, half])
        first = sb("firstk", [P, CAP])
        both = sb("bothk", [E0, 2 * CAP])
        both2 = sb("bothk2", [E0, 2 * CAP])
        found = sb("found", [E0, CAP])
        keys, slotv = t["keys"], t["slotv"]
        own, turned = sem("p5_dve_steps"), sem("p5_turned")
        block = ctx.enter_context(nc.Block())

        @block.vector
        def _(dve):
            s = Steps(dve, own)
            s.done(dve.tensor_copy(fold[0:E0, :], keys[:, 0:half]))
            s.do(dve.tensor_copy(fold[E0:P, :], keys[:, half:N_TOK]))

            def largest(out, a, b):
                for r in range(CAP // 8):
                    s.do(dve.max(out[:, r * 8:(r + 1) * 8], a[:]))
                    s.do(dve.match_replace(b[:], out[:, r * 8:(r + 1) * 8], a[:], 0.0))
                    a, b = b, a
            largest(first, fold, work)
            s.done(dve.tensor_copy(both[:, 0:CAP], first[0:E0, :]))
            s.do(dve.tensor_copy(both[:, CAP:2 * CAP], first[E0:P, :]))
            largest(found, both, both2)
            dve.wait_ge(turned, 1)
            v = ps[0][0:CAP, 0:E0].rearrange("p (j o) -> p j o", o=2)
            s.done(dve.tensor_copy(slotv[0:CAP, :], v[:, :, 0]))
            s.do(dve.tensor_copy(slotv[CAP:P, :], v[:, :, 1]))
            s.do(dve.tensor_scalar(t["tok"][:], slotv[:], -1.0, float(N_TOK), ALU.mult, ALU.add))
            s.do(dve.tensor_scalar(t["gidx"][:], t["tok"][:], float(N_TOK - 1), None, ALU.min))
            s.do(dve.tensor_scalar(t["full"][:], slotv[:], 0.0, None, ALU.is_gt))
            t["pick_steps"] = s.n

        @block.tensor
        def _(e):
            e.wait_ge(own, t["pick_steps"] - 5)
            e.transpose(ps[0][0:CAP, 0:E0], found[:], t["ident"][0:E0, 0:E0]).then_inc(turned, 1)


def routed_experts(nc, t, sem, ps):
    ctx = ExitStack()
    with ctx:
        def sb(name, shape, dt=F32):
            return ctx.enter_context(nc.sbuf_tensor(name, shape, dt))

        GT = 4
        NGR = E0 // 2 // GT
        EG = 2 * GT
        w1 = sb("w1b", [P, 2, EG * I0])
        w3 = sb("w3b", [P, 2, EG * I0])
        w2 = sb("w2b", [I0, 2, EG * D])
        xg = [sb(f"xg{i}", [P, GT, ROW]) for i in range(2)]
        sidx = [sb(f"sidx{i}", [P, GT], I32) for i in range(2)]
        didx = [sb(f"didx{i}", [P, GT], I32) for i in range(2)]
        yo = [sb(f"yo{i}", [P, GT, D]) for i in range(2)]
        xT = sb("xgT", [P, GT * P])
        silu = sb("silu5", [I0, GT * P])
        hid = sb("hid5", [I0, 2, GT * P])
        sr = sb("scorerank", [P, 2, GT, 2])
        dst = sb("dstf", [P, NGR * GT])
        w13, wd = ([sem(f"p6_{n}_weights_{i}") for i in range(2)] for n in ("up", "down"))
        (ixr, dxr, gth, turned, turned_sb, up, sil, hrd, down, own, sct, freed, yrd) = (
            sem("p6_" + n) for n in (
                "index_ready", "target_ready", "gathered", "turned", "turned_copied", "up_done",
                "silu_done", "hidden_ready", "down_done", "dve_steps", "scattered", "scatter_over",
                "y_ready"))
        block = ctx.enter_context(nc.Block())
        DVE_STEPS = EG + 4
        tok, full, gidx = t["tok"], t["full"], t["gidx"]

        def groups(eng, body):
            for g in range(2):
                body(g, g, g, False, 0)
            with eng.Fori(1, NGR // 2 - 1) as g2:
                for i in range(2):
                    body(2 * g2 + i, i, 2, False, g2)
            body(NGR - 2, 0, 2, False, NGR // 2 - 1)
            body(NGR - 1, 1, 2, True, NGR // 2 - 1)

        @block.sync
        def _(sp):
            for counter in (up, down, yrd, hrd, freed):
                sp.sem_inc(counter, START)

            def body(g, i, before, last, pair):
                if before >= 2:
                    sp.wait_ge(up, START + g - 1)
                sp.dma_start(w1[:, i, :], t["w1T"][:, bass.ds(g * EG * I0, EG * I0)]).then_inc(w13[i], 16)
                sp.dma_start(w3[:, i, :], t["w3T"][:, bass.ds(g * EG * I0, EG * I0)]).then_inc(w13[i], 16)
                if before >= 2:
                    sp.wait_ge(down, START + g - 1)
                sp.dma_start(w2[:, i, :], t["w2T"][:, bass.ds(g * EG * D, EG * D)]).then_inc(wd[i], 16)

            groups(sp, body)

        @block.gpsimd
        def _(pool):
            def gather(g, i, before):
                if before:
                    pool.wait_ge(gth, g * 16 * GT)
                if before >= 2:
                    pool.wait_ge(turned, g - 1)
                    pool.wait_ge(own, (g - 1) * DVE_STEPS)
                stand_alone(pool)
                pool.tensor_copy(sidx[i][:], gidx[:, bass.ds(g * GT, GT)]).then_inc(ixr, 1)
                pool.wait_ge(ixr, g + 1)
                stand_alone(pool)
                for k in range(GT):
                    pool.indirect_dma_start(
                        out=xg[i][:, k, :], out_offset=None, in_=t["rows"],
                        in_offset=bass.IndirectOffsetOnAxis(ap=sidx[i][:, k:k + 1], axis=0)
                    ).then_inc(gth, 16)

            def scatter(g, i, before):
                if before:
                    pool.wait_ge(sct, g * 16 * GT)
                pool.sem_inc(freed, 1)
                pool.wait_ge(own, (g + 1) * DVE_STEPS)
                stand_alone(pool)
                pool.tensor_copy(didx[i][:], dst[:, bass.ds(g * GT, GT)]).then_inc(dxr, 1)
                pool.wait_ge(dxr, g + 1)
                pool.wait_ge(yrd, START + g + 1)
                stand_alone(pool)
                for k in range(GT):
                    pool.indirect_dma_start(
                        out=t["ybuf"], out_offset=bass.IndirectOffsetOnAxis(ap=didx[i][:, k:k + 1], axis=0),
                        in_=yo[i][:, k, :], in_offset=None, bounds_check=N_TOK * K0 - 1,
                        oob_is_err=False).then_inc(sct, 16)

            def body(g, i, before, last, pair):
                if not last:
                    gather(g + 1, 1 - i, before + 1)
                if before:
                    scatter(g - 1, 1 - i, before - 1)
                if last:
                    scatter(g, i, before)

            gather(0, 0, 0)
            groups(pool, body)
            pool.wait_ge(sct, 16 * GT * NGR)

        @block.scalar
        def _(a):
            with a.Fori(0, NGR) as g:
                a.wait_ge(up, START + g + 1)
                a.activation(silu[:], ps[1][0:I0, :], ACT.Silu).then_inc(sil, 1)

        @block.tensor
        def _(e):
            def turn(g, i):
                e.wait_ge(gth, (g + 1) * 16 * GT)
                for k in range(GT):
                    last = e.transpose(ps[0][:, k * P:(k + 1) * P], xg[i][:, k, 0:D], t["ident"][:])
                last.then_inc(turned, 1)

            def down_rows(g, i, pair):
                e.wait_ge(wd[i], (pair + 1) * 16)
                e.wait_ge(hrd, START + g + 1)
                e.wait_ge(yrd, START + g)
                for x in range(EG):
                    last = e.matmul(ps[3][(x % 2) * CAP:(x % 2 + 1) * CAP, (x // 2) * D:(x // 2 + 1) * D],
                                    hid[:, i, x * CAP:(x + 1) * CAP], w2[:, i, x * D:(x + 1) * D],
                                    start=True, stop=True)
                last.then_inc(down, 1)

            def body(g, i, before, last_group, pair):
                e.wait_ge(turned_sb, g + 1)
                e.wait_ge(w13[i], (pair + 1) * 32)
                e.wait_ge(hrd, START + g)
                for w, bank in ((w1, 1), (w3, 2)):
                    for x in range(EG):
                        last = e.matmul(ps[bank][0:I0, x * CAP:(x + 1) * CAP],
                                        w[:, i, x * I0:(x + 1) * I0], xT[:, x * CAP:(x + 1) * CAP],
                                        start=True, stop=True)
                last.then_inc(up, 1)
                if before:
                    down_rows(g - 1, 1 - i, pair if i else pair - 1)
                if last_group:
                    down_rows(g, i, pair)
                else:
                    turn(g + 1, 1 - i)

            turn(0, 0)
            groups(e, body)

        @block.vector
        def _(dve):
            def addresses(g, i, before):
                s = Steps(dve, own, g * DVE_STEPS)
                dve.wait_ge(gth, (g + 1) * 16 * GT)
                if before >= 2:
                    dve.wait_ge(yrd, START + g - 1)
                for k in range(GT):
                    v = xg[i][:, k, D:ROW].rearrange("p (a e) -> p a e", a=2)
                    for o in range(2):
                        h = slice(o * CAP, (o + 1) * CAP)
                        s.done(dve.tensor_copy(sr[h, i, k, :], v[h, :, bass.ds(g * EG + 2 * k + o, 1)]
                                               .squeeze(2)))
                s.settle()
                s.do(dve.tensor_tensor(sr[:, i, :, 0], sr[:, i, :, 0], full[:, bass.ds(g * GT, GT)], ALU.mult))
                d = dst[:, bass.ds(g * GT, GT)]
                s.do(dve.scalar_tensor_tensor(out=d, in0=tok[:, bass.ds(g * GT, GT)],
                                              scalar=float(K0), in1=sr[:, i, :, 1], op0=ALU.mult,
                                              op1=ALU.add))
                s.do(dve.scalar_tensor_tensor(out=d, in0=full[:, bass.ds(g * GT, GT)],
                                              scalar=-8.0, in1=d, op0=ALU.mult, op1=ALU.add))
                s.do(dve.tensor_scalar(d, d, 7.0, None, ALU.add))
                assert s.n == DVE_STEPS

            def turned_rows(g):
                dve.wait_ge(turned, g + 1)
                dve.tensor_copy(xT[:], ps[0][:]).then_inc(turned_sb, 1)

            def results(g, i):
                dve.wait_ge(freed, START + g)
                dve.wait_ge(down, START + g + 1)
                dve.tensor_tensor(yo[i][:], ps[3][:].rearrange("p (k d) -> p k d", k=GT),
                                  sr[:, i, :, 0].unsqueeze(2).broadcast_to([P, GT, D]),
                                  ALU.mult).then_inc(yrd, 1)

            def body(g, i, before, last, pair):
                dve.wait_ge(sil, g + 1)
                dve.tensor_tensor(hid[:, i, :], silu[:], ps[2][0:I0, :], ALU.mult).then_inc(hrd, 1)
                if before:
                    results(g - 1, 1 - i)
                if last:
                    results(g, i)
                else:
                    addresses(g + 1, 1 - i, before + 1)
                    turned_rows(g + 1)

            addresses(0, 0, 0)
            turned_rows(0)
            groups(dve, body)
H1, DH1 = 4, 32
FF = 4 * D
E1, F1 = 8, 256
KSCALE = DH1 ** -0.25


def rstd_of(pool, t, own, steps, ready):
    pool.wait_ge(own, steps)
    pool.tensor_tensor(t["mv"][:, 1, :], t["mv"][:, 1, :], t["neg_half"][:, 0:NT], ALU.pow).then_inc(ready, 1)


def expert_weights(nc, t, sb, sem):
    NF = F1 // P
    w = {n: sb(n, [P, E1, F1]) for n in ("gate7", "up7")}
    for n in ("gate7", "up7"):
        w[n + "_high"], w[n + "_low"] = sb(n + "h", [P, E1, F1], F32R), sb(n + "l", [P, E1, F1], F32R)
    w["down7"] = sb("down7", [P, E1, NF, D])
    w["loaded"], w["split_high"], w["split"] = (sem("w7_" + n) for n in ("loaded", "high_parts", "low_parts"))

    def load(sp):
        for dst, n in (("gate7", "gate_w1"), ("up7", "up_w1")):
            sp.dma_start(w[dst][:], t[n].rearrange("e d f -> d e f")).then_inc(w["loaded"], 16)
        sp.dma_start(w["down7"][:].rearrange("p e n d -> p (e n) d"),
                     t["down_w1"].rearrange("e (n p) d -> p (e n) d", p=P)).then_inc(w["loaded"], 16)

    def split(pool):
        pool.wait_ge(w["loaded"], 48)
        for n in ("gate7", "up7"):
            pool.tensor_copy(w[n + "_high"][:], w[n][:]).then_inc(w["split_high"], 1)
        pool.wait_ge(w["split_high"], 2)
        for n in ("gate7", "up7"):
            pool.tensor_tensor(w[n + "_low"][:], w[n][:], w[n + "_high"][:].bitcast(F32), ALU.subtract)\
                .then_inc(w["split"], 1)
        pool.wait_ge(w["split"], 2)
    w["load"], w["do_split"] = load, split
    return w


def combine(nc, t, sem, ps):
    ctx = ExitStack()
    with ctx:
        def sb(name, shape, dt=F32):
            return ctx.enter_context(nc.sbuf_tensor(name, shape, dt))

        YB = 4
        yk = sb("yk", [P, YB, CH, K0 * D])
        ysum = sb("ysumt", [P, 2, CH, D])
        stats, tmp = sb("stats7", [P, NT, 6]), sb("tmp7", [P, 2, NT])
        X, XO, mv = t["X"], t["XO"], t["mv"]
        ld = [sem(f"p7_rows_loaded_{i}") for i in range(YB)]
        summed, added, stat, own, var1, nrm = (sem("p7_" + n) for n in (
            "summed", "added", "stats", "dve_steps", "rstd_ready", "normed"))
        block = ctx.enter_context(nc.Block())
        y = t["ybuf"].rearrange("(c k p s) d -> c p k (s d)", k=CH, p=P, s=K0)

        @block.sync
        def _(sp):
            sp.sem_inc(summed, START)

            def load(c, i):
                sp.dma_start(yk[:, i, :, :], y[c]).then_inc(ld[i], 16)

            for c in range(YB):
                load(c, c)
            with sp.Fori(1, NC // YB) as c4:
                for i in range(YB):
                    c = YB * c4 + i
                    sp.wait_ge(summed, START + c - YB + 1)
                    load(c, i)
            load_weights(sp, t["w8"])
            t["w7"]["load"](sp)

        @block.gpsimd
        def _(pool):
            rstd_of(pool, t, own, STATS_STEPS, var1)
            rstd_of(pool, t, own, 2 * STATS_STEPS, var1)
            pool.wait_ge(var1, 2)

        @block.vector
        def _(dve):
            def statistics(src, c, done):
                for k in range(CH):
                    dve.bn_stats(stats[:, c * CH + k, :], src[:, c * CH + k, :]).then_inc(done, 1)

            def add(c, i, count, first=False):
                dve.wait_ge(ld[i], count)
                for k in range(CH):
                    last = dve.reduce_sum(ysum[:, i % 2, k, :], yk[:, i, k, :].rearrange("p (s d) -> p d s", s=K0),
                                          X_AXIS)
                last.then_inc(summed, 1)
                if not first:
                    dve.wait_ge(added, c)
                    statistics(X, c - 1, stat)
                dve.wait_ge(summed, START + c + 1)
                xc = X[:, bass.ds(c * CH, CH), :]
                dve.tensor_tensor(xc, xc, ysum[:, i % 2, :, :], ALU.add).then_inc(added, 1)

            for c in range(YB):
                add(c, c, 16, first=c == 0)
            with dve.Fori(1, NC // YB) as c4:
                for i in range(YB):
                    add(YB * c4 + i, i, (c4 + 1) * 16)
            dve.wait_ge(added, NC)
            statistics(X, NC - 1, stat)
            dve.wait_ge(stat, NT)
            finish_stats(dve, Steps(dve, own), stats, mv, tmp, NT)
            dve.wait_ge(var1, 1)

            def normalise(c):
                normalise_chunk(dve, XO[:, bass.ds(c * CH, CH), :], X, mv, c).then_inc(nrm, 1)

            normalise(0)
            with dve.Fori(1, NC) as c:
                normalise(c)
                dve.wait_ge(nrm, c)
                statistics(XO, c - 1, stat)
            dve.wait_ge(nrm, NC)
            statistics(XO, NC - 1, stat)
            dve.wait_ge(stat, 2 * NT)
            finish_stats(dve, Steps(dve, own, STATS_STEPS), stats, mv, tmp, NT)


def linear_weights(t, sb, sem):
    shapes = {"wk": [P, D], "wqv": [P, 2 * D], "wo": [P, D], "bo": [P, D], "block32": [P, D], "ln": [P, 2]}
    w = {n: sb("l1_" + n, shape) for n, shape in shapes.items()}
    w["loaded"] = sem("p8_loaded")
    col = lambda v: v.rearrange("(p a) -> p a", a=1)
    w["transfers"] = [(w["wk"][:], t["l1_wk"]), (w["wqv"][:, 0:D], t["l1_wq"]),
                      (w["wqv"][:, D:2 * D], t["l1_wv"]), (w["wo"][:], t["l1_wo"]),
                      (w["block32"][:], t["block32"]), (w["bo"][:], t["l1_bo"].partition_broadcast(P)),
                      (w["ln"][:, 0:1], col(t["ln1_g"])), (w["ln"][:, 1:2], col(t["ln1_b"]))]
    return w


def linear_attention(nc, t, sem, ps):
    ctx = ExitStack()
    with ctx:
        def sb(name, shape, dt=F32):
            return ctx.enter_context(nc.sbuf_tensor(name, shape, dt))

        CB = TB // CH
        assert CB == 2
        W = CH * P
        wk, wqv, wo, bo, lncol, block32, ld = (t["w8"][n] for n in ("wk", "wqv", "wo", "bo", "ln", "block32",
                                                                    "loaded"))
        LOADED = 16 * len(t["w8"]["transfers"])
        h = sb("h1", [P, 2, CH, D])
        hT = sb("h1T", [P, 2, W])
        kT, ke = sb("k1T", [P, N_TOK]), sb("k1e", [P, S])
        ktok, vtok = sb("ktok", [P, TB, D]), sb("vtok", [P, NT, D])
        qs, qe, qn = sb("qs", [P, CH, D]), sb("qe", [P, CH, D]), sb("qn", [P, CH, D])
        qT = sb("q1T", [P, N_TOK])
        qm, qd = sb("qm", [P, CH * H1]), sb("qd", [P, CH * H1])
        km, ksum, krec = sb("km", [P, 2]), sb("ksum", [P, 1]), sb("krec", [P, 1])
        cmat = sb("cmat", [P, D])
        aT = sb("a1T", [P, S])
        stats, tmp = sb("stats8", [P, NT, 6]), sb("tmp8", [P, 2, NT])
        XO, mv = t["XO"], t["mv"]
        nrm, biased, stat, rst, own2, q_own, k_own, added = (sem("p8_" + n) for n in (
            "normed", "xo_biased", "stats", "rstd_ready", "stat_steps", "q_steps", "k_steps",
            "added"))
        turned, kmm, qvm, q_turned, e_turned, ctx_done, applied, projected = (sem("p8_" + n) for n in (
            "turned", "k_done", "qv_done", "q_turned", "exp_k_turned", "context_done", "applied",
            "projected"))
        h_copied, k_copied, v_copied, q_exp, q_copied, k_exp, e_copied, a_copied = (
            sem("p8_" + n) for n in ("h_copied", "k_copied", "v_copied", "q_exp_done", "q_copied",
                                     "k_exp_done", "exp_k_copied", "a_copied"))
        block = ctx.enter_context(nc.Block())
        Q_STEPS, K_STEPS = 5, 4

        def batches(eng, body):
            body(0, True, False)
            with eng.Fori(1, B - 1) as b:
                body(b, False, False)
            body(B - 1, False, True)

        @block.sync
        def _(sp):
            for counter in (k_copied, v_copied, q_copied, added):
                sp.sem_inc(counter, START)
            load_weights(sp, t["w9"])

        @block.gpsimd
        def _(pool):
            t["w7"]["do_split"](pool)
            pool.wait_ge(ld, LOADED)
            with pool.Fori(0, B) as b:
                pool.wait_ge(nrm, (b + 1) * CB)
                xc = XO[:, bass.ds(b * TB, TB), :]
                pool.tensor_tensor(xc, xc, bo[:].unsqueeze(1).broadcast_to([P, TB, D]), ALU.add)\
                    .then_inc(biased, 1)
            rstd_of(pool, t, own2, STATS_STEPS, rst)
            pool.wait_ge(rst, 1)

        @block.tensor
        def _(e):
            e.wait_ge(ld, LOADED)

            def turn(c, i):
                e.wait_ge(nrm, c + 1)
                for k in range(CH):
                    last = e.transpose(ps[0][:, k * P:(k + 1) * P], h[:, i, k, :], t["ident"][:])
                last.then_inc(turned, 1)

            def project(c, i):
                e.wait_ge(h_copied, c + 1)
                e.wait_ge(k_copied, START + c)
                e.matmul(ps[1][:], wk[:], hT[:, i, :], start=True, stop=True).then_inc(kmm, 1)
                e.wait_ge(v_copied, START + c)
                for k in range(CH):
                    last = e.matmul(ps[2 + k // 2][:, (k % 2) * 2 * D:(k % 2 + 1) * 2 * D],
                                    hT[:, i, k * P:(k + 1) * P], wqv[:], start=True, stop=True)
                last.then_inc(qvm, 1)

            def turn_q(c):
                e.wait_ge(q_own, (c + 1) * Q_STEPS)
                e.wait_ge(q_copied, START + c)
                stand_alone(e)
                for k in range(CH):
                    last = e.transpose(ps[4][:, k * P:(k + 1) * P], qn[:, k, :], t["ident"][:])
                last.then_inc(q_turned, 1)

            def turn_k(b):
                e.wait_ge(k_exp, b + 1)
                e.wait_ge(added, START + b * CB)
                stand_alone(e)
                for k in range(TB):
                    last = e.transpose(ps[6 + k // CH][:, (k % CH) * P:(k % CH + 1) * P],
                                       ke[:, k * P:(k + 1) * P], t["ident"][:])
                last.then_inc(e_turned, 1)

            def context(b):
                e.wait_ge(e_copied, b + 1)
                for k in range(TB):
                    last = e.matmul(ps[5][:, 0:D], ktok[:, k, :], vtok[:, b * TB + k, :], start=(k == 0),
                                    stop=(k == TB - 1))
                last.then_inc(ctx_done, 1)

            def apply(b):
                e.wait_ge(k_own, (b + 1) * K_STEPS)
                e.wait_ge(q_copied, START + (b + 1) * CB)
                for c in range(CB):
                    last = e.matmul(ps[6 + c][:], cmat[:], qT[:, bass.ds((b * CB + c) * W, W)],
                                    start=True, stop=True)
                last.then_inc(applied, 1)

            def output(b):
                e.wait_ge(a_copied, b + 1)
                for k in range(TB):
                    last = e.matmul(ps[6 + k // CH][:, (k % CH) * D:(k % CH + 1) * D],
                                    aT[:, k * P:(k + 1) * P], wo[:], start=True, stop=True)
                last.then_inc(projected, 1)

            def body(b, first, last):
                project(b * CB, 0)
                turn(b * CB + 1, 1)
                if not first:
                    turn_q(b * CB - 1)
                    turn_k(b - 1)
                    context(b - 1)
                project(b * CB + 1, 1)
                if not first:
                    apply(b - 1)
                if not last:
                    turn(b * CB + 2, 0)
                turn_q(b * CB)
                if not first:
                    output(b - 1)

            turn(0, 0)
            batches(e, body)
            turn_q(NC - 1)
            turn_k(B - 1)
            context(B - 1)
            apply(B - 1)
            output(B - 1)

        @block.scalar
        def _(a):
            a.wait_ge(ld, LOADED)

            def copy_h(c, i):
                a.wait_ge(turned, c + 1)
                a.activation(hT[:, i, :], ps[0][:], ACT.Identity, bias=lncol[:, 1:2],
                             scale=lncol[:, 0:1]).then_inc(h_copied, 1)

            def copy_k(c):
                a.wait_ge(kmm, c + 1)
                a.activation(kT[:, bass.ds(c * W, W)], ps[1][:], ACT.Copy).then_inc(k_copied, 1)

            def values_and_exp_q(c):
                a.wait_ge(q_own, c * Q_STEPS + 2)
                for j in range(2):
                    last = a.activation(vtok[:, bass.ds(c * CH + 2 * j, 2), :],
                                        ps[2 + j][:].rearrange("p (k w d) -> p k w d", k=2, w=2)[:, :, 1, :],
                                        ACT.Copy)
                last.then_inc(v_copied, 1)
                a.activation(qe[:], qs[:], ACT.Exp, scale=KSCALE).then_inc(q_exp, 1)

            def copy_q(c):
                a.wait_ge(q_turned, c + 1)
                a.activation(qT[:, bass.ds(c * W, W)], ps[4][:], ACT.Copy).then_inc(q_copied, 1)

            def exp_k(b):
                a.wait_ge(k_own, b * K_STEPS + 2)
                a.activation(ke[:], kT[:, bass.ds(b * S, S)], ACT.Exp, bias=km[:, 1:2], scale=KSCALE,
                             accum_out=ksum[:]).then_inc(k_exp, 1)

            def copy_exp_k(b):
                a.wait_ge(e_turned, b + 1)
                a.activation(ktok[:].rearrange("p k d -> p (k d)"), t["bank67"], ACT.Copy)\
                    .then_inc(e_copied, 1)

            def copy_applied(b):
                a.wait_ge(applied, b + 1)
                a.activation(aT[:], t["bank67"], ACT.Copy).then_inc(a_copied, 1)

            def body(b, first, last):
                if not first:
                    exp_k(b - 1)
                copy_k(b * CB)
                copy_h(b * CB + 1, 1)
                if not first:
                    copy_q(b * CB - 1)
                    copy_exp_k(b - 1)
                values_and_exp_q(b * CB)
                copy_k(b * CB + 1)
                if not first:
                    copy_applied(b - 1)
                if not last:
                    copy_h(b * CB + 2, 0)
                values_and_exp_q(b * CB + 1)
                copy_q(b * CB)

            copy_h(0, 0)
            batches(a, body)
            exp_k(B - 1)
            copy_q(NC - 1)
            copy_exp_k(B - 1)
            copy_applied(B - 1)

        @block.vector
        def _(dve):
            dve.wait_ge(ld, LOADED)

            def normalise(c, i):
                normalise_chunk(dve, h[:, i, :, :], XO, mv, c).then_inc(nrm, 1)

            def less_maxima(c):
                s = Steps(dve, q_own, c * Q_STEPS)
                dve.wait_ge(qvm, c + 1)
                v = [ps[2 + j][:].rearrange("p (k w h d) -> p k w h d", k=2, w=2, h=H1) for j in range(2)]
                for j in range(2):
                    last = dve.reduce_max(qm[:, j * 2 * H1:(j + 1) * 2 * H1]
                                          .rearrange("p (k h) -> p k h", k=2), v[j][:, :, 0, :, :], X_AXIS)
                s.do(last)
                for j in range(2):
                    for k in range(2):
                        m = qm[:, (2 * j + k) * H1:(2 * j + k + 1) * H1]
                        last = dve.tensor_tensor(
                            qs[:, 2 * j + k, :].rearrange("p (h d) -> p h d", h=H1), v[j][:, k, 0, :, :],
                            m.unsqueeze(2).broadcast_to([P, H1, DH1]), ALU.subtract)
                s.done(last)

            def softmax_q(c, first=False):
                s = Steps(dve, q_own, c * Q_STEPS + 2)
                dve.wait_ge(q_exp, c + 1)
                q4 = qe[:].rearrange("p k (h d) -> p (k h) d", h=H1)
                s.do(dve.reduce_sum(qd[:], q4, X_AXIS))
                s.do(dve.reciprocal(qd[:], qd[:]))
                if not first:
                    dve.wait_ge(q_turned, c)
                s.done(dve.tensor_tensor(qn[:].rearrange("p k (h d) -> p (k h) d", h=H1), q4,
                                         qd[:].unsqueeze(2).broadcast_to([P, CH * H1, DH1]), ALU.mult))

            def maxima_k(b):
                s = Steps(dve, k_own, b * K_STEPS)
                dve.wait_ge(k_copied, START + (b + 1) * CB)
                s.do(dve.reduce_max(km[:, 0:1], kT[:, bass.ds(b * S, S)], X_AXIS))
                s.done(dve.tensor_scalar(km[:, 1:2], km[:, 0:1], -KSCALE, None, ALU.mult))

            def context(b):
                s = Steps(dve, k_own, b * K_STEPS + 2)
                dve.wait_ge(ctx_done, b + 1)
                s.do(dve.reciprocal(krec[:], ksum[:]))
                s.done(dve.scalar_tensor_tensor(out=cmat[:], in0=ps[5][:, 0:D], scalar=krec[:],
                                                in1=block32[:], op0=ALU.mult, op1=ALU.mult))

            def add(b):
                dve.wait_ge(projected, b + 1)
                dve.wait_ge(biased, b + 1)
                for c in range(CB):
                    xc = XO[:, bass.ds(b * TB + c * CH, CH), :]
                    dve.tensor_tensor(xc, xc, ps[6 + c][:].rearrange("p (k d) -> p k d", k=CH),
                                      ALU.add).then_inc(added, 1)
                dve.wait_ge(added, START + (b + 1) * CB)
                for k in range(TB):
                    dve.bn_stats(stats[:, b * TB + k, :], XO[:, b * TB + k, :]).then_inc(stat, 1)

            def body(b, first, last):
                if not first:
                    maxima_k(b - 1)
                less_maxima(b * CB)
                if not last:
                    dve.wait_ge(turned, b * CB + 1)
                    normalise(b * CB + 2, 0)
                softmax_q(b * CB, first)
                if not first:
                    context(b - 1)
                less_maxima(b * CB + 1)
                if not last:
                    dve.wait_ge(turned, b * CB + 2)
                    normalise(b * CB + 3, 1)
                softmax_q(b * CB + 1)
                if not first:
                    add(b - 1)

            normalise(0, 0)
            normalise(1, 1)
            batches(dve, body)
            maxima_k(B - 1)
            context(B - 1)
            add(B - 1)
            dve.wait_ge(stat, NT)
            finish_stats(dve, Steps(dve, own2), stats, mv, tmp, NT)


def feed_forward_weights(t, sb, sem):
    NF = FF // P
    shapes = {"wf1": [P, FF], "wf2": [P, NF, D], "wd": [P, D], "ln": [P, 2], "bf1": [P, NF], "bf2": [P, D],
              "bd": [P, D]}
    w = {n: sb("ff_" + n, shape) for n, shape in shapes.items()}
    w["loaded"] = sem("p9_loaded")
    col = lambda v: v.rearrange("(p a) -> p a", a=1)
    w["transfers"] = [(w["wf1"][:], t["w_ff1"]), (w["wd"][:], t["w_d"]),
                      (w["wf2"][:], t["w_ff2"].rearrange("(f p) d -> p f d", p=P)), (w["bf1"][:], t["b_ff1"]),
                      (w["bf2"][:], t["b_ff2"].partition_broadcast(P)),
                      (w["bd"][:], t["b_d"].partition_broadcast(P)),
                      (w["ln"][:, 0:1], col(t["ln2_g"])), (w["ln"][:, 1:2], col(t["ln2_b"]))]
    return w


def feed_forward(nc, t, sem, ps):
    ctx = ExitStack()
    with ctx:
        def sb(name, shape, dt=F32):
            return ctx.enter_context(nc.sbuf_tensor(name, shape, dt))

        NF = FF // P
        wf1, wf2, wd, lncol, bf1, bf2, bd, ld = (t["w9"][n] for n in ("wf1", "wf2", "wd", "ln", "bf1", "bf2",
                                                                      "bd", "loaded"))
        LOADED = 16 * len(t["w9"]["transfers"])
        h, hT = sb("h2", [P, 2, CH, D]), sb("h2T", [P, 2, CH * P])
        f = sb("f2", [P, 2, NF, CH * P])
        y, yT = sb("y2", [P, CH, D]), sb("y2T", [P, CH * P])
        yb = sb("yb2", [P, 2, CH, D])
        stats, tmp = sb("stats9", [P, NT, 6]), sb("tmp9", [P, 2, CH])
        X, XO, mv = t["X"], t["XO"], t["mv"]
        nrm, turned, hts, f1, gl, f2, ysum, yturned, yts, d1, xs, stat, own, rst, yb_r, xb_r = (
            sem("p9_" + n) for n in (
                "normed", "turned", "turned_copied", "ff1_done", "gelu_done", "ff2_done",
                "y_summed", "y_turned", "y_copied", "wd_done", "x_added", "stats", "dve_steps",
                "rstd_ready", "y_biased", "x_biased"))
        block = ctx.enter_context(nc.Block())

        @block.sync
        def _(sp):
            for counter in (ysum, yts, xs, gl, f2, turned, yturned):
                sp.sem_inc(counter, START)
            load_weights(sp, t["w10"])

        @block.gpsimd
        def _(pool):
            pool.wait_ge(ld, LOADED)

            def rstd(c):
                v = mv[:, 1, bass.ds(c * CH, CH)]
                pool.wait_ge(own, (c + 1) * STATS_STEPS)
                pool.tensor_tensor(v, v, t["neg_half"][:, 0:CH], ALU.pow).then_inc(rst, 1)

            def body(c, i, first, last):
                cs = bass.ds(c * CH, CH)
                pool.wait_ge(ysum, START + c)
                pool.tensor_tensor(yb[:, i, :, :], XO[:, cs, :],
                                   bf2[:].unsqueeze(1).broadcast_to([P, CH, D]), ALU.add).then_inc(yb_r, 1)
                pool.tensor_tensor(X[:, cs, :], X[:, cs, :],
                                   bd[:].unsqueeze(1).broadcast_to([P, CH, D]), ALU.add).then_inc(xb_r, 1)
                if not first:
                    rstd(c - 1)
                if last:
                    rstd(c)

            chunks(pool, body)
            pool.wait_ge(rst, NC)

        @block.tensor
        def _(e):
            e.wait_ge(ld, LOADED)

            def turn(c, i):
                e.wait_ge(nrm, c + 1)
                for k in range(CH):
                    last = e.transpose(ps[0][:, k * P:(k + 1) * P], h[:, i, k, :], t["ident"][:])
                last.then_inc(turned, 1)

            def back(c, i, between=None):
                e.wait_ge(gl, START + (c + 1) * NF)
                e.wait_ge(ysum, START + c)
                for k in range(CH):
                    for n in range(NF):
                        last = e.matmul(ps[5][:, k * D:(k + 1) * D], f[:, i, n, k * P:(k + 1) * P],
                                        wf2[:, n, :], start=(n == 0), stop=(n == NF - 1))
                last.then_inc(f2, 1)
                if between:
                    between()
                e.wait_ge(ysum, START + c + 1)
                e.wait_ge(yts, START + c)
                for k in range(CH):
                    last = e.transpose(ps[6][:, k * P:(k + 1) * P], y[:, k, :], t["ident"][:])
                last.then_inc(yturned, 1)
                e.wait_ge(yts, START + c + 1)
                e.wait_ge(xs, START + c)
                for k in range(CH):
                    last = e.matmul(ps[7][:, k * D:(k + 1) * D], yT[:, k * P:(k + 1) * P], wd[:],
                                    start=True, stop=True)
                last.then_inc(d1, 1)

            def body(c, i, first, last):
                e.wait_ge(hts, c + 1)
                for n in range(NF):
                    if not first:
                        e.wait_ge(gl, START + (c - 1) * NF + n + 1)
                    e.matmul(ps[1 + n][:], wf1[:, n * P:(n + 1) * P], hT[:, i, :], start=True,
                             stop=True).then_inc(f1, 1)
                following = lambda: None if last else turn(c + 1, 1 - i)
                if first:
                    following()
                else:
                    back(c - 1, 1 - i, following)
                if last:
                    back(c, i)

            turn(0, 0)
            chunks(e, body)

        @block.scalar
        def _(a):
            a.wait_ge(ld, LOADED)

            def turned_rows(c, i):
                a.wait_ge(turned, START + c + 1)
                a.activation(hT[:, i, :], ps[0][:], ACT.Identity, bias=lncol[:, 1:2],
                             scale=lncol[:, 0:1]).then_inc(hts, 1)

            def turned_sums(c):
                a.wait_ge(yturned, START + c + 1)
                a.activation(yT[:], ps[6][:], ACT.Copy).then_inc(yts, 1)

            def body(c, i, first, last):
                if not first:
                    a.wait_ge(f2, START + c - 1)
                for n in range(NF):
                    a.wait_ge(f1, c * NF + n + 1)
                    a.activation(f[:, i, n, :], ps[1 + n][:], ACT.Gelu_apprx_tanh,
                                 bias=bf1[:, n:n + 1]).then_inc(gl, 1)
                if not last:
                    turned_rows(c + 1, 1 - i)
                if not first:
                    turned_sums(c - 1)
                if last:
                    turned_sums(c)

            turned_rows(0, 0)
            chunks(a, body)

        @block.vector
        def _(dve):
            def normalise(c, i, fresh=False):
                if not fresh:
                    dve.wait_ge(turned, START + c - 1)
                normalise_chunk(dve, h[:, i, :, :], XO, mv, c).then_inc(nrm, 1)

            def back(c, i):
                dve.wait_ge(f2, START + c + 1)
                dve.wait_ge(yb_r, c + 1)
                dve.wait_ge(yturned, START + c)
                dve.tensor_tensor(y[:], ps[5][:].rearrange("p (k d) -> p k d", k=CH), yb[:, i, :, :],
                                  ALU.add).then_inc(ysum, 1)
                dve.wait_ge(d1, c + 1)
                dve.wait_ge(xb_r, c + 1)
                xc = X[:, bass.ds(c * CH, CH), :]
                dve.tensor_tensor(xc, xc, ps[7][:].rearrange("p (k d) -> p k d", k=CH),
                                  ALU.add).then_inc(xs, 1)
                dve.wait_ge(xs, START + c + 1)
                for k in range(CH):
                    dve.bn_stats(stats[:, c * CH + k, :], X[:, c * CH + k, :]).then_inc(stat, 1)
                dve.wait_ge(stat, (c + 1) * CH)
                cs = bass.ds(c * CH, CH)
                finish_stats(dve, Steps(dve, own, c * STATS_STEPS, alone=True), stats[:, cs, :],
                             mv[:, :, cs], tmp, CH)

            def body(c, i, first, last):
                if not last:
                    normalise(c + 1, 1 - i, fresh=first)
                if not first:
                    back(c - 1, 1 - i)
                if last:
                    back(c, i)

            normalise(0, 0, fresh=True)
            chunks(dve, body)


def router_weights(t, sb, sem):
    NF = F1 // P
    shapes = {"rw": [P, E1], "bg": [P, E1, NF], "bu": [P, E1, NF], "bdn": [E1, D]}
    w = {n: sb("moe_" + n, shape) for n, shape in shapes.items()}
    w["loaded"] = sem("p10_loaded")
    w["transfers"] = [(w["rw"][:], t["router_wT"]), (w["bdn"][:], t["down_b1"])]\
        + [(w[n][:].rearrange("p e n -> p (e n)"), t[src]) for n, src in (("bg", "gate_b1"), ("bu", "up_b1"))]
    return w


def experts_of_two(nc, t, sem, ps):
    ctx = ExitStack()
    with ctx:
        def sb(name, shape, dt=F32):
            return ctx.enter_context(nc.sbuf_tensor(name, shape, dt))

        NF = F1 // P
        w = t["w7"]
        wdn = w["down7"]
        gate, upw = ([w[n + "_high"], w[n + "_low"]] for n in ("gate7", "up7"))
        rw, bg, bu, bdn, ld = (t["w10"][n] for n in ("rw", "bg", "bu", "bdn", "loaded"))
        LOADED = 16 * len(t["w10"]["transfers"])
        xf, xT = sb("xf7", [P, CH, D]), sb("xf7T", [P, CH * P])
        xh, xl = sb("xf7h", [P, 2, CH * P], F32R), sb("xf7l", [P, 2, CH * P], F32R)
        sc, rep, top = sb("sc7", [P, CH, E1]), sb("rep7", [P, CH, E1]), sb("top7", [P, CH, 8])
        prob, mx, pw = sb("prob7", [P, CH, E1]), sb("mx7", [P, CH]), sb("pw7", [P, 2, CH, E1])
        pT = sb("pT7", [E1, CH * P])
        sil = sb("sil7", [P, 2, CH * P])
        hid = sb("hid7", [P, 2, NF, CH * P])
        acc = sb("acc7", [P, 2, CH, D])
        X, mv = t["X"], t["mv"]
        nrm, turned, xts, xls, own, ex, rt, pt, ptr, db, ini, gu, sl, hd, dn, ac, st = (
            sem("p10_" + n) for n in (
                "normed", "turned", "turned_copied", "low_ready", "dve_steps", "exp_done", "routed",
                "p_turned", "p_copied", "bias_done", "acc_begun", "gate_up_done", "silu_done",
                "hidden_ready", "down_done", "accumulated", "stored"))
        block = ctx.enter_context(nc.Block())
        DVE_STEPS = 12 + 2 * CH
        UN = E1 * NF
        ADDS = E1 * CH
        out = t["out"].rearrange("b (n k p) d -> (b n) p k d", k=CH, p=P)

        @block.sync
        def _(sp):
            for counter in (hd, turned, st, ac, ini, rt):
                sp.sem_inc(counter, START)
            with sp.Fori(0, NC // 2) as c2:
                for i in range(2):
                    c = 2 * c2 + i
                    sp.wait_ge(ac, START + (c + 1) * ADDS)
                    sp.dma_start(out[c], acc[:, i, :, :]).then_inc(st, 16)
            sp.wait_ge(st, START + 16 * NC)

        @block.tensor
        def _(e):
            e.wait_ge(ld, LOADED)

            def turn(c, i):
                e.wait_ge(nrm, c + 1)
                e.wait_ge(ini, START + c)
                for k in range(CH):
                    last = e.transpose(ps[0][:, k * P:(k + 1) * P], xf[:, k, :], t["ident"][:])
                last.then_inc(turned, 1)

            def router(c, i):
                e.wait_ge(xts, 2 * c + 1)
                for k in range(CH):
                    last = e.matmul(ps[1][:, k * E1:(k + 1) * E1], xT[:, k * P:(k + 1) * P], rw[:],
                                    start=True, stop=True)
                last.then_inc(rt, 1)

            def turn_weights(c, i):
                e.wait_ge(own, (c + 1) * DVE_STEPS)
                stand_alone(e)
                for k in range(CH):
                    last = e.transpose(ps[6][0:E1, k * P:(k + 1) * P], pw[:, i, k, :], t["ident"][:])
                last.then_inc(pt, 1)

            def bias(c, i):
                e.wait_ge(ptr, c + 1)
                e.wait_ge(xts, 2 * c + 2)
                for k in range(CH):
                    last = e.matmul(ps[0][:, k * D:(k + 1) * D], pT[:, k * P:(k + 1) * P], bdn[:],
                                    start=True, stop=True)
                last.then_inc(db, 1)

            def down(c, x):
                e.wait_ge(hd, START + c * UN + (x + 1) * NF)
                e.wait_ge(ac, START + c * ADDS + x * CH)
                for k in range(CH):
                    for n in range(NF):
                        last = e.matmul(ps[7][:, k * D:(k + 1) * D], hid[:, x % 2, n, k * P:(k + 1) * P],
                                        wdn[:, x, n, :], start=(n == 0), stop=(n == NF - 1))
                last.then_inc(dn, 1)

            def body(c, i, first, last_chunk):
                for x in range(E1):
                    for n in range(NF):
                        u = x * NF + n
                        if u == 0:
                            e.wait_ge(xls, c + 1)
                        e.wait_ge(hd, START + c * UN + max(u - 1, 0))
                        for bank, wt in ((2, gate), (3, upw)):
                            terms = ((0, xh), (0, xl), (1, xh))
                            for j, (part, rows) in enumerate(terms):
                                m = e.matmul(ps[bank + 2 * (u % 2)][:], wt[part][:, x, n * P:(n + 1) * P],
                                             rows[:, i, :], start=(j == 0), stop=(j == len(terms) - 1))
                        m.then_inc(gu, 1)
                        if first and u == 2:
                            turn_weights(c, i)
                        if first and u == 3:
                            bias(c, i)
                        if not last_chunk:
                            if u == (4 if first else 2):
                                turn(c + 1, 1 - i)
                            elif u == (5 if first else 4):
                                router(c + 1, 1 - i)
                            elif u == 14:
                                turn_weights(c + 1, 1 - i)
                            elif u == 15:
                                bias(c + 1, 1 - i)
                    if x:
                        down(c, x - 1)
                    elif not first:
                        down(c - 1, E1 - 1)
                if last_chunk:
                    down(c, E1 - 1)

            turn(0, 0)
            router(0, 0)
            chunks(e, body)

        @block.scalar
        def _(a):
            a.wait_ge(ld, LOADED)

            def turned_rows(c, i):
                a.wait_ge(turned, START + c + 1)
                a.wait_ge(rt, START + c)
                a.activation(xT[:], ps[0][:], ACT.Copy).then_inc(xts, 1)
                a.activation(xh[:, i, :], ps[0][:], ACT.Copy).then_inc(xts, 1)

            def exponentials(c):
                a.wait_ge(own, c * DVE_STEPS + 2)
                a.activation(prob[:], sc[:], ACT.Exp).then_inc(ex, 1)

            def body(c, i, first, last_chunk):
                for u in range(UN):
                    a.wait_ge(gu, c * UN + u + 1)
                    a.wait_ge(hd, START + c * UN + max(u - 1, 0))
                    a.activation(sil[:, u % 2, :], ps[2 + 2 * (u % 2)][:], ACT.Silu,
                                 bias=bg[:, u // NF, u % NF:u % NF + 1]).then_inc(sl, 1)
                    if first and u == 0:
                        exponentials(c)
                    if not last_chunk:
                        if u == (4 if first else 2):
                            turned_rows(c + 1, 1 - i)
                        elif u == 7:
                            exponentials(c + 1)

            turned_rows(0, 0)
            chunks(a, body)

        @block.vector
        def _(dve):
            dve.wait_ge(ld, LOADED)

            def bc(ap):
                return ap.unsqueeze(2).broadcast_to([P, CH, E1])

            def route(c, i, u, first=False):
                at = {1: 0, 4: 0, 6: 0, 9: 2, 10: 5, 11: 5 + CH, 12: 7 + CH, 13: 8 + 2 * CH}
                s = Steps(dve, own, c * DVE_STEPS + at.get(u, 0), alone=True)
                if u == 1:
                    if not first:
                        dve.wait_ge(turned, START + c)
                    normalise_chunk(dve, xf, X, mv, c).then_inc(nrm, 1)
                elif u == 4:
                    dve.wait_ge(xts, 2 * c + 2)
                    dve.tensor_tensor(xl[:, i, :], xT[:], xh[:, i, :].bitcast(F32), ALU.subtract)\
                        .then_inc(xls, 1)
                elif u == 6:
                    dve.wait_ge(rt, START + c + 1)
                    lg = ps[1][:, 0:CH * E1].rearrange("p (k e) -> p k e", k=CH)
                    s.do(dve.reduce_max(mx[:], lg, X_AXIS))
                    s.do(dve.tensor_tensor(sc[:], lg, bc(mx[:]), ALU.subtract))
                elif u == 9:
                    dve.wait_ge(ex, c + 1)
                    s.do(dve.reduce_sum(mx[:], prob[:], X_AXIS))
                    s.do(dve.reciprocal(mx[:], mx[:]))
                    s.do(dve.tensor_tensor(prob[:], prob[:], bc(mx[:]), ALU.mult))
                elif u == 10:
                    for k in range(CH):
                        s.done(dve.max(top[:, k, :], prob[:, k, :]))
                    s.settle()
                elif u == 11:
                    s.do(dve.tensor_tensor(mx[:], top[:, :, 0], top[:, :, 1], ALU.add))
                    s.done(dve.tensor_scalar(mx[:], mx[:], 1e-9, None, ALU.add))
                elif u == 12:
                    s.do(dve.memset(top[:, :, 2:8], 3.0e38))
                    for k in range(CH):
                        s.done(dve.match_replace(rep[:, k, :], top[:, k, :], prob[:, k, :], -3.0e38))
                    s.settle()
                elif u == 13:
                    s.done(dve.tensor_tensor(rep[:], rep[:], prob[:], ALU.not_equal))
                    s.do(dve.reciprocal(mx[:], mx[:]))
                    s.do(dve.tensor_tensor(pw[:, i, :, :], prob[:], rep[:], ALU.mult))
                    s.do(dve.tensor_tensor(pw[:, i, :, :], pw[:, i, :, :], bc(mx[:]), ALU.mult))
                elif u == 14:
                    dve.wait_ge(pt, c + 1)
                    dve.tensor_copy(pT[:], ps[6][0:E1, :]).then_inc(ptr, 1)
                elif u == 15:
                    dve.wait_ge(db, c + 1)
                    if not first:
                        dve.wait_ge(st, START + 16 * (c - 1))
                    dve.tensor_tensor(acc[:, i, :, :], X[:, bass.ds(c * CH, CH), :],
                                      ps[0][:].rearrange("p (k d) -> p k d", k=CH),
                                      ALU.add).then_inc(ini, 1)

            def add_expert(c, i, x):
                dve.wait_ge(dn, c * E1 + x + 1)
                for k in range(CH):
                    if x:
                        dve.wait_ge(ac, START + c * ADDS + (x - 1) * CH + k + 1)
                    else:
                        dve.wait_ge(ini, START + c + 1)
                    dve.scalar_tensor_tensor(out=acc[:, i, k, :], in0=ps[7][:, k * D:(k + 1) * D],
                                             scalar=pw[:, i, k, x:x + 1], in1=acc[:, i, k, :],
                                             op0=ALU.mult, op1=ALU.add).then_inc(ac, 1)

            def body(c, i, first, last_chunk):
                for x in range(E1):
                    for n in range(NF):
                        u = x * NF + n
                        dve.wait_ge(sl, c * UN + u + 1)
                        dve.scalar_tensor_tensor(out=hid[:, x % 2, n, :], in0=ps[3 + 2 * (u % 2)][:],
                                                 scalar=bu[:, x, n:n + 1], in1=sil[:, u % 2, :],
                                                 op0=ALU.add, op1=ALU.mult).then_inc(hd, 1)
                        if first and u < 4:
                            for v in ((6,), (9, 10, 11, 12, 13), (14,), (15,))[u]:
                                route(c, i, v, first=True)
                        if not last_chunk:
                            route(c + 1, 1 - i, u)
                    if x:
                        add_expert(c, i, x - 1)
                    elif not first:
                        add_expert(c - 1, 1 - i, E1 - 1)
                if last_chunk:
                    add_expert(c, i, E1 - 1)

            for u in (1, 4):
                route(0, 0, u, first=True)
            chunks(dve, body)
def network(nc, t):
    with ExitStack() as ctx:
        def sb(name, shape, dt=F32, c=ctx):
            return c.enter_context(nc.sbuf_tensor(name, shape, dt))

        def sem(name):
            return ctx.enter_context(nc.semaphore(name))

        psum = ctx.enter_context(nc.psum_tensor("psum", [P, 4096], F32))
        ps = [psum[:, i * 512:(i + 1) * 512] for i in range(8)]
        t["tp"] = t["bank01"] = psum[:, 0:1024]
        t["bank67"] = psum[:, 3072:4096]
        t["bank23"], t["bank45"] = psum[:, 1024:2048], psum[:, 2048:3072]
        t["scores"] = psum[:, 0:2048].rearrange("p (a b c) -> p a b c", a=2, b=2)
        ident = sb("ident", [P, P])
        t["X"] = sb("X", [P, NT, D])
        t["mv"] = sb("mv_all", [P, 2, NT])
        t["neg_half"] = sb("neg_half", [P, NT])
        t["rows_steps"] = sem("rows_built")
        t["stat_sem"], t["keys_in"] = sem("p3_stats"), sem("p4_keys_in")
        consts = sem("constants")
        with nc.Block() as block:
            @block.sync
            def _(sp):
                sp.dma_start(ident[:], t["ident"]).then_inc(consts, 16)
                sp.wait_ge(consts, 16)

            @block.gpsimd
            def _(pool):
                pool.memset(t["neg_half"][:], -0.5)
        t["ident"] = ident
        t["w4"] = gate_weights(t, sb, sem)
        with ExitStack() as c:
            t["qkv"] = sb("qkv", [P, NT, 3 * D], F32, c)
            t["att"] = t["qkv"][:, :, 0:D]
            with ExitStack() as c2:
                t["gco"] = sb("gco", [P, NT, 2, H0], F32, c2)
                attention_buffers(t, lambda n, shape, dt=F32: sb(n, shape, dt, c2), sem)
                project_batches(nc, t, sem, ps)
                attend(nc, t, sem, ps)
            output_projection(nc, t, sem, ps)
        with ExitStack() as c:
            for n, dt in (("slotv", F32), ("tok", F32), ("full", F32), ("gidx", I32)):
                t[n] = sb(n, [P, E0 // 2], dt, c)
            with ExitStack() as c2:
                t["keys"] = sb("keys", [E0, N_TOK], F32, c2)
                gate_and_shared(nc, t, sem, ps)
                pick_slots(nc, t, sem, ps)
            routed_experts(nc, t, sem, ps)
        t["XO"] = sb("XO", [P, NT, D])
        t["w7"] = expert_weights(nc, t, sb, sem)
        t["w8"], t["w9"], t["w10"] = (weights(t, sb, sem) for weights in (
            linear_weights, feed_forward_weights, router_weights))
        combine(nc, t, sem, ps)
        linear_attention(nc, t, sem, ps)
        feed_forward(nc, t, sem, ps)
        experts_of_two(nc, t, sem, ps)


def constants(np):
    u = np.arange(S, dtype=np.float64) - S // 2
    u2_low = np.mod(u * u, 128)
    one = np.ones(S)
    krows = np.stack([u * u - u2_low, u2_low, u * u - u2_low, u2_low, u, u, -one, -one], -1)
    part = np.arange(P)
    return {
        "ident": np.eye(P, dtype=np.float32),
        "kconst": np.ascontiguousarray(krows.reshape(TB, P, 8).transpose(1, 0, 2).astype(np.float32)),
        "hmask": (part[:, None] // DH0 == np.arange(H0)[None]).astype(np.float32),
        "block32": (part[:, None] // DH1 == part[None] // DH1).astype(np.float32),
        "tokv": (N_TOK - P * np.arange(NT)[None] - part[:, None]).astype(np.float32),
    }


def kernel(**inputs):
    import numpy as np
    import concourse.bacc as bacc
    from concourse.bass_utils import run_bass_kernel_spmd

    a = {k: np.asarray(v) for k, v in inputs.items()}
    l0, f0, l1, f1 = ({k[len(p):]: v for k, v in a.items() if k.startswith(p)}
                      for p in ("L0_attn_", "L0_ffn_", "L1_attn_", "L1_ffn_"))
    arrays = constants(np)
    arrays["x"] = l0["hidden_states"]
    for n in ("wq", "wk", "wv", "wo", "wfq", "wfg", "bq", "bk", "bv", "bo", "bfq", "bfg", "up", "uz"):
        arrays[n] = l0[n]
    arrays["gate_wT"], arrays["gate_b0"] = f0["gate_w"].T, f0["gate_b"]
    arrays["ws1T"], arrays["ws3T"] = f0["ws1"].T, f0["ws3"].T
    arrays["ws2T"] = f0["ws2"].T.reshape(2, I0, D).transpose(1, 0, 2)
    arrays["w1T"] = f0["w1"].transpose(2, 0, 1).reshape(D, E0 * I0)
    arrays["w3T"] = f0["w3"].transpose(2, 0, 1).reshape(D, E0 * I0)
    arrays["w2T"] = f0["w2"].transpose(2, 0, 1).reshape(I0, E0 * D)
    for n in ("wq", "wk", "wv", "wo", "bo"):
        arrays["l1_" + n] = l1[n]
    for n in ("ln1_g", "ln1_b", "ln2_g", "ln2_b", "w_ff1", "b_ff1", "w_ff2", "b_ff2", "w_d", "b_d"):
        arrays[n] = l1[n]
    arrays["router_wT"] = f1["router_w"].T
    arrays["b_ff1"] = l1["b_ff1"].reshape(FF // P, P).T
    for n in ("gate_w", "up_w", "down_w", "down_b"):
        arrays[n + "1"] = f1[n]
    for n in ("gate_b", "up_b"):
        arrays[n + "1"] = f1[n].reshape(E1 * F1 // P, P).T

    nc = bacc.Bacc("TRN2", target_bir_lowering=False, num_devices=1)
    arrays = {f"in_{n}": np.ascontiguousarray(v) for n, v in arrays.items()}
    t = {n[3:]: nc.dram_tensor(n, v.shape, F32, kind="ExternalInput").ap() for n, v in arrays.items()}
    t["out"] = nc.dram_tensor("out", (B, S, D), F32, kind="ExternalOutput").ap()
    t["rows"] = nc.dram_tensor("token_rows", (N_TOK, ROW), F32, kind="Internal").ap()
    t["ybuf"] = nc.dram_tensor("pick_rows", (N_TOK * K0, D), F32, kind="Internal").ap()
    network(nc, t)
    r = run_bass_kernel_spmd(nc, [arrays], core_ids=[0])
    return r.results[0]["out"]
```
